# Optimizing a Trainium2 kernel written in Bass

```python
import numpy as np
import jax
import jax.numpy as jnp

def _softmax(x, axis=-1):
    return jax.nn.softmax(x, axis=axis)

def _gelu(x):
    return jax.nn.gelu(x, approximate=True)

def _silu(x):
    return jax.nn.silu(x)

def _sigmoid(x):
    return jax.nn.sigmoid(x)

def _layernorm(x, axis=-1, eps=1e-05):
    m = jnp.mean(x, axis=axis, keepdims=True)
    v = jnp.var(x, axis=axis, keepdims=True)
    return (x - m) / jnp.sqrt(v + eps)

def _scatter_add(tgt, idx, src, axis=0):
    return tgt.at[idx].add(src)

def _segment_sum(src, seg, n):
    return jax.ops.segment_sum(src, seg, n)
kernel_name = 'mk_gnn_preln_d2_gnn_r8_153af7'

def setup_inputs(seed: int=0):
    np.random.seed(seed)
    _w = jnp.asarray

    def _rec_inputs():
        import jax
        import jax.numpy as jnp
        _gk = jax.random.key(seed)
        x = -0.000202 + 1 * jax.random.normal(jax.random.fold_in(_gk, 1), (6250, 64), jnp.float32)
        src = jax.random.randint(jax.random.fold_in(_gk, 2), (200000,), 0, 6250, jnp.int32)
        dst = jax.random.randint(jax.random.fold_in(_gk, 3), (200000,), 0, 6250, jnp.int32)
        _o = jnp.argsort(dst, stable=True)
        src = src[_o]
        dst = dst[_o]
        edge_type_8 = jax.random.randint(jax.random.fold_in(_gk, 12), (200000,), 0, 8, jnp.int32)
        return (x, src, dst, edge_type_8)
    x, src, dst, edge_type_8 = _rec_inputs()

    def _L0_gnn_setup():
        import jax, jax.numpy as jnp
        import numpy as np
        N_NODES = 12500
        N_EDGES = 200000
        D = 64

        def _ngcf_conv(x, W1, W2, src, dst, n_nodes):
            ones = jnp.ones(src.shape[0], dtype=x.dtype)
            deg_out = jnp.clip(jax.ops.segment_sum(ones, src, num_segments=n_nodes), 1.0)
            deg_in = jnp.clip(jax.ops.segment_sum(ones, dst, num_segments=n_nodes), 1.0)
            norm = jax.lax.rsqrt(deg_out[src] * deg_in[dst])
            h_src = x[src]
            h_dst = x[dst]
            msg = (h_src @ W1 + h_src * h_dst @ W2) * norm[:, None]
            agg = jax.ops.segment_sum(msg, dst, num_segments=n_nodes)
            return x @ W1 + agg
        key = jax.random.key(seed)
        ks = jax.random.split(key, 8)
        s = 1.0 / np.sqrt(D)
        return {'x': jax.random.normal(ks[0], (N_NODES, D), dtype=jnp.float32), 'edge_src': jax.random.randint(ks[1], (N_EDGES,), 0, N_NODES, dtype=jnp.int32), 'edge_dst': jax.random.randint(ks[2], (N_EDGES,), 0, N_NODES, dtype=jnp.int32), 'W1_1': jax.random.normal(ks[3], (D, D), dtype=jnp.float32) * s, 'W2_1': jax.random.normal(ks[4], (D, D), dtype=jnp.float32) * s, 'W1_2': jax.random.normal(ks[5], (D, D), dtype=jnp.float32) * s, 'W2_2': jax.random.normal(ks[6], (D, D), dtype=jnp.float32) * s}
    _L0_gnn_all = _L0_gnn_setup()
    _L0_gnn_in = {k: v for k, v in _L0_gnn_all.items() if k in ('W1_1', 'W2_1', 'W1_2', 'W2_2')}
    del _L0_gnn_all

    def _L1_gnn_setup():
        import jax, jax.numpy as jnp
        import numpy as np
        N_NODES = 6250
        N_EDGES = 100000
        FEAT_DIM = 64
        NUM_RELS = 8
        key = jax.random.key(seed)
        k1, k2, k3, k4, k5 = jax.random.split(key, 5)
        features = jax.random.normal(k1, (N_NODES, FEAT_DIM), dtype=jnp.float32)
        limit = np.sqrt(2.0) * np.sqrt(6.0 / (FEAT_DIM + FEAT_DIM))
        weight_r = jax.random.uniform(k2, (NUM_RELS, FEAT_DIM, FEAT_DIM), dtype=jnp.float32, minval=-limit, maxval=limit)
        src = jax.random.randint(k3, (N_EDGES,), 0, N_NODES, dtype=jnp.int64 if jax.config.jax_enable_x64 else jnp.int32)
        dst = jax.random.randint(k4, (N_EDGES,), 0, N_NODES, dtype=src.dtype)
        etype = jax.random.randint(k5, (N_EDGES,), 0, NUM_RELS, dtype=src.dtype)
        return {'features': features, 'weight_r': weight_r, 'src': src, 'dst': dst, 'etype': etype}
    _L1_gnn_all = _L1_gnn_setup()
    _L1_gnn_in = {k: v for k, v in _L1_gnn_all.items() if k in ('weight_r',)}
    del _L1_gnn_all
    return {'x': x, 'src': src, 'dst': dst, 'edge_type_8': edge_type_8, 'L0_gnn_W1_1': _L0_gnn_in['W1_1'], 'L0_gnn_W2_1': _L0_gnn_in['W2_1'], 'L0_gnn_W1_2': _L0_gnn_in['W1_2'], 'L0_gnn_W2_2': _L0_gnn_in['W2_2'], 'L1_gnn_weight_r': _L1_gnn_in['weight_r']}

def reference(x, src, dst, edge_type_8, L0_gnn_W1_1, L0_gnn_W2_1, L0_gnn_W1_2, L0_gnn_W2_2, L1_gnn_weight_r):
    import jax
    import jax.numpy as jnp

    def _L0_gnn_ref(x, edge_src, edge_dst, W1_1, W2_1, W1_2, W2_2):
        import jax, jax.numpy as jnp
        import numpy as np
        N_NODES = 12500
        N_EDGES = 200000
        D = 64

        def _ngcf_conv(x, W1, W2, src, dst, n_nodes):
            ones = jnp.ones(src.shape[0], dtype=x.dtype)
            deg_out = jnp.clip(jax.ops.segment_sum(ones, src, num_segments=n_nodes), 1.0)
            deg_in = jnp.clip(jax.ops.segment_sum(ones, dst, num_segments=n_nodes), 1.0)
            norm = jax.lax.rsqrt(deg_out[src] * deg_in[dst])
            h_src = x[src]
            h_dst = x[dst]
            msg = (h_src @ W1 + h_src * h_dst @ W2) * norm[:, None]
            agg = jax.ops.segment_sum(msg, dst, num_segments=n_nodes)
            return x @ W1 + agg
        n = x.shape[0]
        h = _ngcf_conv(x, W1_1, W2_1, edge_src, edge_dst, n)
        h = jax.nn.relu(h)
        h = _ngcf_conv(h, W1_2, W2_2, edge_src, edge_dst, n)
        return h

    def _L1_gnn_ref(features, weight_r, src, dst, etype):
        import jax, jax.numpy as jnp
        import numpy as np
        N_NODES = 6250
        N_EDGES = 100000
        FEAT_DIM = 64
        NUM_RELS = 8
        N, D = features.shape
        c = 0.2
        deg = jax.ops.segment_sum(jnp.ones(dst.shape, dtype=features.dtype), dst, num_segments=N)
        hw = jnp.einsum('nd,rdf->rnf', features, weight_r)
        msg = hw[etype, src] / deg[dst][:, None]
        M = jax.ops.segment_sum(msg, dst, num_segments=N)
        updated = jax.nn.relu(c * features + (1.0 - c) * M)
        return jnp.where((deg > 0)[:, None], updated, features)
    h = jnp.maximum(_layernorm(x, axis=-1), 0.0)
    x = x + _L0_gnn_ref(h, src, dst, L0_gnn_W1_1, L0_gnn_W2_1, L0_gnn_W1_2, L0_gnn_W2_2)
    h = jnp.maximum(_layernorm(x, axis=-1), 0.0)
    x = x + _L1_gnn_ref(h, L1_gnn_weight_r, src, dst, edge_type_8)
    return x

_drawn_inputs = setup_inputs


def setup_inputs(seed=0):
    import zlib

    import numpy as np

    out = dict(_drawn_inputs(seed))
    spreads = {}
    factors = {}
    for name, (base, spread) in spreads.items():
        noise = np.random.default_rng([zlib.crc32(name.encode()), seed]).standard_normal(out[name].shape)
        drawn = base * np.exp(spread * noise) if base else spread * noise
        out[name] = jnp.asarray(drawn.astype(out[name].dtype))
    for name, factor in factors.items():
        out[name] = (out[name] * factor).astype(out[name].dtype)
    return out
```

```python
from contextlib import ExitStack

import concourse.bass as bass
from concourse import mybir

P = 128
F32 = mybir.dt.float32
BF16 = mybir.dt.bfloat16
F16 = mybir.dt.float16
I32 = mybir.dt.int32
U32 = mybir.dt.uint32
ALU = mybir.AluOpType
ACT = mybir.ActivationFunctionType
X = mybir.AxisListType.X
EPS = 1e-5
BANK = 512

GROUP = 8
ROW = 32
GROUP_TILES = 3
PIECES = 3
WIN = 128
MARGIN = 62


class Named:
    pass


def sizes(N, E, D, R):
    z = Named()
    z.N = N
    z.E = E
    z.D = D
    z.R = R
    z.NB = -(-N // P)
    z.NP = z.NB * P
    z.DEG = z.NP // z.NB and E // N
    z.TILES = -(-E // (P * ROW)) * ROW
    z.EP = z.TILES * P
    z.QT = 14
    z.Q = z.TILES // z.QT
    z.QE = z.QT * P
    z.ROWS = z.EP // ROW
    z.TROWS = -(-(z.ROWS + 4 * GROUP_TILES) // 16) * 16
    z.SCR = ROW * (z.TROWS - 1) + P
    z.GB = P // GROUP
    z.CT = z.GB * GROUP_TILES
    z.KEYS = GROUP * z.NB
    z.STEP = 4
    z.SEG = -(-N // BANK)
    z.FLAG_GROUPS = -(-N // GROUP)
    assert z.Q * z.QT == z.TILES and z.TILES * z.STEP == z.NP and z.KEYS <= BANK
    assert z.Q <= P and z.NB <= P and E > (z.Q - 1) * z.QE
    return z


class Steps:

    def __init__(self, eng, sem):
        self.eng, self.sem, self.n = eng, sem, 0

    def did(self, instruction):
        self.n += 1
        instruction.then_inc(self.sem, 1)

    def wait(self):
        self.eng.wait_ge(self.sem, self.n)


def bcast(ap, axis, shape):
    return ap.unsqueeze(axis).broadcast_to(shape)


def layernorm_relu(v, c, z, src, dst, work, stat, eps, var_ready, root_ready, times):
    full = [P, z.NB, z.D]
    mean, var, rstd, t = (stat[:, i, :] for i in range(4))
    c.wait()
    c.did(v.tensor_reduce(mean, src, X, ALU.add))
    c.wait()
    c.did(v.tensor_scalar(mean, mean, 1.0 / z.D, None, ALU.mult))
    c.wait()
    c.did(v.tensor_tensor(dst, src, bcast(mean, 2, full), ALU.subtract))
    c.wait()
    c.did(v.tensor_tensor(work, dst, dst, ALU.mult))
    c.wait()
    c.did(v.tensor_reduce(var, work, X, ALU.add))
    c.wait()
    c.did(v.tensor_scalar(var, var, 1.0 / z.D, EPS, ALU.mult, ALU.add))
    c.wait()
    v.sem_inc(var_ready, 1)
    inverse_root(v, c, var, rstd, t, root_ready, times)
    c.did(v.tensor_tensor(dst, dst, bcast(rstd, 2, full), ALU.mult))
    c.wait()
    c.did(v.tensor_scalar(dst, dst, 0.0, None, ALU.max))
    c.wait()


def inverse_root(v, c, y, r, t, root_ready, times):
    v.wait_ge(root_ready, times)
    c.did(v.reciprocal(r, r))
    c.wait()
    c.did(v.tensor_tensor(t, r, r, ALU.mult))
    c.wait()
    c.did(v.tensor_tensor(t, t, y, ALU.mult))
    c.wait()
    c.did(v.tensor_scalar(t, t, -0.5, 1.5, ALU.mult, ALU.add))
    c.wait()
    c.did(v.tensor_tensor(r, r, t, ALU.mult))
    c.wait()


def constants(nc, z, m, sem):
    made, ready = sem("constants_made"), sem("constants_ready")
    with nc.Block() as block:

        @block.gpsimd
        def _(g):
            small = dict(allow_small_or_imprecise_dtypes=True)
            g.iota(m.iota_row[:, :], pattern=[[1, BANK]], base=0, channel_multiplier=0, **small)
            g.iota(m.iota_part[:, :], pattern=[[0, 1]], base=0, channel_multiplier=1, **small)
            g.iota(m.iota_keys[:, :], pattern=[[1, z.KEYS]], base=0, channel_multiplier=0, **small)
            g.iota(m.iota_low[:, :, :], pattern=[[1, P], [0, 12]], base=0, channel_multiplier=0,
                   **small).then_inc(made, 1)

        @block.vector
        def _(v):
            c = Steps(v, ready)
            v.wait_ge(made, 1)
            c.did(v.memset(m.zeros[:, :], 0.0))
            c.did(v.memset(m.ones[:, :], 1.0))
            c.did(v.memset(m.ones16[:, :, :], 1.0))
            c.did(v.tensor_scalar(m.ident[:, :], m.iota_row[:, 0:P], m.iota_part[:, 0:1], None, ALU.is_equal))
            c.did(v.tensor_scalar(m.ident16[:, :], m.iota_row[:, 0:P], m.iota_part[:, 0:1], None, ALU.is_equal))
            c.did(v.tensor_scalar(m.before[:, :], m.iota_row[:, 0:P], m.iota_part[:, 0:1], None, ALU.is_gt))
            c.wait()


def prepare(nc, z, m, d, sem):
    padded, src_in, dst_in, et_in, next_in = (sem(n) for n in (
        "padded", "src_in", "dst_in", "type_in", "next_in"))
    x_in, w_in, patterns, step = (sem(n) for n in ("x_in", "weights_in", "patterns", "prep_step"))
    fields, scr_out, rows_out, counted = (sem(n) for n in (
        "fields_ready", "scratch_written", "rows_written", "heads_hot"))
    c_made, c_copied, ct_made, ct_copied, pre_made = (sem(n) for n in (
        "counts_made", "counts_copied", "turned_counts", "turned_copied", "prefix_made"))
    starts, turned, bank_free = sem("starts_ready"), sem("tiles_turned"), sem("turn_bank_free")
    landed = [sem(f"group_rows_landed{i}") for i in range(4)]
    slots_free, var_ready, root_ready = sem("row_slots_free"), sem("var0_ready"), sem("root0_ready")
    bad_ready, bad_made, pad_ready = sem("bad_ready"), sem("bad_summed"), sem("pad_ready")
    flat_made, flat_bank = sem("flat_turned"), sem("flat_bank_free")
    rem = z.E - (z.Q - 1) * z.QE
    flat_groups = [(f, t, min(4, z.QT - t)) for f in range(3) for t in range(0, z.QT, 4)]

    with ExitStack() as ctx:
        sb = lambda n, s, t: ctx.enter_context(nc.sbuf_tensor(n, s, t))
        ps = lambda n, s: ctx.enter_context(nc.psum_tensor(n, s, F32))
        edge = [z.Q, z.QE]
        src_i, dst_i, et_i = sb("src_i", edge, I32), sb("dst_i", edge, I32), sb("type_i", edge, I32)
        high_i, low_i = sb("src_high", edge, I32), sb("src_low", edge, I32)
        low, key = sb("low_f", edge, F32), sb("key_f", edge, F32)
        dst, src, idx = sb("dst_f", edge, F32), sb("src_f", edge, F32), sb("row_f", edge, F32)
        centre = sb("centre", edge, F32)
        next_i, next_f = sb("next_i", [z.Q, 1], I32), sb("next_f", [z.Q, 1], F32)
        bad = sb("bad", [P, 8], F32)
        bad1 = sb("bad1", [P, 1], F32)
        heads = z.QE // ROW
        head_hi, head_mid = sb("head_hi", [z.Q, heads], I32), sb("head_mid", [z.Q, heads], I32)
        hot_hi = sb("hot_hi", [z.Q, heads, z.NB], BF16)
        hot_mid = sb("hot_mid", [z.Q, heads, z.GB], BF16)
        cnt, cnt_t = sb("cnt", [z.NB, z.GB], F32), sb("cnt_t", [z.GB, z.NB], F32)
        total, total_b = sb("total", [z.NB, 1], F32), sb("total_b", [z.NB, z.GB], F32)
        start = sb("start", [z.NB, z.GB], F32)
        over = sb("over", [z.NB, z.GB], F32)
        group_no = sb("group_no", [z.NB, z.GB], F32)
        row_no = sb("row_no", [z.NB, z.GB, GROUP_TILES], U32)
        got = sb("got", [z.NB, 16, 2, P], F32)
        offset = sb("offset", [P, z.NB, z.GB, GROUP_TILES], F32)
        pad = sb("pad", [16, 2, (z.SCR - z.EP) // 16], F32)
        turn = [ps(f"turn{i}", [P, BANK]) for i in range(4)]
        p_cnt, p_misc = ps("p_cnt", [P, BANK]), ps("p_misc", [P, BANK])

        with nc.Block() as block:

            @block.sync
            def _(sp):
                sp.wait_ge(padded, 1)
                for ap, t, s in ((d.src, src_i, src_in), (d.dst, dst_i, dst_in), (d.etype, et_i, et_in)):
                    body = ap[0:(z.Q - 1) * z.QE].rearrange("(q e) -> q e", e=z.QE)
                    tail = ap[(z.Q - 1) * z.QE:z.E].rearrange("(q e) -> q e", q=1)
                    sp.dma_start(t[0:z.Q - 1, :], body).then_inc(s, 16)
                    sp.dma_start(t[z.Q - 1:z.Q, 0:rem], tail).then_inc(s, 16)
                sp.dma_start(next_i[0:z.Q - 1, :], bass.AP(d.dst.tensor, z.QE, [[z.QE, z.Q - 1], [1, 1]]),
                             allow_slow_non_contiguous=True).then_inc(next_in, 16)
                sp.wait_ge(fields, 1)
                sp.wait_ge(pad_ready, 1)
                for f, t in enumerate((low, key)):
                    sp.dma_start(d.scr[f, 0:z.EP].rearrange("(q e) -> q e", e=z.QE), t[:, :]).then_inc(scr_out, 16)
                    sp.dma_start(d.scr[f, z.EP:z.SCR].rearrange("(q e) -> q e", q=16), pad[:, f, :]).then_inc(scr_out, 16)
                sp.wait_ge(scr_out, 64)
                for f in range(2):
                    rows = bass.AP(d.scr.tensor, f * z.SCR, [[ROW, z.TROWS], [1, P]])
                    sp.dma_start(d.rows[:, f, :], rows).then_inc(rows_out, 16)
                sp.wait_ge(rows_out, 32)

            @block.scalar
            def _(a):
                a.dma_start(m.x[:, 0:z.NB - 1, :], d.x[0:(z.NB - 1) * P, :].rearrange("(b p) f -> p b f", p=P)).then_inc(x_in, 16)
                a.wait_ge(padded, 2)
                a.dma_start(m.x[0:z.N - (z.NB - 1) * P, z.NB - 1, :], d.x[(z.NB - 1) * P:z.N, :]).then_inc(x_in, 16)
                for i, w in enumerate((d.w1_1, d.w2_1, d.w1_2, d.w2_2)):
                    a.dma_start(m.w12[z.D * (i % 2):z.D * (i % 2) + z.D, i // 2, :], w).then_inc(w_in, 16)
                a.dma_start(m.w3[:, :, :], d.w3.rearrange("r d f -> d r f")).then_inc(w_in, 16)
                a.wait_ge(var_ready, 1)
                a.activation(m.stat[:, 2, :], m.stat[:, 1, :], ACT.Sqrt).then_inc(root_ready, 1)
                a.wait_ge(w_in, 80)

            @block.gpsimd
            def _(g):
                small = dict(allow_small_or_imprecise_dtypes=True)
                g.iota(centre[:, :], pattern=[[z.STEP, z.QT], [0, P]], base=0,
                       channel_multiplier=z.STEP * z.QT, **small)
                g.iota(group_no[:, :], pattern=[[1, z.GB]], base=0, channel_multiplier=z.GB, **small)
                g.iota(m.tile_base[:, :], pattern=[[z.STEP, z.TILES]], base=-MARGIN, channel_multiplier=0, **small)
                g.iota(offset[:, :, :, :], pattern=[[z.KEYS * z.GB, z.NB], [z.KEYS, z.GB], [0, GROUP_TILES]],
                       base=0, channel_multiplier=0, **small).then_inc(patterns, 1)
                g.wait_ge(starts, 1)
                g.wait_ge(rows_out, 32)
                for ct in range(z.CT):
                    k = ct // 4
                    if ct % 4 == 0 and k >= 4:
                        g.wait_ge(slots_free, k - 3)
                    c_, t_ = divmod(ct, GROUP_TILES)
                    g.indirect_dma_start(
                        got[:, ct % 16, :, :].rearrange("p f e -> p (f e)"), None,
                        d.rows.rearrange("r f e -> r (f e)"),
                        bass.IndirectOffsetOnAxis(ap=row_no[:, c_, t_:t_ + 1], axis=0),
                    ).then_inc(landed[k % 4], 16)

            @block.tensor
            def _(t):
                t.wait_ge(counted, 1)
                for h in range(heads):
                    mm = t.matmul(p_cnt[0:z.NB, 0:z.GB], hot_hi[:, h, :], hot_mid[:, h, :],
                                  start=(h == 0), stop=(h == heads - 1))
                mm.then_inc(c_made, 1)
                t.wait_ge(c_copied, 1)
                t.transpose(p_misc[0:z.GB, 0:z.NB], cnt[:, :], m.ident[0:z.NB, 0:z.NB]).then_inc(ct_made, 1)
                t.wait_ge(ct_copied, 1)
                t.matmul(p_cnt[0:z.NB, 64:64 + z.GB], cnt_t[:, :], m.before[0:z.GB, 0:z.GB], start=True, stop=False)
                t.matmul(p_cnt[0:z.NB, 64:64 + z.GB], m.before[0:z.NB, 0:z.NB], total_b[:, :],
                         start=False, stop=True).then_inc(pre_made, 1)
                t.wait_ge(bad_ready, 1)
                t.matmul(p_misc[0:1, 256:257], bad1[:, :], m.ones[:, 0:1], start=True, stop=True).then_inc(bad_made, 1)
                for n, (f, t0, cntt) in enumerate(flat_groups):
                    if n >= 4:
                        t.wait_ge(flat_bank, n - 3)
                    what = (idx, dst, src)[f]
                    for j in range(cntt):
                        mm = t.transpose(turn[n % 4][:, j * z.Q:(j + 1) * z.Q], what[:, (t0 + j) * P:(t0 + j + 1) * P],
                                         m.ident[0:z.Q, 0:z.Q])
                    mm.then_inc(flat_made, 1)
                for k in range(z.CT // 4):
                    t.wait_ge(landed[k % 4], 64 * (k // 4 + 1))
                    if k < 4:
                        t.wait_ge(flat_bank, len(flat_groups) - 3 + k)
                    else:
                        t.wait_ge(bank_free, k - 3)
                    for f in range(2):
                        for j in range(4):
                            at = (f * 4 + j) * z.NB
                            mm = t.transpose(turn[(len(flat_groups) + k) % 4][:, at:at + z.NB],
                                             got[:, (k % 4) * 4 + j, f, :], m.ident[0:z.NB, 0:z.NB])
                    mm.then_inc(turned, 1)

            @block.vector
            def _(v):
                c = Steps(v, step)
                c.did(v.memset(src_i[:, rem:], z.NP - 1))
                c.did(v.memset(dst_i[:, rem:], z.NP - 1))
                c.did(v.memset(et_i[:, rem:], 0))
                c.did(v.memset(next_i[:, :], z.NP - 1))
                c.wait()
                v.sem_inc(padded, 1)
                c.did(v.memset(m.x[:, z.NB - 1, :], 0.0))
                c.wait()
                v.sem_inc(padded, 1)
                c.did(v.memset(pad[:, 0, :], 0.0))
                c.did(v.memset(pad[:, 1, :], -1.0))
                c.did(v.memset(bad[:, :], 0.0))
                c.wait()
                v.sem_inc(pad_ready, 1)
                v.wait_ge(src_in, 32)
                c.did(v.tensor_scalar(high_i[:, :], src_i[:, :], 7, None, ALU.logical_shift_right))
                c.did(v.tensor_scalar(low_i[:, :], src_i[:, :], 127, None, ALU.bitwise_and))
                v.wait_ge(dst_in, 32)
                c.did(v.tensor_scalar(head_hi[:, :], dst_i[:, 0:z.QE:ROW], 7, None, ALU.logical_shift_right))
                c.did(v.tensor_scalar(head_mid[:, :], dst_i[:, 0:z.QE:ROW], 3, z.GB - 1,
                                      ALU.logical_shift_right, ALU.bitwise_and))
                c.wait()
                c.did(v.tensor_copy(low[:, :], low_i[:, :]))
                c.did(v.scalar_tensor_tensor(out=key[:, :], in0=dst_i[:, :], scalar=float(z.NB), in1=high_i[:, :],
                                             op0=ALU.mult, op1=ALU.add))
                c.wait()
                v.sem_inc(fields, 1)
                c.did(v.tensor_tensor(hot_hi[:, :, :], bcast(m.iota_row[0:z.Q, 0:z.NB], 1, [z.Q, heads, z.NB]),
                                      bcast(head_hi[:, :], 2, [z.Q, heads, z.NB]), ALU.is_equal))
                c.did(v.tensor_tensor(hot_mid[:, :, :], bcast(m.iota_row[0:z.Q, 0:z.GB], 1, [z.Q, heads, z.GB]),
                                      bcast(head_mid[:, :], 2, [z.Q, heads, z.GB]), ALU.is_equal))
                c.wait()
                v.sem_inc(counted, 1)
                c.did(v.tensor_copy(dst[:, :], dst_i[:, :]))
                c.did(v.tensor_copy(src[:, :], src_i[:, :]))
                v.wait_ge(et_in, 32)
                c.did(v.scalar_tensor_tensor(out=idx[:, :], in0=src_i[:, :], scalar=float(z.R), in1=et_i[:, :],
                                             op0=ALU.mult, op1=ALU.add))
                v.wait_ge(c_made, 1)
                c.did(v.tensor_copy(cnt[:, :], p_cnt[0:z.NB, 0:z.GB]))
                c.wait()
                v.sem_inc(c_copied, 1)
                c.did(v.tensor_reduce(total[:, :], cnt[:, :], X, ALU.add))
                c.wait()
                c.did(v.tensor_copy(total_b[:, :], total[:, 0:1].broadcast_to([z.NB, z.GB])))
                v.wait_ge(ct_made, 1)
                c.did(v.tensor_copy(cnt_t[:, :], p_misc[0:z.GB, 0:z.NB]))
                c.wait()
                v.sem_inc(ct_copied, 1)
                v.wait_ge(pre_made, 1)
                c.did(v.tensor_scalar(start[:, :], p_cnt[0:z.NB, 64:64 + z.GB], -1.0, 0.0, ALU.add, ALU.max))
                c.wait()
                for t_ in range(GROUP_TILES):
                    c.did(v.tensor_scalar(row_no[:, :, t_], start[:, :], float(4 * t_), None, ALU.add))
                c.wait()
                v.sem_inc(starts, 1)
                v.wait_ge(next_in, 16)
                v.wait_ge(patterns, 1)
                c.did(v.tensor_tensor(low_i[:, 0:z.QE - 1], dst[:, 0:z.QE - 1], dst[:, 1:z.QE], ALU.is_gt))
                c.did(v.tensor_tensor(bad[0:z.Q, 1:2], dst[:, z.QE - 1:z.QE], next_i[:, :], ALU.is_gt))
                c.did(v.tensor_tensor(centre[:, :], dst[:, :], centre[:, :], ALU.subtract))
                c.did(v.tensor_scalar(over[:, :], cnt[:, :], float(4 * GROUP_TILES - 1), None, ALU.is_gt))
                c.did(v.tensor_scalar(group_no[:, :], group_no[:, :], float(z.FLAG_GROUPS), None, ALU.is_lt))
                c.wait()
                c.did(v.tensor_reduce(bad[0:z.Q, 0:1], low_i[:, 0:z.QE - 1], X, ALU.max))
                c.did(v.tensor_reduce(bad[0:z.Q, 5:6], centre[:, :], X, ALU.max))
                c.did(v.tensor_reduce(bad[0:z.Q, 6:7], centre[:, :], X, ALU.min))
                c.did(v.tensor_tensor(over[:, :], over[:, :], group_no[:, :], ALU.mult))
                c.wait()
                c.did(v.tensor_scalar(bad[0:z.Q, 2:3], bad[0:z.Q, 5:6], float(WIN - 1 - MARGIN), None, ALU.is_gt))
                c.did(v.tensor_scalar(bad[0:z.Q, 3:4], bad[0:z.Q, 6:7], float(-MARGIN), None, ALU.is_lt))
                c.did(v.tensor_reduce(bad[0:z.NB, 4:5], over[:, :], X, ALU.max))
                c.wait()
                c.did(v.tensor_reduce(bad1[:, :], bad[:, 0:5], X, ALU.add))
                c.wait()
                v.sem_inc(bad_ready, 1)
                v.wait_ge(bad_made, 1)
                c.did(v.tensor_copy(m.flag[:, :], p_misc[0:1, 256:257]))
                for n, (f, t0, cntt) in enumerate(flat_groups):
                    v.wait_ge(flat_made, n + 1)
                    from_ = turn[n % 4][:, 0:cntt * z.Q].rearrange("p (j q) -> p q j", j=cntt)
                    at = lambda b: b[:, :].rearrange("p (q t) -> p q t", t=z.QT)[:, :, t0:t0 + cntt]
                    if f == 1:
                        c.did(v.tensor_tensor(at(m.in_window), from_, at(m.tile_base), ALU.subtract))
                    else:
                        c.did(v.tensor_copy(at((m.row_index, None, m.src_index)[f]), from_))
                    c.wait()
                    v.sem_inc(flat_bank, 1)
                v.wait_ge(x_in, 32)
                layernorm_relu(v, c, z, m.x[:, :, :], m.h[:, :, :], m.s[:, :, :], m.stat, EPS, var_ready, root_ready, 1)
                off = offset[:, :, :, :].rearrange("p b c t -> p b (c t)")
                for k in range(z.CT // 4):
                    v.wait_ge(turned, k + 1)
                    bank = turn[(len(flat_groups) + k) % 4]
                    half = 4 * z.NB
                    view = lambda b: b[:, :].rearrange("p (b c) -> p b c", c=z.CT)[:, :, 4 * k:4 * k + 4]
                    c.did(v.tensor_copy(view(m.low), bank[:, 0:half].rearrange("p (j b) -> p b j", j=4)))
                    c.did(v.tensor_tensor(view(m.key), bank[:, half:2 * half].rearrange("p (j b) -> p b j", j=4),
                                          off[:, :, 4 * k:4 * k + 4], ALU.subtract))
                    c.wait()
                    v.sem_inc(slots_free, 1)
                    v.sem_inc(bank_free, 1)
                c.wait()


def build(nc, z, m, d, sem):
    low_hot, key_hot, group_made, pair_copied = (sem(n) for n in (
        "low_hot", "key_hot", "group_made", "pair_copied"))
    stored = [sem(f"half_stored{i}") for i in range(2)]
    deg_made, step = sem("degrees_made"), sem("build_step")
    pairs = z.GB // 2
    half = z.GB * z.KEYS // 2
    with ExitStack() as ctx:
        sb = lambda n, s, t: ctx.enter_context(nc.sbuf_tensor(n, s, t))
        low = sb("low_hot_buf", [P, 2, P, 12], BF16)
        keys = sb("key_hot_buf", [P, 2, 12, z.KEYS], BF16)
        a_buf = sb("a_buf", [P, pairs, 2, z.KEYS], BF16)
        bank = [ctx.enter_context(nc.psum_tensor(f"pair{i}", [P, 2, BANK], F32)) for i in range(2)]
        degree = ctx.enter_context(nc.psum_tensor("degree", [P, BANK], F32))
        general = general_buffers(nc, z, ctx, "deg")
        gsem = general_semaphores(sem, "deg")

        with nc.Block() as block:

            @block.vector
            def _(v):
                bad = v.value_load(m.flag[0:1, 0:1], min_val=0, max_val=1024)
                with v.If(bad > 0):
                    general_vector(v, z, m, general, gsem, "degree")
                with v.Else():
                    with v.Fori(0, z.NB) as b:
                        for k in range(4):
                            v.wait_ge(group_made, z.GB * b + 4 * (k + 1))
                            v.tensor_tensor(low[:, k % 2, :, :], m.iota_low[:, :, :],
                                            bcast(m.low[:, bass.ds(z.CT * b + 12 * k, 12)], 1, [P, P, 12]),
                                            ALU.is_equal).then_inc(low_hot, 1)
                            for j in range(12):
                                ins = v.tensor_scalar(keys[:, k % 2, j, :], m.iota_keys[:, :],
                                                      m.key[:, bass.ds(z.CT * b + 12 * k + j, 1)], None, ALU.is_equal)
                                if j % GROUP_TILES == GROUP_TILES - 1:
                                    ins.then_inc(key_hot, 1)
                    v.wait_ge(deg_made, 1)
                    v.tensor_reduce(m.deg_out[:, :], degree[:, 0:z.KEYS].rearrange("p (g s) -> p s g", g=GROUP),
                                    X, ALU.add).then_inc(step, 1)
                    v.wait_ge(step, 1)

            @block.tensor
            def _(t):
                bad = t.value_load(m.flag[0:1, 0:1], min_val=0, max_val=1024)
                with t.If(bad > 0):
                    general_tensor(t, z, m, general, gsem, "degree")
                with t.Else():
                    t.sem_inc(group_made, 8)
                    t.sem_inc(pair_copied, 2)
                    t.matmul(degree[:, 0:z.KEYS], m.zeros[0:1, 0:P], m.zeros[0:1, 0:z.KEYS], start=True, stop=False)

                    def degrees_of(q):
                        for c in range(2):
                            mm = t.matmul(degree[:, 0:z.KEYS], m.ident16[:, :], a_buf[:, q, c, :],
                                          start=False, stop=False)
                        return mm

                    with t.Fori(0, z.NB) as b:
                        for q in range(pairs):
                            t.wait_ge(pair_copied, pairs * b + (q + 1))
                            for c in range(2):
                                g = 2 * q + c
                                if g % 4 == 0:
                                    t.wait_ge(low_hot, 4 * b + (g // 4 + 1))
                                t.wait_ge(key_hot, z.GB * b + (g + 1))
                                for j in range(GROUP_TILES):
                                    at = g * GROUP_TILES + j
                                    mm = t.matmul(bank[q % 2][:, c, 0:z.KEYS], low[:, at // 12 % 2, :, at % 12],
                                                  keys[:, at // 12 % 2, at % 12, :],
                                                  start=(j == 0), stop=(j == GROUP_TILES - 1))
                                mm.then_inc(group_made, 1)
                            if q >= 1:
                                t.wait_ge(pair_copied, pairs * b + (q + 2))
                                degrees_of(q - 1)
                        t.wait_ge(pair_copied, pairs * b + (pairs + 2))
                        degrees_of(pairs - 1)
                    t.matmul(degree[:, 0:z.KEYS], m.zeros[0:1, 0:P], m.zeros[0:1, 0:z.KEYS],
                             start=False, stop=True).then_inc(deg_made, 1)

            @block.scalar
            def _(a):
                bad = a.value_load(m.flag[0:1, 0:1], min_val=0, max_val=1024)
                with a.If(bad > 0):
                    general_scalar(a, z, m, general, gsem, "degree")
                with a.Else():
                    with a.Fori(0, z.NB) as b:
                        for q in range(pairs):
                            if q % (pairs // 2) == 0:
                                a.wait_ge(stored[q // (pairs // 2)], 16 * b + 16)
                            a.wait_ge(group_made, z.GB * b + (8 + 2 * (q + 1)))
                            a.copy(a_buf[:, q, :, :], bank[q % 2][:, :, 0:z.KEYS]).then_inc(pair_copied, 1)

            @block.gpsimd
            def _(g):
                bad = g.value_load(m.flag[0:1, 0:1], min_val=0, max_val=1024)
                with g.If(bad > 0):
                    general_gpsimd(g, z, m, d, general, gsem, "degree")

            @block.sync
            def _(sp):
                bad = sp.value_load(m.flag[0:1, 0:1], min_val=0, max_val=1024)
                with sp.If(bad > 0):
                    sp.nop(nofuse=True)
                with sp.Else():
                    sp.sem_inc(stored[0], 16)
                    sp.sem_inc(stored[1], 16)
                    flat = a_buf[:, :, :, :].rearrange("p q c k -> p (q c k)")
                    with sp.Fori(0, z.NB) as b:
                        for h in range(2):
                            sp.wait_ge(pair_copied, pairs * b + (2 + pairs // 2 * (h + 1)))
                            sp.nop(nofuse=True)
                            sp.dma_start(d.a[bass.ds(b, 1), :, h * half:(h + 1) * half].rearrange("b p k -> (b p) k"),
                                         flat[:, h * half:(h + 1) * half]).then_inc(stored[h], 16)
                    for h in range(2):
                        sp.wait_ge(stored[h], 16 * (z.NB + 1))


def general_semaphores(sem, tag):
    it = Named()
    it.hot = sem(f"general_{tag}_hot")
    it.index = sem(f"general_{tag}_index")
    it.rows = sem(f"general_{tag}_rows")
    it.used = sem(f"general_{tag}_used")
    it.summed = sem(f"general_{tag}_summed")
    it.moved = sem(f"general_{tag}_moved")
    it.staged = sem(f"general_{tag}_staged")
    it.turned = sem(f"general_{tag}_turned")
    it.placed = sem(f"general_{tag}_placed")
    it.own = sem(f"general_{tag}_own")
    return it


def general_buffers(nc, z, ctx, tag):
    sb = lambda n, s, t: ctx.enter_context(nc.sbuf_tensor(f"{n}_{tag}", s, t))
    it = Named()
    it.rows = sb("general_rows", [P, 8, z.D + 1], F32)
    it.hot = sb("general_hot", [P, 8, BANK], F32)
    it.index = sb("general_index", [P, 8], U32)
    it.place = sb("general_place", [P, z.TILES], F32)
    it.sums = sb("general_sums", [z.D + 1, z.SEG * BANK], F32)
    it.stage = sb("general_stage", [z.D + 1, P], F32)
    it.acc = ctx.enter_context(nc.psum_tensor(f"general_acc_{tag}", [P, BANK], F32))
    it.turn = ctx.enter_context(nc.psum_tensor(f"general_turn_{tag}", [P, BANK], F32))
    return it



def general_width(z, kind):
    return {"degree": 1, "sum": z.D + 1, "relation": z.D}[kind]


def general_vector(v, z, m, w, s, kind):
    groups = z.TILES // 8
    c = Steps(v, s.own)
    c.did(v.memset(w.rows[:, :, z.D:z.D + 1], 1.0))
    if kind == "degree":
        c.did(v.tensor_copy(w.place[:, :], m.src_index[:, :]))
    else:
        c.did(v.tensor_tensor(w.place[:, :], m.in_window[:, :], m.tile_base[:, :], ALU.add))
    c.wait()
    v.sem_inc(s.moved, 1)
    with v.Fori(0, z.SEG) as p:
        with v.Fori(0, groups) as i:
            v.wait_ge(s.used, p * groups + i + 1)
            for j in range(8):
                ins = v.tensor_scalar(w.hot[:, j, :], m.iota_row[:, :], w.place[:, bass.ds(8 * i + j, 1)], None,
                                      ALU.is_equal)
            ins.then_inc(s.hot, 1)
        v.wait_ge(s.summed, p + 1)
        v.tensor_copy(w.sums[0:general_width(z, kind), bass.ds(BANK * p, BANK)],
                      w.acc[0:general_width(z, kind), :]).then_inc(s.own, 1)
        v.tensor_scalar(w.place[:, :], w.place[:, :], -float(BANK), None, ALU.add).then_inc(s.own, 1)
        v.wait_ge(s.own, 2 * p + (c.n + 2))
        v.sem_inc(s.moved, 1)
    with v.Fori(0, z.NB) as b:
        v.wait_ge(s.turned, b + 1)
        if kind == "degree":
            v.tensor_copy(m.deg_out[:, bass.ds(b, 1)], w.turn[:, 0:1]).then_inc(s.placed, 1)
        else:
            if kind == "sum":
                v.tensor_copy(m.deg_in[:, bass.ds(b, 1)], w.turn[:, z.D:z.D + 1])
            v.tensor_copy(m.s[:, bass.ds(b, 1), :].rearrange("p b f -> p (b f)"), w.turn[:, 0:z.D]).then_inc(s.placed, 1)
    v.wait_ge(s.placed, z.NB + 1)


def general_tensor(t, z, m, w, s, kind):
    groups = z.TILES // 8
    R = general_width(z, kind)
    t.sem_inc(s.used, 1)
    with t.Fori(0, z.SEG) as p:
        t.wait_ge(s.moved, p + 1)
        t.nop(nofuse=True)
        t.matmul(w.acc[0:R, :], m.zeros[0:1, 0:R], m.zeros[0:1, :], start=True, stop=False)
        with t.Fori(0, groups) as i:
            t.wait_ge(s.hot, p * groups + i + 1)
            if kind != "degree":
                t.wait_ge(s.rows, (p * groups + i) * 128 + 128)
            t.nop(nofuse=True)
            for j in range(8):
                rows = m.ones[:, 0:1] if kind == "degree" else w.rows[:, j, 0:R]
                mm = t.matmul(w.acc[0:R, :], rows, w.hot[:, j, :], start=False, stop=False)
            mm.then_inc(s.used, 1)
        t.matmul(w.acc[0:R, :], m.zeros[0:1, 0:R], m.zeros[0:1, :], start=False, stop=True).then_inc(s.summed, 1)
    t.sem_inc(s.placed, 1)
    with t.Fori(0, z.NB) as b:
        t.wait_ge(s.placed, b + 1)
        t.wait_ge(s.staged, b + 1)
        t.nop(nofuse=True)
        t.transpose(w.turn[:, 0:R], w.stage[0:R, :], m.ident[0:R, 0:R]).then_inc(s.turned, 1)


def general_scalar(a, z, m, w, s, kind):
    groups = z.TILES // 8
    R = general_width(z, kind)
    if kind != "degree":
        index = m.src_index if kind == "sum" else m.row_index
        with a.Fori(0, z.SEG) as p:
            with a.Fori(0, groups) as i:
                a.wait_ge(s.used, p * groups + i + 1)
                a.copy(w.index[:, :], index[:, bass.ds(8 * i, 8)]).then_inc(s.index, 1)
    a.wait_ge(s.moved, z.SEG + 1)
    with a.Fori(0, z.NB) as b:
        a.wait_ge(s.placed, b + 1)
        a.copy(w.stage[0:R, :], w.sums[0:R, bass.ds(P * b, P)]).then_inc(s.staged, 1)


def general_gpsimd(g, z, m, d, w, s, kind):
    if kind == "degree":
        g.nop(nofuse=True)
        return
    groups = z.TILES // 8
    table = d.g_table if kind == "sum" else d.t_table.rearrange("n r f -> (n r) f")
    with g.Fori(0, z.SEG) as p:
        with g.Fori(0, groups) as i:
            g.wait_ge(s.index, p * groups + i + 1)
            g.nop(nofuse=True)
            for j in range(8):
                g.indirect_dma_start(w.rows[:, j, 0:z.D], None, table,
                                     bass.IndirectOffsetOnAxis(ap=w.index[:, j:j + 1], axis=0)).then_inc(s.rows, 16)


def parts(nc, z, m, d, sem, layer):
    y_ready, root_ready, step, g_ready, g_out = (sem(f"{n}{layer}") for n in (
        "degree_ready", "degree_root", "parts_step", "g_ready", "g_stored"))
    full = [P, z.NB, z.D]
    with ExitStack() as ctx:
        rest = ctx.enter_context(nc.sbuf_tensor(f"rest{layer}", full, F32))
        with nc.Block() as block:

            @block.vector
            def _(v):
                c = Steps(v, step)
                if layer == 0:
                    c.did(v.tensor_scalar(m.stat[:, 0, :], m.deg_out[:, :], 1.0, None, ALU.max))
                    c.did(v.memset(m.parts[:, :, PIECES * z.D:], 1.0))
                    c.wait()
                    v.sem_inc(y_ready, 1)
                    inverse_root(v, c, m.stat[:, 0, :], m.do[:, :], m.stat[:, 1, :], root_ready, 1)
                piece = lambda k: m.parts[:, :, k * z.D:(k + 1) * z.D]
                c.did(v.tensor_tensor(m.s[:, :, :], m.h[:, :, :], bcast(m.do[:, :], 2, full), ALU.mult))
                c.wait()
                v.sem_inc(g_ready, 1)
                c.did(v.tensor_copy(piece(0), m.s[:, :, :]))
                c.wait()
                c.did(v.tensor_tensor(rest[:, :, :], m.s[:, :, :], piece(0), ALU.subtract))
                c.wait()
                c.did(v.tensor_copy(piece(1), rest[:, :, :]))
                c.wait()
                c.did(v.tensor_tensor(rest[:, :, :], rest[:, :, :], piece(1), ALU.subtract))
                c.wait()
                c.did(v.tensor_copy(piece(2), rest[:, :, :]))
                c.wait()

            @block.scalar
            def _(a):
                if layer == 0:
                    a.wait_ge(y_ready, 1)
                    a.activation(m.do[:, :], m.stat[:, 0, :], ACT.Sqrt).then_inc(root_ready, 1)

            @block.sync
            def _(sp):
                bad = sp.value_load(m.flag[0:1, 0:1], min_val=0, max_val=1024)
                with sp.If(bad > 0):
                    sp.wait_ge(g_ready, 1)
                    sp.dma_start(d.g_table.rearrange("(b p) f -> p b f", p=P), m.s[:, :, :]).then_inc(g_out, 16)
                    sp.wait_ge(g_out, 16)


def aggregate(nc, z, m, d, sem, layer):
    blocks_made, sums_out, step, y_ready, root_ready = (sem(f"{n}{layer}") for n in (
        "block_made", "sums_out", "aggregate_step", "in_degree_ready", "in_degree_root"))
    loaded = [sem(f"a_block_loaded{layer}{i}") for i in range(3)]
    cols = PIECES * z.D + 1
    with ExitStack() as ctx:
        a_in = ctx.enter_context(nc.sbuf_tensor(f"a_in{layer}", [P, 3, z.GB * z.KEYS], BF16))
        bank = [ctx.enter_context(nc.psum_tensor(f"sums{layer}{i}", [P, BANK], F32)) for i in range(3)]
        general = general_buffers(nc, z, ctx, f"sum{layer}")
        gsem = general_semaphores(sem, f"sum{layer}")
        whole = z.NB // 3

        def over_blocks(eng, one):
            with eng.Fori(0, whole) as i:
                for u in range(3):
                    one(3 * i + u, i, u)
            for u in range(z.NB - 3 * whole):
                one(3 * whole + u, whole, u)

        with nc.Block() as block:

            @block.sync
            def _(sp):
                bad = sp.value_load(m.flag[0:1, 0:1], min_val=0, max_val=1024)
                with sp.If(bad > 0):
                    sp.nop(nofuse=True)
                with sp.Else():
                    def load(b, i, u):
                        sp.wait_ge(blocks_made, b + 1)
                        sp.nop(nofuse=True)
                        sp.dma_start(a_in[:, u, :], d.a[bass.ds(b, 1), :, :].rearrange("b p k -> (b p) k"))\
                          .then_inc(loaded[u], 16)
                    over_blocks(sp, load)

            @block.tensor
            def _(t):
                bad = t.value_load(m.flag[0:1, 0:1], min_val=0, max_val=1024)
                with t.If(bad > 0):
                    general_tensor(t, z, m, general, gsem, "sum")
                with t.Else():
                    t.sem_inc(blocks_made, 3)
                    t.sem_inc(sums_out, 3)

                    def products(b, i, u):
                        t.wait_ge(loaded[u], 16 * i + 16)
                        t.wait_ge(sums_out, b + 1)
                        for k in range(z.NB):
                            mm = t.matmul(bank[u][:, 0:cols], a_in[:, u, k::z.NB], m.parts[:, k, :],
                                          start=(k == 0), stop=(k == z.NB - 1))
                        mm.then_inc(blocks_made, 1)
                    over_blocks(t, products)

            @block.vector
            def _(v):
                bad = v.value_load(m.flag[0:1, 0:1], min_val=0, max_val=1024)
                with v.If(bad > 0):
                    general_vector(v, z, m, general, gsem, "sum")
                with v.Else():
                    def sums(b, i, u):
                        v.wait_ge(blocks_made, b + 4)
                        if layer == 0:
                            v.tensor_copy(m.deg_in[:, bass.ds(b, 1)], bank[u][:, cols - 1:cols])
                        v.tensor_reduce(m.s[:, bass.ds(b, 1), :].rearrange("p b f -> p (b f)"),
                                        bank[u][:, 0:cols - 1].rearrange("p (k f) -> p f k", k=PIECES),
                                        X, ALU.add).then_inc(sums_out, 1)
                    over_blocks(v, sums)
                    v.wait_ge(sums_out, z.NB + 3)
                if layer == 0:
                    c = Steps(v, step)
                    c.did(v.tensor_scalar(m.stat[:, 0, :], m.deg_in[:, :], 1.0, None, ALU.max))
                    c.wait()
                    v.sem_inc(y_ready, 1)
                    inverse_root(v, c, m.stat[:, 0, :], m.di[:, :], m.stat[:, 1, :], root_ready, 1)

            @block.scalar
            def _(a):
                bad = a.value_load(m.flag[0:1, 0:1], min_val=0, max_val=1024)
                with a.If(bad > 0):
                    general_scalar(a, z, m, general, gsem, "sum")
                if layer == 0:
                    a.wait_ge(y_ready, 1)
                    a.activation(m.di[:, :], m.stat[:, 0, :], ACT.Sqrt).then_inc(root_ready, 1)

            @block.gpsimd
            def _(g):
                bad = g.value_load(m.flag[0:1, 0:1], min_val=0, max_val=1024)
                with g.If(bad > 0):
                    general_gpsimd(g, z, m, d, general, gsem, "sum")


CHUNK = 7
HALVES = ((0, 4), (4, 3))


def convolve(nc, z, m, d, sem, layer):
    uv_ready, turned, uvt_ready, made, used, step = (sem(f"{n}{layer}") for n in (
        "uv_ready", "uv_turned", "uvt_ready", "conv_made", "conv_used", "conv_step"))
    assert z.NB % CHUNK == 0 and 2 * z.D == P
    with ExitStack() as ctx:
        sb = lambda n, s: ctx.enter_context(nc.sbuf_tensor(n, s, F32))
        uv = [sb(f"uv{layer}{i}", [P, n, 2, z.D]) for i, (_, n) in enumerate(HALVES)]
        ds_ = [sb(f"di_s{layer}{i}", [P, n, z.D]) for i, (_, n) in enumerate(HALVES)]
        uvt = [sb(f"uvt{layer}{i}", [P, n * P]) for i, (_, n) in enumerate(HALVES)]
        tb = [ctx.enter_context(nc.psum_tensor(f"uv_turn{layer}{i}", [P, BANK], F32)) for i in range(2)]
        ob = [ctx.enter_context(nc.psum_tensor(f"conv_out{layer}{i}", [P, BANK], F32)) for i in range(2)]
        with nc.Block() as block:

            @block.vector
            def _(v):
                steps = 8
                with v.Fori(0, z.NB // CHUNK) as i:
                    own = 0

                    def did(ins):
                        nonlocal own
                        own += 1
                        ins.then_inc(step, 1)
                        v.wait_ge(step, i * steps + own)
                    for h, (b0, n) in enumerate(HALVES):
                        at = bass.ds(CHUNK * i + b0, n)
                        v.wait_ge(turned, 2 * i + (h + 1))
                        did(v.tensor_tensor(ds_[h][:, :, :], m.s[:, at, :], bcast(m.di[:, at], 2, [P, n, z.D]), ALU.mult))
                        did(v.tensor_tensor(uv[h][:, :, 0, :], ds_[h][:, :, :], m.h[:, at, :], ALU.add))
                        did(v.tensor_tensor(uv[h][:, :, 1, :], ds_[h][:, :, :], m.h[:, at, :], ALU.mult))
                        v.sem_inc(uv_ready, 1)
                    for h, (b0, n) in enumerate(HALVES):
                        at = bass.ds(CHUNK * i + b0, n)
                        v.wait_ge(made, 2 * i + (h + 1))
                        out = ob[h][:, 0:n * z.D].rearrange("p (b f) -> p b f", b=n)
                        if layer == 0:
                            did(v.tensor_scalar(m.h[:, at, :], out, 0.0, None, ALU.max))
                        else:
                            did(v.tensor_tensor(m.x[:, at, :], out, m.x[:, at, :], ALU.add))
                        v.sem_inc(used, 1)

            @block.tensor
            def _(t):
                t.sem_inc(turned, 2)
                t.sem_inc(used, 2)
                t.sem_inc(uvt_ready, 2)
                with t.Fori(0, z.NB // CHUNK) as i:
                    for h, (b0, n) in enumerate(HALVES):
                        t.wait_ge(uv_ready, 2 * i + (h + 1))
                        t.wait_ge(uvt_ready, 2 * i + (h + 1))
                        for j in range(n):
                            mm = t.transpose(tb[h][:, j * P:(j + 1) * P], uv[h][:, j, :, :].rearrange("p k f -> p (k f)"),
                                             m.ident[:, :])
                        mm.then_inc(turned, 1)
                    for h, (b0, n) in enumerate(HALVES):
                        t.wait_ge(uvt_ready, 2 * i + (h + 3))
                        t.wait_ge(used, 2 * i + (h + 1))
                        for j in range(n):
                            mm = t.matmul(ob[h][:, j * z.D:(j + 1) * z.D], uvt[h][:, j * P:(j + 1) * P],
                                          m.w12[:, layer, :], start=True, stop=True)
                        mm.then_inc(made, 1)

            @block.scalar
            def _(a):
                with a.Fori(0, z.NB // CHUNK) as i:
                    for h, (b0, n) in enumerate(HALVES):
                        a.wait_ge(turned, 2 * i + (h + 3))
                        a.copy(uvt[h][:, :], tb[h][:, 0:n * P]).then_inc(uvt_ready, 1)


def norm_again(nc, z, m, sem):
    var_ready, root_ready, step = sem("var1_ready"), sem("root1_ready"), sem("norm1_step")
    with nc.Block() as block:

        @block.vector
        def _(v):
            c = Steps(v, step)
            layernorm_relu(v, c, z, m.x[:, :, :], m.h[:, :, :], m.s[:, :, :], m.stat, EPS, var_ready, root_ready, 1)

        @block.scalar
        def _(a):
            a.wait_ge(var_ready, 1)
            a.activation(m.stat[:, 2, :], m.stat[:, 1, :], ACT.Sqrt).then_inc(root_ready, 1)


def relation_table(nc, z, m, d, sem):
    staged, turned, ht_ready, block_made, by_scalar, by_vector = (sem(n) for n in (
        "h_staged", "h_turned", "ht_ready", "table_made", "copied_by_scalar", "copied_by_vector"))
    stored = [sem(f"table_stored{i}") for i in range(2)]
    RF = z.R * z.D
    with ExitStack() as ctx:
        sb = lambda n, s: ctx.enter_context(nc.sbuf_tensor(n, s, F32))
        hs = [sb(f"hs{i}", [P, n, z.D]) for i, (_, n) in enumerate(HALVES)]
        ht = [sb(f"ht{i}", [z.D, n * P]) for i, (_, n) in enumerate(HALVES)]
        tab = [sb(f"tab{i}", [P, n, RF]) for i, (_, n) in enumerate(HALVES)]
        tb = [ctx.enter_context(nc.psum_tensor(f"h_turn{i}", [P, BANK], F32)) for i in range(2)]
        bank = [ctx.enter_context(nc.psum_tensor(f"table{i}", [P, BANK], F32)) for i in range(4)]
        with nc.Block() as block:

            @block.tensor
            def _(t):
                for s, n in ((turned, 2), (ht_ready, 2), (by_scalar, 2), (by_vector, 1)):
                    t.sem_inc(s, n)
                with t.Fori(0, z.NB // CHUNK) as i:
                    for h, (b0, n) in enumerate(HALVES):
                        t.wait_ge(staged, 2 * i + (h + 1))
                        t.wait_ge(ht_ready, 2 * i + (h + 1))
                        t.nop(nofuse=True)
                        for j in range(n):
                            mm = t.transpose(tb[h][0:z.D, j * P:(j + 1) * P], hs[h][:, j, :], m.ident[:, :])
                        mm.then_inc(turned, 1)
                    for h, (b0, n) in enumerate(HALVES):
                        t.wait_ge(ht_ready, 2 * i + (h + 3))
                        for j in range(n):
                            at = b0 + j
                            if at % 2 == 0:
                                t.wait_ge(by_scalar, 4 * i + (at // 2 + 1))
                            else:
                                t.wait_ge(by_vector, 3 * i + (at // 2 + 1))
                            t.matmul(bank[at % 4][:, 0:RF], ht[h][:, j * P:(j + 1) * P],
                                     m.w3[:, :, :].rearrange("d r f -> d (r f)"), start=True, stop=True
                                     ).then_inc(block_made, 1)

            @block.scalar
            def _(a):
                with a.Fori(0, z.NB // CHUNK) as i:
                    for h, (b0, n) in enumerate(HALVES):
                        a.wait_ge(turned, 2 * i + (h + 1))
                        a.copy(hs[h][:, :, :], m.h[:, bass.ds(CHUNK * i + b0, n), :]).then_inc(staged, 1)
                    for h, (b0, n) in enumerate(HALVES):
                        a.wait_ge(stored[h], 16 * i + 16)
                        for j in range(n):
                            if (b0 + j) % 2 == 0:
                                a.wait_ge(block_made, CHUNK * i + (b0 + j + 1))
                                a.copy(tab[h][:, j, :], bank[(b0 + j) % 4][:, 0:RF]).then_inc(by_scalar, 1)

            @block.vector
            def _(v):
                with v.Fori(0, z.NB // CHUNK) as i:
                    for h, (b0, n) in enumerate(HALVES):
                        v.wait_ge(turned, 2 * i + (h + 3))
                        v.tensor_copy(ht[h][:, :], tb[h][0:z.D, 0:n * P]).then_inc(ht_ready, 1)
                    for h, (b0, n) in enumerate(HALVES):
                        v.wait_ge(stored[h], 16 * i + 16)
                        for j in range(n):
                            if (b0 + j) % 2 == 1:
                                v.wait_ge(block_made, CHUNK * i + (b0 + j + 1))
                                v.tensor_copy(tab[h][:, j, :], bank[(b0 + j) % 4][:, 0:RF]).then_inc(by_vector, 1)

            @block.sync
            def _(sp):
                sp.sem_inc(stored[0], 16)
                sp.sem_inc(stored[1], 16)
                table = d.t_table.rearrange("(b p) r f -> p b (r f)", p=P)
                with sp.Fori(0, z.NB // CHUNK) as i:
                    for h, (b0, n) in enumerate(HALVES):
                        sp.wait_ge(by_scalar, 4 * i + (2 + 2 * (h + 1)))
                        sp.nop(nofuse=True)
                        sp.wait_ge(by_vector, 3 * i + (1 + 2 + h))
                        sp.nop(nofuse=True)
                        sp.dma_start(table[:, bass.ds(CHUNK * i + b0, n), :], tab[h][:, :, :]).then_inc(stored[h], 16)
                for h in range(2):
                    sp.wait_ge(stored[h], 16 * (z.NB // CHUNK + 1))


GATHERS = 8
SLOTS = 4


def relate(nc, z, m, d, sem):
    index_ready, hot_ready, used, added = (sem(f"relate_{n}") for n in ("index", "hot", "used", "added"))
    rows_in = [sem(f"relation_rows_in{k}") for k in range(SLOTS)]
    staged, turned, placed = (sem(f"relate_{n}") for n in ("staged", "turned", "placed"))
    zeroed = sem("relate_zeroed")
    span = z.STEP * (GATHERS - 1) + WIN
    iters = z.TILES // (SLOTS * GATHERS)
    width = z.NP + 2 * P
    with ExitStack() as ctx:
        sb = lambda n, s, t: ctx.enter_context(nc.sbuf_tensor(n, s, t))
        general = general_buffers(nc, z, ctx, "relation")
        index = sb("relate_index", [P, SLOTS, GATHERS], U32)
        rows = sb("relate_rows", [P, SLOTS, GATHERS, z.D], F32)
        hot = sb("relate_hot", [P, 2, GATHERS, WIN], F32)
        sums = general.sums[0:z.D, 0:width]
        stage = [sb(f"relate_stage{i}", [z.D, n * P], F32) for i, (_, n) in enumerate(HALVES)]
        bank = [ctx.enter_context(nc.psum_tensor(f"window{i}", [P, BANK], F32)) for i in range(SLOTS)]
        tb = bank[0:2]
        gsem = general_semaphores(sem, "relation")
        with nc.Block() as block:

            @block.scalar
            def _(a):
                bad = a.value_load(m.flag[0:1, 0:1], min_val=0, max_val=1024)
                with a.If(bad > 0):
                    general_scalar(a, z, m, general, gsem, "relation")
                with a.Else():
                    with a.Fori(0, iters) as i:
                        for k in range(SLOTS):
                            a.wait_ge(used, SLOTS * i + (k + 1))
                            a.copy(index[:, k, :], m.row_index[:, bass.ds(GATHERS * (SLOTS * i + k), GATHERS)])\
                             .then_inc(index_ready, 1)
                    a.wait_ge(added, SLOTS * (iters + 1))
                    with a.Fori(0, z.NB // CHUNK) as i:
                        for h, (b0, n) in enumerate(HALVES):
                            a.wait_ge(turned, 2 * i + (h + 1))
                            a.copy(stage[h][:, :], sums[:, bass.ds(P * (CHUNK * i + b0) + MARGIN, n * P)])\
                             .then_inc(staged, 1)

            @block.gpsimd
            def _(g):
                bad = g.value_load(m.flag[0:1, 0:1], min_val=0, max_val=1024)
                with g.If(bad > 0):
                    general_gpsimd(g, z, m, d, general, gsem, "relation")
                with g.Else():
                    table = d.t_table.rearrange("n r f -> (n r) f")
                    with g.Fori(0, iters) as i:
                        for k in range(SLOTS):
                            g.wait_ge(index_ready, SLOTS * i + (k + 1))
                            g.nop(nofuse=True)
                            for j in range(GATHERS):
                                g.indirect_dma_start(rows[:, k, j, :], None, table,
                                                     bass.IndirectOffsetOnAxis(ap=index[:, k, j:j + 1], axis=0)
                                                     ).then_inc(rows_in[k], 16)

            @block.vector
            def _(v):
                bad = v.value_load(m.flag[0:1, 0:1], min_val=0, max_val=1024)
                with v.If(bad > 0):
                    general_vector(v, z, m, general, gsem, "relation")
                with v.Else():
                    v.memset(sums, 0.0).then_inc(added, SLOTS)
                    with v.Fori(0, iters) as i:
                        for k in range(SLOTS):
                            v.wait_ge(used, SLOTS * i + (k + 3))
                            v.tensor_tensor(hot[:, k % 2, :, :], bcast(m.iota_row[:, 0:WIN], 1, [P, GATHERS, WIN]),
                                            bcast(m.in_window[:, bass.ds(GATHERS * (SLOTS * i + k), GATHERS)], 2,
                                                  [P, GATHERS, WIN]), ALU.is_equal).then_inc(hot_ready, 1)
                            v.wait_ge(used, SLOTS * i + (k + 1 + SLOTS))
                            v.wait_ge(added, SLOTS * i + (k + SLOTS))
                            at = sums[:, bass.ds(z.STEP * GATHERS * (SLOTS * i + k), span)]
                            v.tensor_tensor(at, bank[k][0:z.D, 0:span], at, ALU.add).then_inc(added, 1)
                    with v.Fori(0, z.NB // CHUNK) as i:
                        for h, (b0, n) in enumerate(HALVES):
                            v.wait_ge(turned, 2 * i + (h + 3))
                            v.tensor_copy(m.s[:, bass.ds(CHUNK * i + b0, n), :],
                                          tb[h][:, 0:n * z.D].rearrange("p (b f) -> p b f", b=n)).then_inc(placed, 1)

            @block.tensor
            def _(t):
                bad = t.value_load(m.flag[0:1, 0:1], min_val=0, max_val=1024)
                with t.If(bad > 0):
                    general_tensor(t, z, m, general, gsem, "relation")
                with t.Else():
                    t.sem_inc(used, SLOTS)
                    with t.Fori(0, iters) as i:
                        for k in range(SLOTS):
                            t.wait_ge(added, SLOTS * i + (k + 1))
                            t.nop(nofuse=True)
                            t.matmul(bank[k][0:z.D, 0:span], m.zeros[0:1, 0:z.D], m.zeros[0:1, 0:span],
                                     start=True, stop=False)
                            t.wait_ge(hot_ready, SLOTS * i + (k + 1))
                            t.wait_ge(rows_in[k], 16 * GATHERS * i + 16 * GATHERS)
                            t.nop(nofuse=True)
                            for j in range(GATHERS):
                                mm = t.matmul(bank[k][0:z.D, z.STEP * j:z.STEP * j + WIN], rows[:, k, j, :],
                                              hot[:, k % 2, j, :], start=False, stop=(j == GATHERS - 1))
                            mm.then_inc(used, 1)
                    t.wait_ge(added, SLOTS * (iters + 1))
                    t.sem_inc(turned, 2)
                    t.sem_inc(placed, 2)
                    with t.Fori(0, z.NB // CHUNK) as i:
                        for h, (b0, n) in enumerate(HALVES):
                            t.wait_ge(staged, 2 * i + (h + 1))
                            t.wait_ge(placed, 2 * i + (h + 1))
                            t.nop(nofuse=True)
                            for j in range(n):
                                mm = t.transpose(tb[h][:, j * z.D:(j + 1) * z.D], stage[h][:, j * P:(j + 1) * P],
                                                 m.ident[0:z.D, 0:z.D])
                            mm.then_inc(turned, 1)


def finish(nc, z, m, d, sem):
    step, ready, out_sem = sem("finish_step"), sem("out_ready"), sem("out_stored")
    full = [P, z.NB, z.D]
    rem = z.N - (z.NB - 1) * P
    with nc.Block() as block:

        @block.vector
        def _(v):
            c = Steps(v, step)
            some, factor_h, factor_m = (m.stat[:, i, :] for i in range(3))
            c.did(v.tensor_scalar(some, m.deg_in[:, :], 0.0, None, ALU.is_gt))
            c.did(v.tensor_scalar(factor_m, m.deg_in[:, :], 1.0, None, ALU.max))
            c.wait()
            c.did(v.tensor_scalar(factor_h, some, 0.2 - 1.0, 1.0, ALU.mult, ALU.add))
            c.did(v.reciprocal(factor_m, factor_m))
            c.wait()
            c.did(v.tensor_scalar(factor_m, factor_m, 1.0 - 0.2, None, ALU.mult))
            c.did(v.tensor_tensor(m.h[:, :, :], m.h[:, :, :], bcast(factor_h, 2, full), ALU.mult))
            c.wait()
            c.did(v.tensor_tensor(m.s[:, :, :], m.s[:, :, :], bcast(factor_m, 2, full), ALU.mult))
            c.wait()
            c.did(v.tensor_tensor(m.s[:, :, :], m.s[:, :, :], m.h[:, :, :], ALU.add))
            c.wait()
            c.did(v.scalar_tensor_tensor(out=m.s[:, :, :], in0=m.s[:, :, :], scalar=0.0, in1=m.x[:, :, :],
                                         op0=ALU.max, op1=ALU.add))
            c.wait()
            v.sem_inc(ready, 1)

        @block.sync
        def _(sp):
            sp.wait_ge(ready, 1)
            sp.dma_start(d.out[0:(z.NB - 1) * P, :].rearrange("(b p) f -> p b f", p=P),
                         m.s[:, 0:z.NB - 1, :]).then_inc(out_sem, 16)
            sp.dma_start(d.out[(z.NB - 1) * P:z.N, :], m.s[0:rem, z.NB - 1, :]).then_inc(out_sem, 16)
            sp.wait_ge(out_sem, 32)


def program(nc, x, src, dst, etype, w1_1, w2_1, w1_2, w2_2, w3, out, stop=None):
    z = sizes(x.shape[0], src.shape[0], x.shape[1], w3.shape[0])
    dram = lambda n, s, t: nc.dram_tensor(n, s, t, kind="Internal").ap()
    d = Named()
    d.x = x
    d.src = src
    d.dst = dst
    d.etype = etype
    d.w1_1 = w1_1
    d.w2_1 = w2_1
    d.w1_2 = w1_2
    d.w2_2 = w2_2
    d.w3 = w3
    d.out = out
    d.scr = dram("edge_fields", (2, z.SCR), F32)
    d.rows = dram("edge_rows", (z.TROWS, 2, P), F32)
    d.a = dram("adjacency", (z.NB, P, z.GB * z.KEYS), BF16)
    d.g_table = dram("g_rows", (z.NP, z.D), F32)
    d.t_table = dram("relation_rows", (z.NP, z.R, z.D), F32)
    with ExitStack() as ctx:
        sb = lambda n, s, t: ctx.enter_context(nc.sbuf_tensor(n, s, t))
        sem = lambda n: ctx.enter_context(nc.semaphore(n))
        nodes = [P, z.NB, z.D]
        m = Named()
        m.x = sb("x", nodes, F32)
        m.h = sb("h", nodes, F32)
        m.s = sb("s", nodes, F32)
        m.low = sb("low", [P, z.NB * z.CT], BF16)
        m.key = sb("key", [P, z.NB * z.CT], F32)
        m.row_index = sb("row_index", [P, z.TILES], U32)
        m.src_index = sb("src_index", [P, z.TILES], U32)
        m.in_window = sb("in_window", [P, z.TILES], F32)
        m.tile_base = sb("tile_base", [P, z.TILES], F32)
        m.deg_out = sb("deg_out", [P, z.NB], F32)
        m.deg_in = sb("deg_in", [P, z.NB], F32)
        m.do = sb("do", [P, z.NB], F32)
        m.di = sb("di", [P, z.NB], F32)
        m.stat = sb("stat", [P, 4, z.NB], F32)
        m.w12 = sb("w12", [P, 2, z.D], F32)
        m.w3 = sb("w3", [z.D, z.R, z.D], F32)
        m.iota_row = sb("iota_row", [P, BANK], F32)
        m.iota_part = sb("iota_part", [P, 1], F32)
        m.iota_keys = sb("iota_keys", [P, z.KEYS], F16)
        m.iota_low = sb("iota_low", [P, P, 12], BF16)
        m.ident = sb("ident", [P, P], F32)
        m.ident16 = sb("ident16", [P, P], BF16)
        m.before = sb("before", [P, P], F32)
        m.zeros = sb("zeros", [P, BANK], F32)
        m.ones = sb("ones", [P, 1], F32)
        m.ones16 = sb("ones16", [P, 1, 2], BF16)
        m.flag = sb("flag", [1, 1], I32)

        def later():
            m.parts = sb("parts", [P, z.NB, PIECES * z.D + 1], BF16)

        stages = [
            lambda: constants(nc, z, m, sem),
            lambda: prepare(nc, z, m, d, sem),
            later,
            lambda: build(nc, z, m, d, sem),
            lambda: parts(nc, z, m, d, sem, 0),
            lambda: aggregate(nc, z, m, d, sem, 0),
            lambda: convolve(nc, z, m, d, sem, 0),
            lambda: parts(nc, z, m, d, sem, 1),
            lambda: aggregate(nc, z, m, d, sem, 1),
            lambda: convolve(nc, z, m, d, sem, 1),
            lambda: norm_again(nc, z, m, sem),
            lambda: relation_table(nc, z, m, d, sem),
            lambda: relate(nc, z, m, d, sem),
            lambda: finish(nc, z, m, d, sem),
        ]
        for stage in stages[:stop]:
            stage()
        return m


_INS = ["x", "src", "dst", "edge_type_8", "L0_gnn_W1_1", "L0_gnn_W2_1", "L0_gnn_W1_2", "L0_gnn_W2_2",
        "L1_gnn_weight_r"]


def kernel(**inputs):
    import numpy as np
    import concourse.bacc as bacc
    from concourse.bass_utils import run_bass_kernel_spmd

    nc = bacc.Bacc("TRN2", target_bir_lowering=False, num_devices=1)
    arrays, args = {}, []
    for name in _INS:
        a = np.ascontiguousarray(inputs[name])
        arrays[f"in_{name}"] = a
        args.append(nc.dram_tensor(f"in_{name}", a.shape, mybir.dt.from_np(a.dtype), kind="ExternalInput").ap())
    args.append(nc.dram_tensor("out", inputs["x"].shape, F32, kind="ExternalOutput").ap())
    program(nc, *args)
    return run_bass_kernel_spmd(nc, [arrays], core_ids=[0]).results[0]["out"]
```

```python
from contextlib import ExitStack

import concourse.bass as bass
from concourse import mybir

P = 128
F32 = mybir.dt.float32
BF16 = mybir.dt.bfloat16
F16 = mybir.dt.float16
I32 = mybir.dt.int32
U32 = mybir.dt.uint32
ALU = mybir.AluOpType
ACT = mybir.ActivationFunctionType
X = mybir.AxisListType.X
EPS = 1e-5
BANK = 512

GROUP = 8
ROW = 32
GROUP_TILES = 3
PIECES = 3
WIN = 128
MARGIN = 62
PAIR_ROW = 16
UNIT = 16
UNITS = 3
UNIT_PAIRS = UNIT // 2


class Named:
    pass


def sizes(N, E, D, R):
    z = Named()
    z.N = N
    z.E = E
    z.D = D
    z.R = R
    z.NB = -(-N // P)
    z.NP = z.NB * P
    z.DEG = z.NP // z.NB and E // N
    z.TILES = -(-E // (P * ROW)) * ROW
    z.EP = z.TILES * P
    z.QT = 14
    z.Q = z.TILES // z.QT
    z.QE = z.QT * P
    z.ROWS = z.EP // ROW
    z.TROWS = -(-(z.ROWS + 4 * GROUP_TILES) // 16) * 16
    z.SCR = ROW * (z.TROWS - 1) + P
    z.GB = P // GROUP
    z.CT = z.GB * GROUP_TILES
    z.KEYS = GROUP * z.NB
    z.STEP = 4
    z.SEG = -(-N // BANK)
    z.ITERS = (z.NP + P // 2) // (P + UNITS * UNIT)
    z.DENSE = z.ITERS * P - P // 2
    z.PAIR_BLOCK = z.DENSE // P
    z.PAIR_BLOCKS = z.NB - z.PAIR_BLOCK
    z.PB = P // 2
    z.PKEYS = 2 * R * z.NB
    z.PHEADS = z.QE // PAIR_ROW
    z.PBASE = (z.DENSE - (WIN - 1 - MARGIN)) // z.STEP * P // PAIR_ROW
    z.PROWS = z.EP // PAIR_ROW - z.PBASE
    z.FLAG_GROUPS = -(-N // GROUP)
    assert z.Q * z.QT == z.TILES and z.TILES * z.STEP == z.NP and z.KEYS <= BANK
    assert z.Q <= P and z.NB <= P and E > (z.Q - 1) * z.QE
    assert z.DENSE + z.ITERS * UNITS * UNIT == z.NP and z.DENSE % P == P // 2 and z.PKEYS == 2 * z.KEYS
    return z


class Count:

    def __init__(self, sem):
        self.sem, self.n = sem, 0


class Steps:

    def __init__(self, eng, count):
        self.eng, self.count = eng, count

    def did(self, instruction):
        self.count.n += 1
        instruction.then_inc(self.count.sem, 1)

    def wait(self):
        self.eng.wait_ge(self.count.sem, self.count.n)


def bcast(ap, axis, shape):
    return ap.unsqueeze(axis).broadcast_to(shape)


def layernorm_relu(v, c, z, m, src, dst, work, stat, times):
    full = [P, z.NB, z.D]
    mean, var, rstd, t = (stat[:, i, :] for i in range(4))
    c.wait()
    c.did(v.tensor_reduce(mean, src, X, ALU.add))
    c.wait()
    c.did(v.tensor_scalar(mean, mean, 1.0 / z.D, None, ALU.mult))
    c.wait()
    c.did(v.tensor_tensor(dst, src, bcast(mean, 2, full), ALU.subtract))
    c.wait()
    c.did(v.tensor_tensor(work, dst, dst, ALU.mult))
    c.wait()
    c.did(v.tensor_reduce(var, work, X, ALU.add))
    c.wait()
    c.did(v.tensor_scalar(var, var, 1.0 / z.D, EPS, ALU.mult, ALU.add))
    c.wait()
    inverse_root(v, c, m, var, rstd, t, times)
    c.did(v.tensor_tensor(dst, dst, bcast(rstd, 2, full), ALU.mult))
    c.wait()
    c.did(v.tensor_scalar(dst, dst, 0.0, None, ALU.max))
    c.wait()


def inverse_root(v, c, m, y, r, t, times):
    v.sem_inc(m.square, 1)
    v.wait_ge(m.root, times)
    c.did(v.reciprocal(r, r))
    c.wait()
    c.did(v.tensor_tensor(t, r, r, ALU.mult))
    c.wait()
    c.did(v.tensor_tensor(t, t, y, ALU.mult))
    c.wait()
    c.did(v.tensor_scalar(t, t, -0.5, 1.5, ALU.mult, ALU.add))
    c.wait()
    c.did(v.tensor_tensor(r, r, t, ALU.mult))
    c.wait()


def split(v, c, z, m, x, rest):
    piece = lambda k: m.parts[:, :, k * z.D:(k + 1) * z.D]
    c.did(v.tensor_copy(piece(0), x))
    c.wait()
    c.did(v.tensor_tensor(rest, x, piece(0), ALU.subtract))
    c.wait()
    c.did(v.tensor_copy(piece(1), rest))
    c.wait()
    c.did(v.tensor_tensor(rest, rest, piece(1), ALU.subtract))
    c.wait()
    c.did(v.tensor_copy(piece(2), rest))
    c.wait()


def constants(nc, z, m, sem):
    made = sem("constants_made")
    with nc.Block() as block:

        @block.gpsimd
        def _(g):
            small = dict(allow_small_or_imprecise_dtypes=True)
            g.iota(m.iota_row[:, :], pattern=[[1, BANK]], base=0, channel_multiplier=0, **small)
            g.iota(m.iota_part[:, :], pattern=[[0, 1]], base=0, channel_multiplier=1, **small)
            g.iota(m.iota_keys[:, :], pattern=[[1, z.PKEYS]], base=0, channel_multiplier=0, **small)
            g.iota(m.iota_low[:, :, :], pattern=[[1, P], [0, 12]], base=0, channel_multiplier=0,
                   **small).then_inc(made, 1)

        @block.vector
        def _(v):
            c = Steps(v, m.steps)
            v.wait_ge(made, 1)
            c.did(v.memset(m.zeros[:, :], 0.0))
            c.did(v.memset(m.ones[:, :], 1.0))
            c.did(v.memset(m.ones16[:, :, :], 1.0))
            c.did(v.tensor_scalar(m.ident[:, :], m.iota_row[:, 0:P], m.iota_part[:, 0:1], None, ALU.is_equal))
            c.did(v.tensor_scalar(m.ident16[:, :], m.iota_row[:, 0:P], m.iota_part[:, 0:1], None, ALU.is_equal))
            c.did(v.tensor_scalar(m.before[:, :], m.iota_row[:, 0:P], m.iota_part[:, 0:1], None, ALU.is_gt))
            c.wait()


def prepare(nc, z, m, d, sem):
    padded, src_in, dst_in, et_in, next_in = (sem(n) for n in (
        "padded", "src_in", "dst_in", "type_in", "next_in"))
    x_in, w_in, patterns = (sem(n) for n in ("x_in", "weights_in", "patterns"))
    fields, scr_out, rows_out, counted = (sem(n) for n in (
        "fields_ready", "scratch_written", "rows_written", "heads_hot"))
    c_made, c_copied, ct_made, ct_copied, pre_made = (sem(n) for n in (
        "counts_made", "counts_copied", "turned_counts", "turned_copied", "prefix_made"))
    starts, turned, bank_free = sem("starts_ready"), sem("tiles_turned"), sem("turn_bank_free")
    landed = [sem(f"group_rows_landed{i}") for i in range(4)]
    slots_free = sem("row_slots_free")
    bad_ready, bad_made, pad_ready = sem("bad_ready"), sem("bad_summed"), sem("pad_ready")
    pair_key_ready, pair_scr_out = sem("pair_key_ready"), sem("pair_key_written")
    pair_hot, pair_counted, pair_copied, pair_total, total_copied, pair_prefix = (sem(f"pairs_{n}") for n in (
        "hot", "counted", "copied", "total", "total_copied", "prefix"))
    flat_made, flat_bank = sem("flat_turned"), sem("flat_bank_free")
    rem = z.E - (z.Q - 1) * z.QE
    flat_groups = [(f, t, min(4, z.QT - t)) for f in range(3) for t in range(0, z.QT, 4)]

    with ExitStack() as ctx:
        sb = lambda n, s, t: ctx.enter_context(nc.sbuf_tensor(n, s, t))
        ps = lambda n, s: ctx.enter_context(nc.psum_tensor(n, s, F32))
        edge = [z.Q, z.QE]
        src_i, dst_i, et_i = sb("src_i", edge, I32), sb("dst_i", edge, I32), sb("type_i", edge, I32)
        high_i, low_i = sb("src_high", edge, I32), sb("src_low", edge, I32)
        low, key = sb("low_f", edge, F32), sb("key_f", edge, F32)
        dst, src, idx = sb("dst_f", edge, F32), sb("src_f", edge, F32), sb("row_f", edge, F32)
        centre = sb("centre", edge, F32)
        pair_key = low_i[:, :].bitcast(F32)
        pair_hi, pair_mid = (m.row_index[0:z.Q, i * z.PHEADS:(i + 1) * z.PHEADS].bitcast(I32) for i in range(2))
        H2 = z.PHEADS // 2
        as_hot = lambda b, n: b[0:z.Q, 0:n // 2].bitcast(BF16)
        hot_block = as_hot(m.h[:, :, :].rearrange("p b f -> p (b f)"), z.PHEADS * z.NB).rearrange("p (h n) -> p h n", n=z.NB)
        hot_pair = [as_hot(b, H2 * z.PB).rearrange("p (h n) -> p h n", n=z.PB)
                    for b in (m.s[:, :, :].rearrange("p b f -> p (b f)"), m.key[:, :])]
        pcnt, ptot = sb("pair_cnt", [z.PB, z.NB], F32), sb("pair_total", [z.NB, z.PB], F32)
        pstart, ones = sb("pair_start", [z.PB, z.PAIR_BLOCKS], F32), sb("prep_ones", [z.PB, z.PB], F32)
        pair_no, pover = sb("pair_no", [z.PB, z.PAIR_BLOCKS], F32), sb("pair_over", [z.PB, z.PAIR_BLOCKS], F32)
        next_i, next_f = sb("next_i", [z.Q, 1], I32), sb("next_f", [z.Q, 1], F32)
        bad = sb("bad", [P, 8], F32)
        bad1 = sb("bad1", [P, 1], F32)
        heads = z.QE // ROW
        head_hi, head_mid = sb("head_hi", [z.Q, heads], I32), sb("head_mid", [z.Q, heads], I32)
        hot_hi = sb("hot_hi", [z.Q, heads, z.NB], BF16)
        hot_mid = sb("hot_mid", [z.Q, heads, z.GB], BF16)
        cnt, cnt_t = sb("cnt", [z.NB, z.GB], F32), sb("cnt_t", [z.GB, z.NB], F32)
        total, total_b = sb("total", [z.NB, 1], F32), sb("total_b", [z.NB, z.GB], F32)
        start = sb("start", [z.NB, z.GB], F32)
        over = sb("over", [z.NB, z.GB], F32)
        group_no = sb("group_no", [z.NB, z.GB], F32)
        row_no = sb("row_no", [z.NB, z.GB, GROUP_TILES], U32)
        got = sb("got", [z.NB, 16, 2, P], F32)
        offset = sb("offset", [P, z.NB, z.GB, GROUP_TILES], F32)
        pad = sb("pad", [16, 3, (z.SCR - z.EP) // 16], F32)
        turn = [ps(f"turn{i}", [P, BANK]) for i in range(4)]
        p_cnt, p_misc = ps("p_cnt", [P, BANK]), ps("p_misc", [P, BANK])

        with nc.Block() as block:

            @block.sync
            def _(sp):
                sp.wait_ge(padded, 1)
                for ap, t, s in ((d.src, src_i, src_in), (d.dst, dst_i, dst_in), (d.etype, et_i, et_in)):
                    body = ap[0:(z.Q - 1) * z.QE].rearrange("(q e) -> q e", e=z.QE)
                    tail = ap[(z.Q - 1) * z.QE:z.E].rearrange("(q e) -> q e", q=1)
                    sp.dma_start(t[0:z.Q - 1, :], body).then_inc(s, 16)
                    sp.dma_start(t[z.Q - 1:z.Q, 0:rem], tail).then_inc(s, 16)
                sp.dma_start(next_i[0:z.Q - 1, :], bass.AP(d.dst.tensor, z.QE, [[z.QE, z.Q - 1], [1, 1]]),
                             allow_slow_non_contiguous=True).then_inc(next_in, 16)
                sp.wait_ge(fields, 1)
                sp.wait_ge(pad_ready, 1)
                for f, t in enumerate((low, key)):
                    sp.dma_start(d.scr[f, 0:z.EP].rearrange("(q e) -> q e", e=z.QE), t[:, :]).then_inc(scr_out, 16)
                    sp.dma_start(d.scr[f, z.EP:z.SCR].rearrange("(q e) -> q e", q=16), pad[:, f, :]).then_inc(scr_out, 16)
                sp.wait_ge(scr_out, 64)
                for f in range(2):
                    rows = bass.AP(d.scr.tensor, f * z.SCR, [[ROW, z.TROWS], [1, P]])
                    sp.dma_start(d.rows[:, f, :], rows).then_inc(rows_out, 16)
                sp.wait_ge(pair_key_ready, 1)
                sp.dma_start(d.scr[2, 0:z.EP].rearrange("(q e) -> q e", e=z.QE), pair_key).then_inc(pair_scr_out, 16)
                sp.dma_start(d.scr[2, z.EP:z.SCR].rearrange("(q e) -> q e", q=16), pad[:, 2, :]).then_inc(pair_scr_out, 16)
                sp.wait_ge(pair_scr_out, 32)
                for i, f in enumerate((0, 2)):
                    rows = bass.AP(d.scr.tensor, f * z.SCR + z.PBASE * PAIR_ROW, [[PAIR_ROW, z.PROWS], [1, P]])
                    sp.dma_start(d.pair_rows[:, i, :], rows).then_inc(m.pair_rows_out, 16)
                sp.wait_ge(rows_out, 32)

            @block.scalar
            def _(a):
                a.dma_start(m.x[:, 0:z.NB - 1, :], d.x[0:(z.NB - 1) * P, :].rearrange("(b p) f -> p b f", p=P)).then_inc(x_in, 16)
                a.wait_ge(padded, 2)
                a.dma_start(m.x[0:z.N - (z.NB - 1) * P, z.NB - 1, :], d.x[(z.NB - 1) * P:z.N, :]).then_inc(x_in, 16)
                for i, w in enumerate((d.w1_1, d.w2_1, d.w1_2, d.w2_2)):
                    a.dma_start(m.w12[z.D * (i % 2):z.D * (i % 2) + z.D, i // 2, :], w).then_inc(w_in, 16)
                a.dma_start(m.w3[:, :, :], d.w3.rearrange("r d f -> d r f")).then_inc(w_in, 16)
                a.wait_ge(m.square, 1)
                a.activation(m.stat[:, 2, :], m.stat[:, 1, :], ACT.Sqrt).then_inc(m.root, 1)
                a.wait_ge(w_in, 80)

            @block.gpsimd
            def _(g):
                small = dict(allow_small_or_imprecise_dtypes=True)
                g.iota(centre[:, :], pattern=[[z.STEP, z.QT], [0, P]], base=0,
                       channel_multiplier=z.STEP * z.QT, **small)
                g.iota(pair_no[:, :], pattern=[[z.PB, z.PAIR_BLOCKS]], base=z.PB * z.PAIR_BLOCK, channel_multiplier=1, **small)
                g.iota(group_no[:, :], pattern=[[1, z.GB]], base=0, channel_multiplier=z.GB, **small)
                g.iota(m.tile_base[:, :], pattern=[[z.STEP, z.TILES]], base=-MARGIN, channel_multiplier=0, **small)
                g.iota(offset[:, :, :, :], pattern=[[z.KEYS * z.GB, z.NB], [z.KEYS, z.GB], [0, GROUP_TILES]],
                       base=0, channel_multiplier=0, **small).then_inc(patterns, 1)
                g.wait_ge(starts, 1)
                g.wait_ge(rows_out, 32)
                for ct in range(z.CT):
                    k = ct // 4
                    if ct % 4 == 0 and k >= 4:
                        g.wait_ge(slots_free, k - 3)
                    c_, t_ = divmod(ct, GROUP_TILES)
                    g.indirect_dma_start(
                        got[:, ct % 16, :, :].rearrange("p f e -> p (f e)"), None,
                        d.rows.rearrange("r f e -> r (f e)"),
                        bass.IndirectOffsetOnAxis(ap=row_no[:, c_, t_:t_ + 1], axis=0),
                    ).then_inc(landed[k % 4], 16)

            @block.tensor
            def _(t):
                t.wait_ge(counted, 1)
                for h in range(heads):
                    mm = t.matmul(p_cnt[0:z.NB, 0:z.GB], hot_hi[:, h, :], hot_mid[:, h, :],
                                  start=(h == 0), stop=(h == heads - 1))
                mm.then_inc(c_made, 1)
                t.wait_ge(c_copied, 1)
                t.transpose(p_misc[0:z.GB, 0:z.NB], cnt[:, :], m.ident[0:z.NB, 0:z.NB]).then_inc(ct_made, 1)
                t.wait_ge(ct_copied, 1)
                t.matmul(p_cnt[0:z.NB, 64:64 + z.GB], cnt_t[:, :], m.before[0:z.GB, 0:z.GB], start=True, stop=False)
                t.matmul(p_cnt[0:z.NB, 64:64 + z.GB], m.before[0:z.NB, 0:z.NB], total_b[:, :],
                         start=False, stop=True).then_inc(pre_made, 1)
                t.wait_ge(pair_hot, 1)
                for h in range(z.PHEADS):
                    mm = t.matmul(p_cnt[0:z.PB, 128:128 + z.NB], hot_pair[h // H2][:, h % H2, :], hot_block[:, h, :],
                                  start=(h == 0), stop=(h == z.PHEADS - 1))
                mm.then_inc(pair_counted, 1)
                t.wait_ge(pair_copied, 1)
                t.matmul(p_misc[0:z.NB, 128:128 + z.PB], pcnt[:, :], ones[:, :], start=True, stop=True).then_inc(pair_total, 1)
                t.wait_ge(total_copied, 1)
                t.matmul(p_cnt[0:z.PB, 256:256 + z.NB], m.before[0:z.PB, 0:z.PB], pcnt[:, :], start=True, stop=False)
                t.matmul(p_cnt[0:z.PB, 256:256 + z.NB], ptot[:, :], m.before[0:z.NB, 0:z.NB],
                         start=False, stop=True).then_inc(pair_prefix, 1)
                t.wait_ge(bad_ready, 1)
                t.matmul(p_misc[0:1, 256:257], bad1[:, :], m.ones[:, 0:1], start=True, stop=True).then_inc(bad_made, 1)
                for n, (f, t0, cntt) in enumerate(flat_groups):
                    if n >= 4:
                        t.wait_ge(flat_bank, n - 3)
                    what = (idx, dst, src)[f]
                    for j in range(cntt):
                        mm = t.transpose(turn[n % 4][:, j * z.Q:(j + 1) * z.Q], what[:, (t0 + j) * P:(t0 + j + 1) * P],
                                         m.ident[0:z.Q, 0:z.Q])
                    mm.then_inc(flat_made, 1)
                for k in range(z.CT // 4):
                    t.wait_ge(landed[k % 4], 64 * (k // 4 + 1))
                    if k < 4:
                        t.wait_ge(flat_bank, len(flat_groups) - 3 + k)
                    else:
                        t.wait_ge(bank_free, k - 3)
                    for f in range(2):
                        for j in range(4):
                            at = (f * 4 + j) * z.NB
                            mm = t.transpose(turn[(len(flat_groups) + k) % 4][:, at:at + z.NB],
                                             got[:, (k % 4) * 4 + j, f, :], m.ident[0:z.NB, 0:z.NB])
                    mm.then_inc(turned, 1)

            @block.vector
            def _(v):
                c = Steps(v, m.steps)
                c.did(v.memset(src_i[:, rem:], z.NP - 1))
                c.did(v.memset(dst_i[:, rem:], z.NP - 1))
                c.did(v.memset(et_i[:, rem:], 0))
                c.did(v.memset(next_i[:, :], z.NP - 1))
                c.wait()
                v.sem_inc(padded, 1)
                c.did(v.memset(m.x[:, z.NB - 1, :], 0.0))
                c.wait()
                v.sem_inc(padded, 1)
                c.did(v.memset(pad[:, 0, :], 0.0))
                c.did(v.memset(pad[:, 1:3, :], -1.0))
                c.did(v.memset(ones[:, :], 1.0))
                c.did(v.memset(bad[:, :], 0.0))
                c.wait()
                v.sem_inc(pad_ready, 1)
                v.wait_ge(src_in, 32)
                c.did(v.tensor_scalar(high_i[:, :], src_i[:, :], 7, None, ALU.logical_shift_right))
                c.did(v.tensor_scalar(low_i[:, :], src_i[:, :], 127, None, ALU.bitwise_and))
                v.wait_ge(dst_in, 32)
                c.did(v.tensor_scalar(head_hi[:, :], dst_i[:, 0:z.QE:ROW], 7, None, ALU.logical_shift_right))
                c.did(v.tensor_scalar(head_mid[:, :], dst_i[:, 0:z.QE:ROW], 3, z.GB - 1,
                                      ALU.logical_shift_right, ALU.bitwise_and))
                c.wait()
                c.did(v.tensor_copy(low[:, :], low_i[:, :]))
                c.did(v.scalar_tensor_tensor(out=key[:, :], in0=dst_i[:, :], scalar=float(z.NB), in1=high_i[:, :],
                                             op0=ALU.mult, op1=ALU.add))
                c.wait()
                v.sem_inc(fields, 1)
                c.did(v.tensor_tensor(hot_hi[:, :, :], bcast(m.iota_row[0:z.Q, 0:z.NB], 1, [z.Q, heads, z.NB]),
                                      bcast(head_hi[:, :], 2, [z.Q, heads, z.NB]), ALU.is_equal))
                c.did(v.tensor_tensor(hot_mid[:, :, :], bcast(m.iota_row[0:z.Q, 0:z.GB], 1, [z.Q, heads, z.GB]),
                                      bcast(head_mid[:, :], 2, [z.Q, heads, z.GB]), ALU.is_equal))
                c.wait()
                v.sem_inc(counted, 1)
                c.did(v.tensor_copy(dst[:, :], dst_i[:, :]))
                c.did(v.tensor_copy(src[:, :], src_i[:, :]))
                v.wait_ge(et_in, 32)
                c.did(v.scalar_tensor_tensor(out=idx[:, :], in0=src_i[:, :], scalar=float(z.R), in1=et_i[:, :],
                                             op0=ALU.mult, op1=ALU.add))
                c.did(v.scalar_tensor_tensor(out=pair_key, in0=dst_i[:, :], scalar=float(z.R), in1=et_i[:, :],
                                             op0=ALU.mult, op1=ALU.add))
                v.wait_ge(c_made, 1)
                c.did(v.tensor_copy(cnt[:, :], p_cnt[0:z.NB, 0:z.GB]))
                c.wait()
                v.sem_inc(c_copied, 1)
                c.did(v.tensor_reduce(total[:, :], cnt[:, :], X, ALU.add))
                c.wait()
                c.did(v.tensor_copy(total_b[:, :], total[:, 0:1].broadcast_to([z.NB, z.GB])))
                v.wait_ge(ct_made, 1)
                c.did(v.tensor_copy(cnt_t[:, :], p_misc[0:z.GB, 0:z.NB]))
                c.wait()
                v.sem_inc(ct_copied, 1)
                v.wait_ge(pre_made, 1)
                c.did(v.tensor_scalar(start[:, :], p_cnt[0:z.NB, 64:64 + z.GB], -1.0, 0.0, ALU.add, ALU.max))
                c.wait()
                for t_ in range(GROUP_TILES):
                    c.did(v.tensor_scalar(row_no[:, :, t_], start[:, :], float(4 * t_), None, ALU.add))
                c.wait()
                v.sem_inc(starts, 1)
                c.did(v.scalar_tensor_tensor(out=pair_key, in0=pair_key, scalar=float(z.NB), in1=high_i[:, :],
                                             op0=ALU.mult, op1=ALU.add))
                c.did(v.tensor_scalar(pair_hi, dst_i[:, 0:z.QE:PAIR_ROW], 7, None, ALU.logical_shift_right))
                c.did(v.tensor_scalar(pair_mid, dst_i[:, 0:z.QE:PAIR_ROW], 1, z.PB - 1,
                                      ALU.logical_shift_right, ALU.bitwise_and))
                c.wait()
                v.sem_inc(pair_key_ready, 1)
                shape = [z.Q, z.PHEADS, z.NB]
                c.did(v.tensor_tensor(hot_block, bcast(m.iota_row[0:z.Q, 0:z.NB], 1, shape),
                                      bcast(pair_hi, 2, shape), ALU.is_equal))
                shape = [z.Q, H2, z.PB]
                for i in range(2):
                    c.did(v.tensor_tensor(hot_pair[i], bcast(m.iota_row[0:z.Q, 0:z.PB], 1, shape),
                                          bcast(pair_mid[:, i * H2:(i + 1) * H2], 2, shape), ALU.is_equal))
                c.wait()
                v.sem_inc(pair_hot, 1)
                v.wait_ge(pair_counted, 1)
                c.did(v.tensor_copy(pcnt[:, :], p_cnt[0:z.PB, 128:128 + z.NB]))
                c.wait()
                v.sem_inc(pair_copied, 1)
                v.wait_ge(pair_total, 1)
                c.did(v.tensor_copy(ptot[:, :], p_misc[0:z.NB, 128:128 + z.PB]))
                c.wait()
                v.sem_inc(total_copied, 1)
                v.wait_ge(pair_prefix, 1)
                c.did(v.tensor_scalar(pstart[:, :], p_cnt[0:z.PB, 256 + z.PAIR_BLOCK:256 + z.NB], -1.0 - z.PBASE, 0.0,
                                      ALU.add, ALU.max))
                c.wait()
                c.did(v.tensor_copy(m.pair_row[:, :], pstart[:, :]))
                v.wait_ge(next_in, 16)
                v.wait_ge(patterns, 1)
                c.did(v.tensor_tensor(et_i[:, 0:z.QE - 1], dst[:, 0:z.QE - 1], dst[:, 1:z.QE], ALU.is_gt))
                c.did(v.tensor_tensor(bad[0:z.Q, 1:2], dst[:, z.QE - 1:z.QE], next_i[:, :], ALU.is_gt))
                c.did(v.tensor_tensor(centre[:, :], dst[:, :], centre[:, :], ALU.subtract))
                c.did(v.tensor_scalar(over[:, :], cnt[:, :], float(4 * GROUP_TILES - 1), None, ALU.is_gt))
                c.did(v.tensor_scalar(pover[:, :], pcnt[:, z.PAIR_BLOCK:z.NB], float(P // PAIR_ROW - 1), None, ALU.is_gt))
                c.did(v.tensor_scalar(pair_no[:, :], pair_no[:, :], float(-(-z.N // 2)), None, ALU.is_lt))
                c.did(v.tensor_scalar(group_no[:, :], group_no[:, :], float(z.FLAG_GROUPS), None, ALU.is_lt))
                c.wait()
                c.did(v.tensor_reduce(bad[0:z.Q, 0:1], et_i[:, 0:z.QE - 1], X, ALU.max))
                c.did(v.tensor_reduce(bad[0:z.Q, 6:7], centre[:, :], X, ALU.max))
                c.did(v.tensor_reduce(bad[0:z.Q, 7:8], centre[:, :], X, ALU.min))
                c.did(v.tensor_tensor(over[:, :], over[:, :], group_no[:, :], ALU.mult))
                c.did(v.tensor_tensor(pover[:, :], pover[:, :], pair_no[:, :], ALU.mult))
                c.wait()
                c.did(v.tensor_scalar(bad[0:z.Q, 2:3], bad[0:z.Q, 6:7], float(WIN - 1 - MARGIN), None, ALU.is_gt))
                c.did(v.tensor_scalar(bad[0:z.Q, 3:4], bad[0:z.Q, 7:8], float(-MARGIN), None, ALU.is_lt))
                c.did(v.tensor_reduce(bad[0:z.NB, 4:5], over[:, :], X, ALU.max))
                c.did(v.tensor_reduce(bad[0:z.PB, 5:6], pover[:, :], X, ALU.max))
                c.wait()
                c.did(v.tensor_reduce(bad1[:, :], bad[:, 0:6], X, ALU.add))
                c.wait()
                v.sem_inc(bad_ready, 1)
                v.wait_ge(bad_made, 1)
                c.did(v.tensor_copy(m.flag[:, :], p_misc[0:1, 256:257]))
                for n, (f, t0, cntt) in enumerate(flat_groups):
                    v.wait_ge(flat_made, n + 1)
                    from_ = turn[n % 4][:, 0:cntt * z.Q].rearrange("p (j q) -> p q j", j=cntt)
                    at = lambda b: b[:, :].rearrange("p (q t) -> p q t", t=z.QT)[:, :, t0:t0 + cntt]
                    if f == 1:
                        c.did(v.tensor_tensor(at(m.in_window), from_, at(m.tile_base), ALU.subtract))
                    else:
                        c.did(v.tensor_copy(at((m.row_index, None, m.src_index)[f]), from_))
                    c.wait()
                    v.sem_inc(flat_bank, 1)
                v.wait_ge(x_in, 32)
                layernorm_relu(v, c, z, m, m.x[:, :, :], m.h[:, :, :], m.s[:, :, :], m.stat, 1)
                off = offset[:, :, :, :].rearrange("p b c t -> p b (c t)")
                for k in range(z.CT // 4):
                    v.wait_ge(turned, k + 1)
                    bank = turn[(len(flat_groups) + k) % 4]
                    half = 4 * z.NB
                    view = lambda b: b[:, :].rearrange("p (b c) -> p b c", c=z.CT)[:, :, 4 * k:4 * k + 4]
                    c.did(v.tensor_copy(view(m.low), bank[:, 0:half].rearrange("p (j b) -> p b j", j=4)))
                    c.did(v.tensor_tensor(view(m.key), bank[:, half:2 * half].rearrange("p (j b) -> p b j", j=4),
                                          off[:, :, 4 * k:4 * k + 4], ALU.subtract))
                    c.wait()
                    v.sem_inc(slots_free, 1)
                    v.sem_inc(bank_free, 1)
                c.wait()


def build(nc, z, m, d, sem):
    low_hot, key_hot, group_made, pair_copied = (sem(n) for n in (
        "low_hot", "key_hot", "group_made", "pair_copied"))
    stored = [sem(f"half_stored{i}") for i in range(2)]
    deg_made, step = sem("degrees_made"), sem("build_step")
    pairs = z.GB // 2
    half = z.GB * z.KEYS // 2
    with ExitStack() as ctx:
        sb = lambda n, s, t: ctx.enter_context(nc.sbuf_tensor(n, s, t))
        low = sb("low_hot_buf", [P, 2, P, 12], BF16)
        keys = sb("key_hot_buf", [P, 2, 12, z.KEYS], BF16)
        a_buf = sb("a_buf", [P, pairs, 2, z.KEYS], BF16)
        bank = [ctx.enter_context(nc.psum_tensor(f"pair{i}", [P, 2, BANK], F32)) for i in range(2)]
        degree = ctx.enter_context(nc.psum_tensor("degree", [P, BANK], F32))
        general = general_buffers(nc, z, ctx, "deg")
        gsem = general_run(m, sem, 0)

        with nc.Block() as block:

            @block.vector
            def _(v):
                bad = v.value_load(m.flag[0:1, 0:1], min_val=0, max_val=1024)
                with v.If(bad > 0):
                    general_vector(v, z, m, general, gsem, "degree")
                with v.Else():
                    with v.Fori(0, z.NB) as b:
                        for k in range(4):
                            v.wait_ge(group_made, z.GB * b + 4 * (k + 1))
                            v.tensor_tensor(low[:, k % 2, :, :], m.iota_low[:, :, :],
                                            bcast(m.low[:, bass.ds(z.CT * b + 12 * k, 12)], 1, [P, P, 12]),
                                            ALU.is_equal).then_inc(low_hot, 1)
                            for j in range(12):
                                ins = v.tensor_scalar(keys[:, k % 2, j, :], m.iota_keys[:, 0:z.KEYS],
                                                      m.key[:, bass.ds(z.CT * b + 12 * k + j, 1)], None, ALU.is_equal)
                                if j % GROUP_TILES == GROUP_TILES - 1:
                                    ins.then_inc(key_hot, 1)
                    v.wait_ge(deg_made, 1)
                    v.tensor_reduce(m.deg_out[:, :], degree[:, 0:z.KEYS].rearrange("p (g s) -> p s g", g=GROUP),
                                    X, ALU.add).then_inc(step, 1)
                    v.wait_ge(step, 1)

            @block.tensor
            def _(t):
                bad = t.value_load(m.flag[0:1, 0:1], min_val=0, max_val=1024)
                with t.If(bad > 0):
                    general_tensor(t, z, m, general, gsem, "degree")
                with t.Else():
                    t.sem_inc(group_made, 8)
                    t.sem_inc(pair_copied, 2)
                    t.matmul(degree[:, 0:z.KEYS], m.zeros[0:1, 0:P], m.zeros[0:1, 0:z.KEYS], start=True, stop=False)

                    def degrees_of(q):
                        for c in range(2):
                            mm = t.matmul(degree[:, 0:z.KEYS], m.ident16[:, :], a_buf[:, q, c, :],
                                          start=False, stop=False)
                        return mm

                    with t.Fori(0, z.NB) as b:
                        for q in range(pairs):
                            t.wait_ge(pair_copied, pairs * b + (q + 1))
                            for c in range(2):
                                g = 2 * q + c
                                if g % 4 == 0:
                                    t.wait_ge(low_hot, 4 * b + (g // 4 + 1))
                                t.wait_ge(key_hot, z.GB * b + (g + 1))
                                for j in range(GROUP_TILES):
                                    at = g * GROUP_TILES + j
                                    mm = t.matmul(bank[q % 2][:, c, 0:z.KEYS], low[:, at // 12 % 2, :, at % 12],
                                                  keys[:, at // 12 % 2, at % 12, :],
                                                  start=(j == 0), stop=(j == GROUP_TILES - 1))
                                mm.then_inc(group_made, 1)
                            if q >= 1:
                                t.wait_ge(pair_copied, pairs * b + (q + 2))
                                degrees_of(q - 1)
                        t.wait_ge(pair_copied, pairs * b + (pairs + 2))
                        degrees_of(pairs - 1)
                    t.matmul(degree[:, 0:z.KEYS], m.zeros[0:1, 0:P], m.zeros[0:1, 0:z.KEYS],
                             start=False, stop=True).then_inc(deg_made, 1)

            @block.scalar
            def _(a):
                bad = a.value_load(m.flag[0:1, 0:1], min_val=0, max_val=1024)
                with a.If(bad > 0):
                    general_scalar(a, z, m, general, gsem, "degree")
                with a.Else():
                    with a.Fori(0, z.NB) as b:
                        for q in range(pairs):
                            if q % (pairs // 2) == 0:
                                a.wait_ge(stored[q // (pairs // 2)], 16 * b + 16)
                            a.wait_ge(group_made, z.GB * b + (8 + 2 * (q + 1)))
                            a.copy(a_buf[:, q, :, :], bank[q % 2][:, :, 0:z.KEYS]).then_inc(pair_copied, 1)

            @block.gpsimd
            def _(g):
                bad = g.value_load(m.flag[0:1, 0:1], min_val=0, max_val=1024)
                with g.If(bad > 0):
                    general_gpsimd(g, z, m, d, general, gsem, "degree")

            @block.sync
            def _(sp):
                bad = sp.value_load(m.flag[0:1, 0:1], min_val=0, max_val=1024)
                with sp.If(bad > 0):
                    sp.nop(nofuse=True)
                with sp.Else():
                    sp.sem_inc(stored[0], 16)
                    sp.sem_inc(stored[1], 16)
                    flat = a_buf[:, :, :, :].rearrange("p q c k -> p (q c k)")
                    with sp.Fori(0, z.NB) as b:
                        for h in range(2):
                            sp.wait_ge(pair_copied, pairs * b + (2 + pairs // 2 * (h + 1)))
                            sp.nop(nofuse=True)
                            sp.dma_start(d.a[bass.ds(b, 1), :, h * half:(h + 1) * half].rearrange("b p k -> (b p) k"),
                                         flat[:, h * half:(h + 1) * half]).then_inc(stored[h], 16)
                    for h in range(2):
                        sp.wait_ge(stored[h], 16 * (z.NB + 1))


def general_semaphores(sem):
    it = Named()
    it.hot = sem("general_hot")
    it.index = sem("general_index")
    it.used = sem("general_used")
    it.summed = sem("general_summed")
    it.moved = sem("general_moved")
    it.staged = sem("general_staged")
    it.turned = sem("general_turned")
    it.placed = sem("general_placed")
    it.own = Count(sem("general_own"))
    return it


def general_run(m, sem, run):
    it = Named()
    it.run = run
    it.rows = [sem(f"general_rows{run}{j}") for j in range(8 if run > 0 else 0)]
    g = m.general
    it.hot, it.index, it.used, it.summed, it.moved = g.hot, g.index, g.used, g.summed, g.moved
    it.staged, it.turned, it.placed, it.own = g.staged, g.turned, g.placed, g.own
    return it


def general_buffers(nc, z, ctx, tag):
    sb = lambda n, s, t: ctx.enter_context(nc.sbuf_tensor(f"{n}_{tag}", s, t))
    it = Named()
    it.rows = sb("general_rows", [P, 8, z.D + 1], F32)
    it.hot = sb("general_hot", [P, 8, BANK], F32)
    it.index = sb("general_index", [P, 8], U32)
    it.place = sb("general_place", [P, z.TILES], F32)
    it.sums = sb("general_sums", [z.D + 1, z.SEG * BANK], F32)
    it.stage = sb("general_stage", [z.D + 1, P], F32)
    it.acc = ctx.enter_context(nc.psum_tensor(f"general_acc_{tag}", [P, BANK], F32))
    it.turn = ctx.enter_context(nc.psum_tensor(f"general_turn_{tag}", [P, BANK], F32))
    return it



def general_width(z, kind):
    return {"degree": 1, "sum": z.D + 1, "relation": z.D}[kind]


def general_vector(v, z, m, w, s, kind):
    groups = z.TILES // 8
    p0, b0 = s.run * z.SEG, s.run * z.NB
    c = Steps(v, s.own)
    c.did(v.memset(w.rows[:, :, z.D:z.D + 1], 1.0))
    if kind == "degree":
        c.did(v.tensor_copy(w.place[:, :], m.src_index[:, :]))
    else:
        c.did(v.tensor_tensor(w.place[:, :], m.in_window[:, :], m.tile_base[:, :], ALU.add))
    c.wait()
    v.sem_inc(s.moved, 1)
    before = s.own.n
    with v.Fori(0, z.SEG) as p:
        with v.Fori(0, groups) as i:
            v.wait_ge(s.used, p * groups + i + (p0 * groups + 1))
            for j in range(8):
                ins = v.tensor_scalar(w.hot[:, j, :], m.iota_row[:, :], w.place[:, bass.ds(8 * i + j, 1)], None,
                                      ALU.is_equal)
            ins.then_inc(s.hot, 1)
        v.wait_ge(s.summed, p + (p0 + 1))
        v.tensor_copy(w.sums[0:general_width(z, kind), bass.ds(BANK * p, BANK)],
                      w.acc[0:general_width(z, kind), :]).then_inc(s.own.sem, 1)
        v.tensor_scalar(w.place[:, :], w.place[:, :], -float(BANK), None, ALU.add).then_inc(s.own.sem, 1)
        v.wait_ge(s.own.sem, 2 * p + (before + 2))
        v.sem_inc(s.moved, 1)
    s.own.n += 2 * z.SEG
    with v.Fori(0, z.NB) as b:
        v.wait_ge(s.turned, b + (b0 + 1))
        if kind == "degree":
            v.tensor_copy(m.deg_out[:, bass.ds(b, 1)], w.turn[:, 0:1]).then_inc(s.placed, 1)
        else:
            if kind == "sum":
                v.tensor_copy(m.deg_in[:, bass.ds(b, 1)], w.turn[:, z.D:z.D + 1])
            v.tensor_copy(m.s[:, bass.ds(b, 1), :].rearrange("p b f -> p (b f)"), w.turn[:, 0:z.D]).then_inc(s.placed, 1)
    v.wait_ge(s.placed, b0 + z.NB + 1)


def general_tensor(t, z, m, w, s, kind):
    groups = z.TILES // 8
    p0, b0 = s.run * z.SEG, s.run * z.NB
    R = general_width(z, kind)
    if s.run == 0:
        t.sem_inc(s.used, 1)
        t.sem_inc(s.placed, 1)
    with t.Fori(0, z.SEG) as p:
        t.wait_ge(s.moved, p + (p0 + s.run + 1))
        t.nop(nofuse=True)
        t.matmul(w.acc[0:R, :], m.zeros[0:1, 0:R], m.zeros[0:1, :], start=True, stop=False)
        with t.Fori(0, groups) as i:
            t.wait_ge(s.hot, p * groups + i + (p0 * groups + 1))
            t.nop(nofuse=True)
            if kind != "degree":
                for j in range(8):
                    t.wait_ge(s.rows[j], (p * groups + i) * 16 + 16)
                    t.nop(nofuse=True)
            for j in range(8):
                rows = m.ones[:, 0:1] if kind == "degree" else w.rows[:, j, 0:R]
                mm = t.matmul(w.acc[0:R, :], rows, w.hot[:, j, :], start=False, stop=False)
            mm.then_inc(s.used, 1)
        t.matmul(w.acc[0:R, :], m.zeros[0:1, 0:R], m.zeros[0:1, :], start=False, stop=True).then_inc(s.summed, 1)
    with t.Fori(0, z.NB) as b:
        t.wait_ge(s.placed, b + (b0 + 1))
        t.wait_ge(s.staged, b + (b0 + 1))
        t.nop(nofuse=True)
        t.transpose(w.turn[:, 0:R], w.stage[0:R, :], m.ident[0:R, 0:R]).then_inc(s.turned, 1)


def general_scalar(a, z, m, w, s, kind):
    groups = z.TILES // 8
    p0, b0 = s.run * z.SEG, s.run * z.NB
    R = general_width(z, kind)
    if kind != "degree":
        index = m.src_index if kind == "sum" else m.row_index
        with a.Fori(0, z.SEG) as p:
            with a.Fori(0, groups) as i:
                a.wait_ge(s.used, p * groups + i + (p0 * groups + 1))
                a.copy(w.index[:, :], index[:, bass.ds(8 * i, 8)]).then_inc(s.index, 1)
    a.wait_ge(s.moved, (s.run + 1) * (z.SEG + 1))
    with a.Fori(0, z.NB) as b:
        a.wait_ge(s.placed, b + (b0 + 1))
        a.copy(w.stage[0:R, :], w.sums[0:R, bass.ds(P * b, P)]).then_inc(s.staged, 1)


def general_gpsimd(g, z, m, d, w, s, kind):
    if kind == "degree":
        g.nop(nofuse=True)
        return
    groups = z.TILES // 8
    i0 = (s.run - 1) * z.SEG * groups
    table = d.g_table if kind == "sum" else d.t_table.rearrange("n r f -> (n r) f")
    with g.Fori(0, z.SEG) as p:
        with g.Fori(0, groups) as i:
            g.wait_ge(s.index, p * groups + i + (i0 + 1))
            g.nop(nofuse=True)
            for j in range(8):
                g.indirect_dma_start(w.rows[:, j, 0:z.D], None, table,
                                     bass.IndirectOffsetOnAxis(ap=w.index[:, j:j + 1], axis=0)).then_inc(s.rows[j], 16)


def parts(nc, z, m, d, sem, layer):
    g_ready, g_out = (sem(f"{n}{layer}") for n in ("g_ready", "g_stored"))
    full = [P, z.NB, z.D]
    with ExitStack() as ctx:
        rest = ctx.enter_context(nc.sbuf_tensor(f"rest{layer}", full, F32))
        with nc.Block() as block:

            @block.vector
            def _(v):
                c = Steps(v, m.steps)
                if layer == 0:
                    c.did(v.tensor_scalar(m.stat[:, 0, :], m.deg_out[:, :], 1.0, None, ALU.max))
                    c.did(v.memset(m.parts[:, :, PIECES * z.D:], 1.0))
                    c.wait()
                    inverse_root(v, c, m, m.stat[:, 0, :], m.do[:, :], m.stat[:, 1, :], 2)
                c.did(v.tensor_tensor(m.s[:, :, :], m.h[:, :, :], bcast(m.do[:, :], 2, full), ALU.mult))
                c.wait()
                v.sem_inc(g_ready, 1)
                split(v, c, z, m, m.s[:, :, :], rest[:, :, :])

            @block.scalar
            def _(a):
                if layer == 0:
                    a.wait_ge(m.square, 2)
                    a.activation(m.do[:, :], m.stat[:, 0, :], ACT.Sqrt).then_inc(m.root, 1)

            @block.sync
            def _(sp):
                bad = sp.value_load(m.flag[0:1, 0:1], min_val=0, max_val=1024)
                with sp.If(bad > 0):
                    sp.wait_ge(g_ready, 1)
                    sp.dma_start(d.g_table.rearrange("(b p) f -> p b f", p=P), m.s[:, :, :]).then_inc(g_out, 16)
                    sp.wait_ge(g_out, 16)


def aggregate(nc, z, m, d, sem, layer):
    blocks_made, sums_out = (sem(f"{n}{layer}") for n in ("block_made", "sums_out"))
    loaded = [sem(f"a_block_loaded{layer}{i}") for i in range(3)]
    cols = PIECES * z.D + 1
    with ExitStack() as ctx:
        a_in = ctx.enter_context(nc.sbuf_tensor(f"a_in{layer}", [P, 3, z.GB * z.KEYS], BF16))
        bank = [ctx.enter_context(nc.psum_tensor(f"sums{layer}{i}", [P, BANK], F32)) for i in range(3)]
        general = general_buffers(nc, z, ctx, f"sum{layer}")
        gsem = general_run(m, sem, 1 + layer)
        whole = z.NB // 3

        def over_blocks(eng, one):
            with eng.Fori(0, whole) as i:
                for u in range(3):
                    one(3 * i + u, i, u)
            for u in range(z.NB - 3 * whole):
                one(3 * whole + u, whole, u)

        with nc.Block() as block:

            @block.sync
            def _(sp):
                bad = sp.value_load(m.flag[0:1, 0:1], min_val=0, max_val=1024)
                with sp.If(bad > 0):
                    sp.nop(nofuse=True)
                with sp.Else():
                    def load(b, i, u):
                        sp.wait_ge(blocks_made, b + 1)
                        sp.nop(nofuse=True)
                        sp.dma_start(a_in[:, u, :], d.a[bass.ds(b, 1), :, :].rearrange("b p k -> (b p) k"))\
                          .then_inc(loaded[u], 16)
                    over_blocks(sp, load)

            @block.tensor
            def _(t):
                bad = t.value_load(m.flag[0:1, 0:1], min_val=0, max_val=1024)
                with t.If(bad > 0):
                    general_tensor(t, z, m, general, gsem, "sum")
                with t.Else():
                    t.sem_inc(blocks_made, 3)
                    t.sem_inc(sums_out, 3)

                    def products(b, i, u):
                        t.wait_ge(loaded[u], 16 * i + 16)
                        t.wait_ge(sums_out, b + 1)
                        for k in range(z.NB):
                            mm = t.matmul(bank[u][:, 0:cols], a_in[:, u, k::z.NB], m.parts[:, k, :],
                                          start=(k == 0), stop=(k == z.NB - 1))
                        mm.then_inc(blocks_made, 1)
                    over_blocks(t, products)

            @block.vector
            def _(v):
                bad = v.value_load(m.flag[0:1, 0:1], min_val=0, max_val=1024)
                with v.If(bad > 0):
                    general_vector(v, z, m, general, gsem, "sum")
                with v.Else():
                    def sums(b, i, u):
                        v.wait_ge(blocks_made, b + 4)
                        if layer == 0:
                            v.tensor_copy(m.deg_in[:, bass.ds(b, 1)], bank[u][:, cols - 1:cols])
                        v.tensor_reduce(m.s[:, bass.ds(b, 1), :].rearrange("p b f -> p (b f)"),
                                        bank[u][:, 0:cols - 1].rearrange("p (k f) -> p f k", k=PIECES),
                                        X, ALU.add).then_inc(sums_out, 1)
                    over_blocks(v, sums)
                    v.wait_ge(sums_out, z.NB + 3)
                if layer == 0:
                    c = Steps(v, m.steps)
                    c.did(v.tensor_scalar(m.stat[:, 0, :], m.deg_in[:, :], 1.0, None, ALU.max))
                    c.wait()
                    inverse_root(v, c, m, m.stat[:, 0, :], m.di[:, :], m.stat[:, 1, :], 3)

            @block.scalar
            def _(a):
                bad = a.value_load(m.flag[0:1, 0:1], min_val=0, max_val=1024)
                with a.If(bad > 0):
                    general_scalar(a, z, m, general, gsem, "sum")
                if layer == 0:
                    a.wait_ge(m.square, 3)
                    a.activation(m.di[:, :], m.stat[:, 0, :], ACT.Sqrt).then_inc(m.root, 1)

            @block.gpsimd
            def _(g):
                bad = g.value_load(m.flag[0:1, 0:1], min_val=0, max_val=1024)
                with g.If(bad > 0):
                    general_gpsimd(g, z, m, d, general, gsem, "sum")


CHUNK = 7
HALVES = ((0, 4), (4, 3))


def convolve(nc, z, m, d, sem, layer):
    uv_ready, turned, uvt_ready, made, used, step = (sem(f"{n}{layer}") for n in (
        "uv_ready", "uv_turned", "uvt_ready", "conv_made", "conv_used", "conv_step"))
    assert z.NB % CHUNK == 0 and 2 * z.D == P
    with ExitStack() as ctx:
        sb = lambda n, s: ctx.enter_context(nc.sbuf_tensor(n, s, F32))
        uv = [sb(f"uv{layer}{i}", [P, n, 2, z.D]) for i, (_, n) in enumerate(HALVES)]
        ds_ = [sb(f"di_s{layer}{i}", [P, n, z.D]) for i, (_, n) in enumerate(HALVES)]
        uvt = [sb(f"uvt{layer}{i}", [P, n * P]) for i, (_, n) in enumerate(HALVES)]
        tb = [ctx.enter_context(nc.psum_tensor(f"uv_turn{layer}{i}", [P, BANK], F32)) for i in range(2)]
        ob = [ctx.enter_context(nc.psum_tensor(f"conv_out{layer}{i}", [P, BANK], F32)) for i in range(2)]
        with nc.Block() as block:

            @block.vector
            def _(v):
                steps = 8
                with v.Fori(0, z.NB // CHUNK) as i:
                    own = 0

                    def did(ins):
                        nonlocal own
                        own += 1
                        ins.then_inc(step, 1)
                        v.wait_ge(step, i * steps + own)
                    for h, (b0, n) in enumerate(HALVES):
                        at = bass.ds(CHUNK * i + b0, n)
                        v.wait_ge(turned, 2 * i + (h + 1))
                        did(v.tensor_tensor(ds_[h][:, :, :], m.s[:, at, :], bcast(m.di[:, at], 2, [P, n, z.D]), ALU.mult))
                        did(v.tensor_tensor(uv[h][:, :, 0, :], ds_[h][:, :, :], m.h[:, at, :], ALU.add))
                        did(v.tensor_tensor(uv[h][:, :, 1, :], ds_[h][:, :, :], m.h[:, at, :], ALU.mult))
                        v.sem_inc(uv_ready, 1)
                    for h, (b0, n) in enumerate(HALVES):
                        at = bass.ds(CHUNK * i + b0, n)
                        v.wait_ge(made, 2 * i + (h + 1))
                        out = ob[h][:, 0:n * z.D].rearrange("p (b f) -> p b f", b=n)
                        if layer == 0:
                            did(v.tensor_scalar(m.h[:, at, :], out, 0.0, None, ALU.max))
                        else:
                            did(v.tensor_tensor(m.x[:, at, :], out, m.x[:, at, :], ALU.add))
                        v.sem_inc(used, 1)

            @block.tensor
            def _(t):
                t.sem_inc(turned, 2)
                t.sem_inc(used, 2)
                t.sem_inc(uvt_ready, 2)
                with t.Fori(0, z.NB // CHUNK) as i:
                    for h, (b0, n) in enumerate(HALVES):
                        t.wait_ge(uv_ready, 2 * i + (h + 1))
                        t.wait_ge(uvt_ready, 2 * i + (h + 1))
                        for j in range(n):
                            mm = t.transpose(tb[h][:, j * P:(j + 1) * P], uv[h][:, j, :, :].rearrange("p k f -> p (k f)"),
                                             m.ident[:, :])
                        mm.then_inc(turned, 1)
                    for h, (b0, n) in enumerate(HALVES):
                        t.wait_ge(uvt_ready, 2 * i + (h + 3))
                        t.wait_ge(used, 2 * i + (h + 1))
                        for j in range(n):
                            mm = t.matmul(ob[h][:, j * z.D:(j + 1) * z.D], uvt[h][:, j * P:(j + 1) * P],
                                          m.w12[:, layer, :], start=True, stop=True)
                        mm.then_inc(made, 1)

            @block.scalar
            def _(a):
                with a.Fori(0, z.NB // CHUNK) as i:
                    for h, (b0, n) in enumerate(HALVES):
                        a.wait_ge(turned, 2 * i + (h + 3))
                        a.copy(uvt[h][:, :], tb[h][:, 0:n * P]).then_inc(uvt_ready, 1)


def norm_again(nc, z, m, d, sem):
    landed, turned, patterns = sem("pair_rows_landed"), sem("pairs_turned"), sem("pair_patterns")
    per = BANK // z.PB
    banks = -(-z.PAIR_BLOCKS // per)
    with ExitStack() as ctx:
        sb = lambda n, s: ctx.enter_context(nc.sbuf_tensor(n, s, F32))
        got = sb("pair_got", [z.PB, z.PAIR_BLOCKS, 2, P])
        offset = sb("pair_offset", [P, z.PAIR_BLOCKS * z.PB])
        rest = sb("rest2", [P, z.NB, z.D])
        turn = [[ctx.enter_context(nc.psum_tensor(f"pair_turn{f}{i}", [P, BANK], F32)) for i in range(banks)]
                for f in range(2)]
        with nc.Block() as block:

            @block.gpsimd
            def _(g):
                g.wait_ge(m.pair_rows_out, 32)
                for b in range(z.PAIR_BLOCKS):
                    g.indirect_dma_start(got[:, b, :, :].rearrange("p f e -> p (f e)"), None,
                                         d.pair_rows.rearrange("r f e -> r (f e)"),
                                         bass.IndirectOffsetOnAxis(ap=m.pair_row[:, b:b + 1], axis=0)).then_inc(landed, 16)
                g.iota(offset[:, :], pattern=[[z.PKEYS, z.PAIR_BLOCKS * z.PB]], base=z.PKEYS * z.PB * z.PAIR_BLOCK,
                       channel_multiplier=0, allow_small_or_imprecise_dtypes=True).then_inc(patterns, 1)

            @block.tensor
            def _(t):
                t.wait_ge(landed, 16 * z.PAIR_BLOCKS)
                for f in range(2):
                    for b in range(z.PAIR_BLOCKS):
                        mm = t.transpose(turn[f][b // per][:, b % per * z.PB:(b % per + 1) * z.PB], got[:, b, f, :],
                                         m.ident[0:z.PB, 0:z.PB])
                mm.then_inc(turned, 1)

            @block.vector
            def _(v):
                c = Steps(v, m.steps)
                layernorm_relu(v, c, z, m, m.x[:, :, :], m.h[:, :, :], m.s[:, :, :], m.stat, 4)
                split(v, c, z, m, m.h[:, :, :], rest[:, :, :])
                v.wait_ge(turned, 1)
                v.wait_ge(patterns, 1)
                n = z.PAIR_BLOCKS * z.PB
                c.did(v.memset(m.pair_low[:, n:], 0.0))
                c.did(v.memset(m.pair_key[:, n:], -1.0))
                for i in range(banks):
                    a, w = i * BANK, min(BANK, n - i * BANK)
                    c.did(v.tensor_copy(m.pair_low[:, a:a + w], turn[0][i][:, 0:w]))
                    c.did(v.tensor_tensor(m.pair_key[:, a:a + w], turn[1][i][:, 0:w], offset[:, a:a + w], ALU.subtract))
                c.wait()

            @block.scalar
            def _(a):
                a.wait_ge(m.square, 4)
                a.activation(m.stat[:, 2, :], m.stat[:, 1, :], ACT.Sqrt).then_inc(m.root, 1)


def relation_table(nc, z, m, d, sem):
    staged, turned, ht_ready, block_made, by_scalar, by_vector = (sem(n) for n in (
        "h_staged", "h_turned", "ht_ready", "table_made", "copied_by_scalar", "copied_by_vector"))
    stored = [sem(f"table_stored{i}") for i in range(2)]
    RF = z.R * z.D
    with ExitStack() as ctx:
        sb = lambda n, s: ctx.enter_context(nc.sbuf_tensor(n, s, F32))
        hs = [sb(f"hs{i}", [P, n, z.D]) for i, (_, n) in enumerate(HALVES)]
        ht = [sb(f"ht{i}", [z.D, n * P]) for i, (_, n) in enumerate(HALVES)]
        tab = [sb(f"tab{i}", [P, n, RF]) for i, (_, n) in enumerate(HALVES)]
        tb = [ctx.enter_context(nc.psum_tensor(f"h_turn{i}", [P, BANK], F32)) for i in range(2)]
        bank = [ctx.enter_context(nc.psum_tensor(f"table{i}", [P, BANK], F32)) for i in range(4)]
        with nc.Block() as block:

            @block.tensor
            def _(t):
                for s, n in ((turned, 2), (ht_ready, 2), (by_scalar, 2), (by_vector, 1)):
                    t.sem_inc(s, n)
                with t.Fori(0, z.NB // CHUNK) as i:
                    for h, (b0, n) in enumerate(HALVES):
                        t.wait_ge(staged, 2 * i + (h + 1))
                        t.wait_ge(ht_ready, 2 * i + (h + 1))
                        t.nop(nofuse=True)
                        for j in range(n):
                            mm = t.transpose(tb[h][0:z.D, j * P:(j + 1) * P], hs[h][:, j, :], m.ident[:, :])
                        mm.then_inc(turned, 1)
                    for h, (b0, n) in enumerate(HALVES):
                        t.wait_ge(ht_ready, 2 * i + (h + 3))
                        for j in range(n):
                            at = b0 + j
                            if at % 2 == 0:
                                t.wait_ge(by_scalar, 4 * i + (at // 2 + 1))
                            else:
                                t.wait_ge(by_vector, 3 * i + (at // 2 + 1))
                            t.matmul(bank[at % 4][:, 0:RF], ht[h][:, j * P:(j + 1) * P],
                                     m.w3[:, :, :].rearrange("d r f -> d (r f)"), start=True, stop=True
                                     ).then_inc(block_made, 1)

            @block.scalar
            def _(a):
                with a.Fori(0, z.NB // CHUNK) as i:
                    for h, (b0, n) in enumerate(HALVES):
                        a.wait_ge(turned, 2 * i + (h + 1))
                        a.copy(hs[h][:, :, :], m.h[:, bass.ds(CHUNK * i + b0, n), :]).then_inc(staged, 1)
                    for h, (b0, n) in enumerate(HALVES):
                        a.wait_ge(stored[h], 16 * i + 16)
                        for j in range(n):
                            if (b0 + j) % 2 == 0:
                                a.wait_ge(block_made, CHUNK * i + (b0 + j + 1))
                                a.copy(tab[h][:, j, :], bank[(b0 + j) % 4][:, 0:RF]).then_inc(by_scalar, 1)

            @block.vector
            def _(v):
                with v.Fori(0, z.NB // CHUNK) as i:
                    for h, (b0, n) in enumerate(HALVES):
                        v.wait_ge(turned, 2 * i + (h + 3))
                        v.tensor_copy(ht[h][:, :], tb[h][0:z.D, 0:n * P]).then_inc(ht_ready, 1)
                    for h, (b0, n) in enumerate(HALVES):
                        v.wait_ge(stored[h], 16 * i + 16)
                        for j in range(n):
                            if (b0 + j) % 2 == 1:
                                v.wait_ge(block_made, CHUNK * i + (b0 + j + 1))
                                v.tensor_copy(tab[h][:, j, :], bank[(b0 + j) % 4][:, 0:RF]).then_inc(by_vector, 1)

            @block.sync
            def _(sp):
                sp.sem_inc(stored[0], 16)
                sp.sem_inc(stored[1], 16)
                table = d.t_table.rearrange("(b p) r f -> p b (r f)", p=P)
                with sp.Fori(0, z.NB // CHUNK) as i:
                    for h, (b0, n) in enumerate(HALVES):
                        sp.wait_ge(by_scalar, 4 * i + (2 + 2 * (h + 1)))
                        sp.nop(nofuse=True)
                        sp.wait_ge(by_vector, 3 * i + (1 + 2 + h))
                        sp.nop(nofuse=True)
                        sp.dma_start(table[:, bass.ds(CHUNK * i + b0, n), :], tab[h][:, :, :]).then_inc(stored[h], 16)
                for h in range(2):
                    sp.wait_ge(stored[h], 16 * (z.NB // CHUNK + 1))


GATHERS = 8
SLOTS = 4
BATCH = 4


def relate(nc, z, m, d, sem):
    index_ready, hot_ready, used, added = (sem(f"relate_{n}") for n in ("index", "hot", "used", "added"))
    rows_in = [sem(f"relation_rows_in{k}") for k in range(SLOTS)]
    staged, turned, placed = (sem(f"relate_{n}") for n in ("staged", "turned", "placed"))
    batch_made, pair_made, pair_copied, unit_used, unit_reduced = (sem(f"dense_{n}") for n in (
        "hot_made", "pair_made", "pair_copied", "unit_used", "unit_reduced"))
    units_turned, turned_copied, weighted, dense_placed = (sem(f"dense_{n}") for n in (
        "turned", "turned_copied", "weighted", "placed"))
    span = z.STEP * (GATHERS - 1) + WIN
    PAIRS = UNITS * UNIT_PAIRS
    BATCHES = PAIRS // BATCH
    NEW = UNITS * UNIT
    DCOL = z.STEP * SLOTS * GATHERS * z.ITERS + 2 * P
    parts_cols = PIECES * z.D
    assert SLOTS * GATHERS * z.STEP == P and z.DENSE + P // 2 + span <= DCOL
    assert DCOL + NEW * z.ITERS <= z.SEG * BANK and z.PAIR_BLOCK % CHUNK == 0
    with ExitStack() as ctx:
        sb = lambda n, s, t: ctx.enter_context(nc.sbuf_tensor(n, s, t))
        general = general_buffers(nc, z, ctx, "relation")
        index = sb("relate_index", [P, SLOTS, GATHERS], U32)
        flat = general.hot[:, :, :].rearrange("p a b -> p (a b)")
        hots, gathered = 2 * GATHERS * WIN, SLOTS * GATHERS * z.D
        hot = flat[:, 0:hots].rearrange("p (k j w) -> p k j w", k=2, j=GATHERS)
        rows = flat[:, hots:hots + gathered].rearrange("p (k j f) -> p k j f", k=SLOTS, j=GATHERS)
        sums = general.sums[0:z.D, :]
        low = sb("pair_low_hot", [P, 2, P, BATCH], BF16)
        keys = sb("pair_key_hot", [P, 2, BATCH, z.PKEYS], BF16)
        a_buf = [m.s[:, :, :].rearrange("p b f -> p (b f)").bitcast(BF16),
                 *(sb(f"unit_a{i}", [P, UNIT_PAIRS * z.PKEYS], BF16)[:, :] for i in (1, 2))]
        halves, turned_cols = CHUNK * P, UNITS * P
        stage = [general.place[0:z.D, b0 * P:(b0 + n) * P] for b0, n in HALVES]
        turned_sums = general.place[0:z.D, halves:halves + turned_cols]
        per_relation = general.place[:, halves + turned_cols:halves + turned_cols + UNITS * z.D]\
                              .rearrange("p (u f) -> p u f", u=UNITS)
        bank = [ctx.enter_context(nc.psum_tensor(f"window{i}", [P, BANK], F32)) for i in range(2)]
        pair_bank = [ctx.enter_context(nc.psum_tensor(f"pair_bank{i}", [P, 2, BANK], F32)) for i in range(2)]
        unit_bank, tail_bank = general.turn, general.acc
        tb = bank
        gsem = general_run(m, sem, 3)
        with nc.Block() as block:

            @block.scalar
            def _(a):
                bad = a.value_load(m.flag[0:1, 0:1], min_val=0, max_val=1024)
                with a.If(bad > 0):
                    general_scalar(a, z, m, general, gsem, "relation")
                with a.Else():
                    def next_index(i, k):
                        a.copy(index[:, k, :], m.row_index[:, bass.ds(GATHERS * (SLOTS * i + k), GATHERS)])\
                         .then_inc(index_ready, 1)

                    def copy_pairs(i, first, last):
                        for p in range(first, last):
                            a.wait_ge(pair_made, PAIRS * i + (p + 1))
                            at = p % UNIT_PAIRS * z.PKEYS
                            a.copy(a_buf[p // UNIT_PAIRS % UNITS][:, at:at + z.PKEYS].rearrange("p (c k) -> p c k", c=2),
                                   pair_bank[p % 2][:, :, 0:z.KEYS]).then_inc(pair_copied, 1)

                    def buffer_free(i, u):
                        a.wait_ge(unit_used, UNITS * i + u)

                    def copy_turned(i):
                        a.wait_ge(units_turned, i + 1)
                        a.copy(turned_sums, tail_bank[0:z.D, 0:UNITS * P]).then_inc(turned_copied, 1)

                    def place(i):
                        a.wait_ge(weighted, i + 1)
                        a.copy(sums[:, bass.ds(NEW * i + (DCOL - NEW), NEW)],
                               tail_bank[0:z.D, UNITS * P:UNITS * P + NEW]).then_inc(dense_placed, 1)

                    for k in range(SLOTS):
                        next_index(0, k)
                    copy_pairs(0, 0, UNIT_PAIRS)
                    with a.Fori(0, z.ITERS) as i:
                        buffer_free(i, 1)
                        copy_pairs(i, UNIT_PAIRS, 2 * UNIT_PAIRS)
                        copy_turned(i)
                        a.wait_ge(used, SLOTS * i + 3)
                        next_index(i + 1, 0)
                        buffer_free(i, 2)
                        copy_pairs(i, 2 * UNIT_PAIRS, 2 * UNIT_PAIRS + BATCH)
                        a.wait_ge(used, SLOTS * i + 4)
                        next_index(i + 1, 1)
                        copy_pairs(i, 2 * UNIT_PAIRS + BATCH, 3 * UNIT_PAIRS)
                        place(i)
                        a.wait_ge(used, SLOTS * i + 5)
                        next_index(i + 1, 2)
                        buffer_free(i, 3)
                        copy_pairs(i, 3 * UNIT_PAIRS, 4 * UNIT_PAIRS)
                        a.wait_ge(used, SLOTS * i + 6)
                        next_index(i + 1, 3)
                    copy_turned(z.ITERS)
                    place(z.ITERS)
                    a.wait_ge(added, SLOTS * z.ITERS + 2)
                    a.wait_ge(dense_placed, z.ITERS + 2)
                    a.copy(sums[:, DCOL - P // 2:DCOL], sums[:, z.DENSE - P // 2 + MARGIN:z.DENSE + MARGIN])\
                     .then_inc(dense_placed, 1)
                    a.wait_ge(dense_placed, z.ITERS + 3)
                    for first, last, at in ((0, z.PAIR_BLOCK, MARGIN), (z.PAIR_BLOCK, z.NB, DCOL - z.DENSE)):
                        with a.Fori(first // CHUNK, last // CHUNK) as i:
                            for h, (b0, n) in enumerate(HALVES):
                                a.wait_ge(turned, 2 * i + (h + 1))
                                a.copy(stage[h], sums[:, bass.ds(P * (CHUNK * i + b0) + at, n * P)])\
                                 .then_inc(staged, 1)

            @block.gpsimd
            def _(g):
                bad = g.value_load(m.flag[0:1, 0:1], min_val=0, max_val=1024)
                with g.If(bad > 0):
                    general_gpsimd(g, z, m, d, general, gsem, "relation")
                with g.Else():
                    table = d.t_table.rearrange("n r f -> (n r) f")
                    with g.Fori(0, z.ITERS) as i:
                        for k in range(SLOTS):
                            g.wait_ge(index_ready, SLOTS * i + (k + 1))
                            g.nop(nofuse=True)
                            for j in range(GATHERS):
                                g.indirect_dma_start(rows[:, k, j, :], None, table,
                                                     bass.IndirectOffsetOnAxis(ap=index[:, k, j:j + 1], axis=0)
                                                     ).then_inc(rows_in[k], 16)

            @block.vector
            def _(v):
                bad = v.value_load(m.flag[0:1, 0:1], min_val=0, max_val=1024)
                with v.If(bad > 0):
                    general_vector(v, z, m, general, gsem, "relation")
                with v.Else():
                    def pair_hots(i, n):
                        at = PAIRS * i + (z.PB // 2 + BATCH * n)
                        v.tensor_tensor(low[:, n % 2, :, :], m.iota_low[:, :, 0:BATCH],
                                        bcast(m.pair_low[:, bass.ds(at, BATCH)], 1, [P, P, BATCH]), ALU.is_equal)
                        for j in range(BATCH):
                            ins = v.tensor_scalar(keys[:, n % 2, j, :], m.iota_keys[:, :],
                                                  m.pair_key[:, bass.ds(at + j, 1)], None, ALU.is_equal)
                        ins.then_inc(batch_made, 1)

                    def batch(i, n):
                        v.wait_ge(pair_made, PAIRS * i + BATCH * (n - 1))
                        pair_hots(i, n)

                    def window_hots(i, k):
                        v.wait_ge(used, SLOTS * i + (k + 1))
                        v.tensor_tensor(hot[:, k % 2, :, :], bcast(m.iota_row[:, 0:WIN], 1, [P, GATHERS, WIN]),
                                        bcast(m.in_window[:, bass.ds(GATHERS * (SLOTS * i + k), GATHERS)], 2,
                                              [P, GATHERS, WIN]), ALU.is_equal).then_inc(hot_ready, 1)

                    def add_window(i, k):
                        v.wait_ge(used, SLOTS * i + (k + 3))
                        v.wait_ge(added, SLOTS * i + (k + 2))
                        at = sums[:, bass.ds(z.STEP * GATHERS * (SLOTS * i + k), span)]
                        v.tensor_tensor(at, bank[k % 2][0:z.D, 0:span], at, ALU.add).then_inc(added, 1)

                    def reduce_unit(i, u):
                        v.wait_ge(unit_used, UNITS * i + (u + 3))
                        if u == 0:
                            v.wait_ge(units_turned, i + 1)
                        v.tensor_reduce(per_relation[:, u, :],
                                        unit_bank[:, 0:parts_cols].rearrange("p (k f) -> p f k", k=PIECES),
                                        X, ALU.add).then_inc(unit_reduced, 1)

                    v.memset(sums[:, 0:DCOL - P // 2], 0.0).then_inc(added, 2)
                    v.memset(per_relation[:, :, :], 0.0).then_inc(unit_reduced, 1)
                    pair_hots(0, 0)
                    pair_hots(0, 1)
                    batch(0, 2)
                    batch(0, 3)
                    with v.Fori(0, z.ITERS) as i:
                        window_hots(i, 0)
                        window_hots(i, 1)
                        batch(i, 4)
                        batch(i, 5)
                        reduce_unit(i, 0)
                        add_window(i, 0)
                        window_hots(i, 2)
                        batch(i, 6)
                        add_window(i, 1)
                        window_hots(i, 3)
                        batch(i, 7)
                        reduce_unit(i, 1)
                        add_window(i, 2)
                        batch(i, 8)
                        batch(i, 9)
                        reduce_unit(i, 2)
                        add_window(i, 3)
                    with v.Fori(0, z.NB // CHUNK) as i:
                        for h, (b0, n) in enumerate(HALVES):
                            v.wait_ge(turned, 2 * i + (h + 3))
                            v.tensor_copy(m.s[:, bass.ds(CHUNK * i + b0, n), :],
                                          tb[h][:, 0:n * z.D].rearrange("p (b f) -> p b f", b=n)).then_inc(placed, 1)

            @block.tensor
            def _(t):
                bad = t.value_load(m.flag[0:1, 0:1], min_val=0, max_val=1024)
                with t.If(bad > 0):
                    general_tensor(t, z, m, general, gsem, "relation")
                with t.Else():
                    def build_pair(i, p):
                        if p % BATCH == 0:
                            t.wait_ge(batch_made, BATCHES * i + (p // BATCH + 1))
                        t.wait_ge(pair_copied, PAIRS * i + (p + 1))
                        for c in range(2):
                            mm = t.matmul(pair_bank[p % 2][:, c, 0:z.KEYS], low[:, p // BATCH % 2, :, p % BATCH],
                                          keys[:, p // BATCH % 2, p % BATCH, c * z.KEYS:(c + 1) * z.KEYS],
                                          start=True, stop=True)
                        mm.then_inc(pair_made, 1)

                    def build_under_use(i, u, first, last):
                        if first == 0:
                            t.wait_ge(unit_reduced, UNITS * i + (u + 1))
                        each = -(-z.NB // UNIT_PAIRS)
                        for q in range(first, last):
                            build_pair(i, (u + 1) * UNIT_PAIRS + q)
                            if q == 0:
                                t.wait_ge(pair_copied, PAIRS * i + ((u + 1) * UNIT_PAIRS + 2))
                            for k in range(q * each, min((q + 1) * each, z.NB)):
                                mm = t.matmul(unit_bank[:, 0:parts_cols], a_buf[u][:, k::z.NB],
                                              m.parts[:, k, 0:parts_cols], start=(k == 0), stop=(k == z.NB - 1))
                        if last == UNIT_PAIRS:
                            mm.then_inc(unit_used, 1)

                    def sum_group(i, k):
                        t.wait_ge(added, SLOTS * i + (k + 1))
                        t.nop(nofuse=True)
                        t.matmul(bank[k % 2][0:z.D, 0:span], m.zeros[0:1, 0:z.D], m.zeros[0:1, 0:span],
                                 start=True, stop=False)
                        t.wait_ge(hot_ready, SLOTS * i + (k + 1))
                        t.wait_ge(rows_in[k], 16 * GATHERS * i + 16 * GATHERS)
                        t.nop(nofuse=True)
                        for j in range(GATHERS):
                            mm = t.matmul(bank[k % 2][0:z.D, z.STEP * j:z.STEP * j + WIN], rows[:, k, j, :],
                                          hot[:, k % 2, j, :], start=False, stop=(j == GATHERS - 1))
                        mm.then_inc(used, 1)

                    def turn_units(i):
                        t.wait_ge(unit_reduced, UNITS * i + 1)
                        t.nop(nofuse=True)
                        t.wait_ge(dense_placed, i + 1)
                        t.nop(nofuse=True)
                        for u in range(UNITS):
                            mm = t.transpose(tail_bank[0:z.D, u * P:(u + 1) * P], per_relation[:, u, :], m.ident[:, :])
                        mm.then_inc(units_turned, 1)

                    def weigh(i):
                        t.wait_ge(turned_copied, i + 1)
                        t.nop(nofuse=True)
                        for r in range(z.R):
                            mm = t.matmul(tail_bank[0:z.D, UNITS * P:UNITS * P + NEW], m.w3[:, r, :],
                                          turned_sums[:, r::z.R], start=(r == 0), stop=(r == z.R - 1))
                        mm.then_inc(weighted, 1)

                    t.sem_inc(used, 2)
                    t.sem_inc(pair_copied, 2)
                    t.sem_inc(unit_used, 2)
                    t.sem_inc(dense_placed, 1)
                    for p in range(UNIT_PAIRS):
                        build_pair(0, p)
                    with t.Fori(0, z.ITERS) as i:
                        build_under_use(i, 0, 0, UNIT_PAIRS)
                        turn_units(i)
                        sum_group(i, 0)
                        build_under_use(i, 1, 0, BATCH)
                        sum_group(i, 1)
                        build_under_use(i, 1, BATCH, UNIT_PAIRS)
                        weigh(i)
                        sum_group(i, 2)
                        build_under_use(i, 2, 0, UNIT_PAIRS)
                        sum_group(i, 3)
                    turn_units(z.ITERS)
                    weigh(z.ITERS)
                    t.wait_ge(added, SLOTS * z.ITERS + 2)
                    t.sem_inc(turned, 2)
                    t.sem_inc(placed, 2)
                    with t.Fori(0, z.NB // CHUNK) as i:
                        for h, (b0, n) in enumerate(HALVES):
                            t.wait_ge(staged, 2 * i + (h + 1))
                            t.wait_ge(placed, 2 * i + (h + 1))
                            t.nop(nofuse=True)
                            for j in range(n):
                                mm = t.transpose(tb[h][:, j * z.D:(j + 1) * z.D], stage[h][:, j * P:(j + 1) * P],
                                                 m.ident[0:z.D, 0:z.D])
                            mm.then_inc(turned, 1)


def finish(nc, z, m, d, sem):
    ready, out_sem = sem("out_ready"), sem("out_stored")
    full = [P, z.NB, z.D]
    rem = z.N - (z.NB - 1) * P
    with nc.Block() as block:

        @block.vector
        def _(v):
            c = Steps(v, m.steps)
            some, factor_h, factor_m = (m.stat[:, i, :] for i in range(3))
            c.did(v.tensor_scalar(some, m.deg_in[:, :], 0.0, None, ALU.is_gt))
            c.did(v.tensor_scalar(factor_m, m.deg_in[:, :], 1.0, None, ALU.max))
            c.wait()
            c.did(v.tensor_scalar(factor_h, some, 0.2 - 1.0, 1.0, ALU.mult, ALU.add))
            c.did(v.reciprocal(factor_m, factor_m))
            c.wait()
            c.did(v.tensor_scalar(factor_m, factor_m, 1.0 - 0.2, None, ALU.mult))
            c.did(v.tensor_tensor(m.h[:, :, :], m.h[:, :, :], bcast(factor_h, 2, full), ALU.mult))
            c.wait()
            c.did(v.tensor_tensor(m.s[:, :, :], m.s[:, :, :], bcast(factor_m, 2, full), ALU.mult))
            c.wait()
            c.did(v.tensor_tensor(m.s[:, :, :], m.s[:, :, :], m.h[:, :, :], ALU.add))
            c.wait()
            c.did(v.scalar_tensor_tensor(out=m.s[:, :, :], in0=m.s[:, :, :], scalar=0.0, in1=m.x[:, :, :],
                                         op0=ALU.max, op1=ALU.add))
            c.wait()
            v.sem_inc(ready, 1)

        @block.sync
        def _(sp):
            sp.wait_ge(ready, 1)
            sp.dma_start(d.out[0:(z.NB - 1) * P, :].rearrange("(b p) f -> p b f", p=P),
                         m.s[:, 0:z.NB - 1, :]).then_inc(out_sem, 16)
            sp.dma_start(d.out[(z.NB - 1) * P:z.N, :], m.s[0:rem, z.NB - 1, :]).then_inc(out_sem, 16)
            sp.wait_ge(out_sem, 32)


def program(nc, x, src, dst, etype, w1_1, w2_1, w1_2, w2_2, w3, out, stop=None):
    z = sizes(x.shape[0], src.shape[0], x.shape[1], w3.shape[0])
    dram = lambda n, s, t: nc.dram_tensor(n, s, t, kind="Internal").ap()
    d = Named()
    d.x = x
    d.src = src
    d.dst = dst
    d.etype = etype
    d.w1_1 = w1_1
    d.w2_1 = w2_1
    d.w1_2 = w1_2
    d.w2_2 = w2_2
    d.w3 = w3
    d.out = out
    d.scr = dram("edge_fields", (3, z.SCR), F32)
    d.rows = dram("edge_rows", (z.TROWS, 2, P), F32)
    d.pair_rows = dram("pair_rows", (z.PROWS, 2, P), F32)
    d.a = dram("adjacency", (z.NB, P, z.GB * z.KEYS), BF16)
    d.g_table = dram("g_rows", (z.NP, z.D), F32)
    d.t_table = dram("relation_rows", (z.NP, z.R, z.D), F32)
    with ExitStack() as ctx:
        sb = lambda n, s, t: ctx.enter_context(nc.sbuf_tensor(n, s, t))
        sem = lambda n: ctx.enter_context(nc.semaphore(n))
        nodes = [P, z.NB, z.D]
        m = Named()
        m.steps = Count(sem("vector_step"))
        m.general = general_semaphores(sem)
        m.pair_rows_out = sem("pair_rows_written")
        m.square, m.root = sem("square_ready"), sem("root_ready")
        m.x = sb("x", nodes, F32)
        m.h = sb("h", nodes, F32)
        m.s = sb("s", nodes, F32)
        m.low = sb("low", [P, z.NB * z.CT], BF16)
        m.key = sb("key", [P, z.NB * z.CT], F32)
        m.row_index = sb("row_index", [P, z.TILES], U32)
        m.src_index = sb("src_index", [P, z.TILES], U32)
        m.in_window = sb("in_window", [P, z.TILES], F32)
        m.tile_base = sb("tile_base", [P, z.TILES], F32)
        m.deg_out = sb("deg_out", [P, z.NB], F32)
        m.deg_in = sb("deg_in", [P, z.NB], F32)
        m.do = sb("do", [P, z.NB], F32)
        m.di = sb("di", [P, z.NB], F32)
        m.stat = sb("stat", [P, 4, z.NB], F32)
        m.w12 = sb("w12", [P, 2, z.D], F32)
        m.w3 = sb("w3", [z.D, z.R, z.D], F32)
        m.iota_row = sb("iota_row", [P, BANK], F32)
        m.iota_part = sb("iota_part", [P, 1], F32)
        m.iota_keys = sb("iota_keys", [P, z.PKEYS], F16)
        m.pair_row = sb("pair_row", [z.PB, z.PAIR_BLOCKS], U32)
        m.iota_low = sb("iota_low", [P, P, 12], BF16)
        m.ident = sb("ident", [P, P], F32)
        m.ident16 = sb("ident16", [P, P], BF16)
        m.before = sb("before", [P, P], F32)
        m.zeros = sb("zeros", [P, BANK], F32)
        m.ones = sb("ones", [P, 1], F32)
        m.ones16 = sb("ones16", [P, 1, 2], BF16)
        m.flag = sb("flag", [1, 1], I32)

        def later():
            m.parts = sb("parts", [P, z.NB, PIECES * z.D + 1], BF16)
            m.pair_low = sb("pair_low", [P, z.PAIR_BLOCKS * z.PB + 2 * UNIT_PAIRS], BF16)
            m.pair_key = sb("pair_keys", [P, z.PAIR_BLOCKS * z.PB + 2 * UNIT_PAIRS], F32)

        stages = [
            lambda: constants(nc, z, m, sem),
            lambda: prepare(nc, z, m, d, sem),
            later,
            lambda: build(nc, z, m, d, sem),
            lambda: parts(nc, z, m, d, sem, 0),
            lambda: aggregate(nc, z, m, d, sem, 0),
            lambda: convolve(nc, z, m, d, sem, 0),
            lambda: parts(nc, z, m, d, sem, 1),
            lambda: aggregate(nc, z, m, d, sem, 1),
            lambda: convolve(nc, z, m, d, sem, 1),
            lambda: norm_again(nc, z, m, d, sem),
            lambda: relation_table(nc, z, m, d, sem),
            lambda: relate(nc, z, m, d, sem),
            lambda: finish(nc, z, m, d, sem),
        ]
        for stage in stages[:stop]:
            stage()
        return m


_INS = ["x", "src", "dst", "edge_type_8", "L0_gnn_W1_1", "L0_gnn_W2_1", "L0_gnn_W1_2", "L0_gnn_W2_2",
        "L1_gnn_weight_r"]


def kernel(**inputs):
    import numpy as np
    import concourse.bacc as bacc
    from concourse.bass_utils import run_bass_kernel_spmd

    nc = bacc.Bacc("TRN2", target_bir_lowering=False, num_devices=1)
    arrays, args = {}, []
    for name in _INS:
        a = np.ascontiguousarray(inputs[name])
        arrays[f"in_{name}"] = a
        args.append(nc.dram_tensor(f"in_{name}", a.shape, mybir.dt.from_np(a.dtype), kind="ExternalInput").ap())
    args.append(nc.dram_tensor("out", inputs["x"].shape, F32, kind="ExternalOutput").ap())
    program(nc, *args)
    return run_bass_kernel_spmd(nc, [arrays], core_ids=[0]).results[0]["out"]
```

```python
from contextlib import ExitStack

import concourse.bass as bass
from concourse import mybir

P = 128
F32 = mybir.dt.float32
BF16 = mybir.dt.bfloat16
F16 = mybir.dt.float16
I32 = mybir.dt.int32
U32 = mybir.dt.uint32
ALU = mybir.AluOpType
ACT = mybir.ActivationFunctionType
X = mybir.AxisListType.X
EPS = 1e-5
BANK = 512

GROUP = 8
ROW = 32
GROUP_TILES = 3
SPANS = ((0, 6), (0, 8), (5, 8))
PIECES = 3
FAR = 1e7
WIN = 128
MARGIN = 62
PAIR_ROW = 16
UNIT = 16
UNITS = 3
UNIT_PAIRS = UNIT // 2


class Named:
    pass


def sizes(N, E, D, R):
    z = Named()
    z.N = N
    z.E = E
    z.D = D
    z.R = R
    z.NB = -(-N // P)
    z.NP = z.NB * P
    z.DEG = z.NP // z.NB and E // N
    z.TILES = -(-E // (P * ROW)) * ROW
    z.EP = z.TILES * P
    z.QT = 14
    z.Q = z.TILES // z.QT
    z.QE = z.QT * P
    z.ROWS = z.EP // ROW
    z.TROWS = -(-(z.ROWS + 4 * GROUP_TILES) // 16) * 16
    z.SCR = ROW * (z.TROWS - 1) + P
    z.GB = P // GROUP
    z.CT = z.GB * GROUP_TILES
    z.KEYS = GROUP * z.NB
    z.STEP = 4
    z.SEG = -(-N // BANK)
    z.ITERS = (z.NP + P // 2) // (P + UNITS * UNIT)
    z.DENSE = z.ITERS * P - P // 2
    z.PAIR_BLOCK = z.DENSE // P
    z.PAIR_BLOCKS = z.NB - z.PAIR_BLOCK
    z.PB = P // 2
    z.PKEYS = 2 * R * z.NB
    z.PHEADS = z.QE // PAIR_ROW
    z.PBASE = (z.DENSE - (WIN - 1 - MARGIN)) // z.STEP * P // PAIR_ROW
    z.PROWS = z.EP // PAIR_ROW - z.PBASE
    z.FLAG_GROUPS = -(-N // GROUP)
    assert z.Q * z.QT == z.TILES and z.TILES * z.STEP == z.NP and z.KEYS <= BANK
    assert z.Q <= P and z.NB <= P and E > (z.Q - 1) * z.QE
    assert z.DENSE + z.ITERS * UNITS * UNIT == z.NP and z.DENSE % P == P // 2 and z.PKEYS == 2 * z.KEYS
    return z


class Count:

    def __init__(self, sem):
        self.sem, self.n = sem, 0


class Steps:

    def __init__(self, eng, count):
        self.eng, self.count = eng, count

    def did(self, instruction):
        self.count.n += 1
        instruction.then_inc(self.count.sem, 1)

    def wait(self):
        self.eng.wait_ge(self.count.sem, self.count.n)


def bcast(ap, axis, shape):
    return ap.unsqueeze(axis).broadcast_to(shape)


def layernorm_start(v, c, z, m, src, dst, work, stat, times):
    full = [P, z.NB, z.D]
    mean, var, rstd, t = (stat[:, i, :] for i in range(4))
    c.wait()
    c.did(v.tensor_reduce(mean, src, X, ALU.add))
    c.wait()
    c.did(v.tensor_scalar(mean, mean, 1.0 / z.D, None, ALU.mult))
    c.wait()
    c.did(v.tensor_tensor(dst, src, bcast(mean, 2, full), ALU.subtract))
    c.wait()
    c.did(v.tensor_tensor(work, dst, dst, ALU.mult))
    c.wait()
    c.did(v.tensor_reduce(var, work, X, ALU.add))
    c.wait()
    c.did(v.tensor_scalar(var, var, 1.0 / z.D, EPS, ALU.mult, ALU.add))
    c.wait()
    v.sem_inc(m.square, 1)


def layernorm_end(v, c, z, m, dst, stat, times):
    full = [P, z.NB, z.D]
    mean, var, rstd, t = (stat[:, i, :] for i in range(4))
    inverse_root(v, c, m, var, rstd, t, times)
    c.did(v.tensor_tensor(dst, dst, bcast(rstd, 2, full), ALU.mult))
    c.wait()
    c.did(v.tensor_scalar(dst, dst, 0.0, None, ALU.max))
    c.wait()


def inverse_root(v, c, m, y, r, t, times):
    v.wait_ge(m.root, times)
    c.did(v.reciprocal(r, r))
    c.wait()
    c.did(v.tensor_tensor(t, r, r, ALU.mult))
    c.wait()
    c.did(v.tensor_tensor(t, t, y, ALU.mult))
    c.wait()
    c.did(v.tensor_scalar(t, t, -0.5, 1.5, ALU.mult, ALU.add))
    c.wait()
    c.did(v.tensor_tensor(r, r, t, ALU.mult))
    c.wait()


def patterns_for_all(g, z, m, made):
    small = dict(allow_small_or_imprecise_dtypes=True)
    g.iota(m.iota_row[:, :], pattern=[[1, BANK]], base=0, channel_multiplier=0, **small)
    g.iota(m.iota_part[:, :], pattern=[[0, 1]], base=0, channel_multiplier=1, **small)
    g.iota(m.iota_keys[:, :], pattern=[[1, z.PKEYS]], base=0, channel_multiplier=0, **small)
    g.iota(m.iota_low[:, :, :], pattern=[[1, P], [0, 12]], base=0, channel_multiplier=0, **small).then_inc(made, 1)


def constants_for_all(v, c, m, made):
    c.did(v.memset(m.zeros[:, :], 0.0))
    c.did(v.memset(m.ones[:, :], 1.0))
    v.wait_ge(made, 1)
    c.did(v.tensor_scalar(m.ident[:, :], m.iota_row[:, 0:P], m.iota_part[:, 0:1], None, ALU.is_equal))
    c.did(v.tensor_scalar(m.ident16[:, :], m.iota_row[:, 0:P], m.iota_part[:, 0:1], None, ALU.is_equal))
    c.did(v.tensor_scalar(m.before[:, :], m.iota_row[:, 0:P], m.iota_part[:, 0:1], None, ALU.is_gt))
    c.wait()


def prepare(nc, z, m, d, sem):
    padded, src_in, dst_in, et_in, next_in = (sem(n) for n in (
        "padded", "src_in", "dst_in", "type_in", "next_in"))
    x_in, w_in, patterns = (sem(n) for n in ("x_in", "weights_in", "patterns"))
    fields, scr_out, rows_out, counted = (sem(n) for n in (
        "fields_ready", "scratch_written", "rows_written", "heads_hot"))
    c_made, c_copied, ct_made, ct_copied, pre_made = (sem(n) for n in (
        "counts_made", "counts_copied", "turned_counts", "turned_copied", "prefix_made"))
    made = sem("constants_made")
    starts, turned, bank_free = sem("starts_ready"), sem("turned"), sem("turn_bank_free")
    landed = [sem(f"group_rows_landed{i}") for i in range(4)]
    slots_free = sem("row_slots_free")
    bad_ready, bad_made, pad_ready = sem("bad_ready"), sem("bad_summed"), sem("pad_ready")
    pair_key_ready, pair_scr_out = sem("pair_key_ready"), sem("pair_key_written")
    pair_hot, pair_counted, pair_copied, pair_total, total_copied, pair_prefix = (sem(f"pairs_{n}") for n in (
        "hot", "counted", "copied", "total", "total_copied", "prefix"))
    rem = z.E - (z.Q - 1) * z.QE
    flat_groups = [(f, t, min(4, z.QT - t)) for f in range(3) for t in range(0, z.QT, 4)]
    turns = [("rows", k) for k in range(5)] + [("flat", n) for n in range(len(flat_groups))]
    turns += [("rows", k) for k in range(5, z.CT // 4)]
    TURNS_AT_NORM = len(flat_groups) + 7

    with ExitStack() as ctx:
        sb = lambda n, s, t: ctx.enter_context(nc.sbuf_tensor(n, s, t))
        ps = lambda n, s: ctx.enter_context(nc.psum_tensor(n, s, F32))
        edge = [z.Q, z.QE]
        src_i, dst_i, et_i = sb("src_i", edge, I32), sb("dst_i", edge, I32), sb("type_i", edge, I32)
        high_i, low_i = sb("src_high", edge, I32), sb("src_low", edge, I32)
        low, key = sb("low_f", edge, F32), sb("key_f", edge, F32)
        dst, src, idx = sb("dst_f", edge, F32), sb("src_f", edge, F32), sb("row_f", edge, F32)
        centre = sb("centre", edge, F32)
        pair_key = low_i[:, :].bitcast(F32)
        pair_hi, pair_mid = (m.row_index[0:z.Q, i * z.PHEADS:(i + 1) * z.PHEADS].bitcast(I32) for i in range(2))
        H2 = z.PHEADS // 2
        as_hot = lambda b, n: b[0:z.Q, 0:n // 2].bitcast(BF16)
        hot_block = as_hot(m.h[:, :, :].rearrange("p b f -> p (b f)"), z.PHEADS * z.NB).rearrange("p (h n) -> p h n", n=z.NB)
        hot_pair = [as_hot(b, H2 * z.PB).rearrange("p (h n) -> p h n", n=z.PB)
                    for b in (m.s[:, :, :].rearrange("p b f -> p (b f)"), m.key[:, :])]
        pcnt, ptot = sb("pair_cnt", [z.PB, z.NB], F32), sb("pair_total", [z.NB, z.PB], F32)
        pstart, ones = sb("pair_start", [z.PB, z.PAIR_BLOCKS], F32), sb("prep_ones", [z.PB, z.PB], F32)
        pair_no, pover = sb("pair_no", [z.PB, z.PAIR_BLOCKS], F32), sb("pair_over", [z.PB, z.PAIR_BLOCKS], F32)
        next_i, next_f = sb("next_i", [z.Q, 1], I32), sb("next_f", [z.Q, 1], F32)
        bad = sb("bad", [P, 8], F32)
        bad1 = sb("bad1", [P, 1], F32)
        heads = z.QE // ROW
        head_hi, head_mid = sb("head_hi", [z.Q, heads], I32), sb("head_mid", [z.Q, heads], I32)
        hot_hi = sb("hot_hi", [z.Q, heads, z.NB], BF16)
        hot_mid = sb("hot_mid", [z.Q, heads, z.GB], BF16)
        cnt, cnt_t = sb("cnt", [z.NB, z.GB], F32), sb("cnt_t", [z.GB, z.NB], F32)
        total, total_b = sb("total", [z.NB, 1], F32), sb("total_b", [z.NB, z.GB], F32)
        start = sb("start", [z.NB, z.GB], F32)
        over = sb("over", [z.NB, z.GB], F32)
        group_no = sb("group_no", [z.NB, z.GB], F32)
        row_no = sb("row_no", [z.NB, z.GB, GROUP_TILES], U32)
        got = sb("got", [z.NB, 16, 2, P], F32)
        offset = sb("offset", [P, z.NB, z.GB, GROUP_TILES], F32)
        pad = sb("pad", [16, 3, (z.SCR - z.EP) // 16], F32)
        turn = [ps(f"turn{i}", [P, BANK]) for i in range(4)]
        p_cnt, p_misc = ps("p_cnt", [P, BANK]), ps("p_misc", [P, BANK])

        with nc.Block() as block:

            @block.sync
            def _(sp):
                sp.wait_ge(padded, 1)
                for ap, t, s in ((d.src, src_i, src_in), (d.dst, dst_i, dst_in), (d.etype, et_i, et_in)):
                    body = ap[0:(z.Q - 1) * z.QE].rearrange("(q e) -> q e", e=z.QE)
                    tail = ap[(z.Q - 1) * z.QE:z.E].rearrange("(q e) -> q e", q=1)
                    sp.dma_start(t[0:z.Q - 1, :], body).then_inc(s, 16)
                    sp.dma_start(t[z.Q - 1:z.Q, 0:rem], tail).then_inc(s, 16)
                sp.dma_start(next_i[0:z.Q - 1, :], bass.AP(d.dst.tensor, z.QE, [[z.QE, z.Q - 1], [1, 1]]),
                             allow_slow_non_contiguous=True).then_inc(next_in, 16)
                sp.wait_ge(fields, 1)
                sp.wait_ge(pad_ready, 1)
                for f, t in enumerate((low, key)):
                    sp.dma_start(d.scr[f, 0:z.EP].rearrange("(q e) -> q e", e=z.QE), t[:, :]).then_inc(scr_out, 16)
                    sp.dma_start(d.scr[f, z.EP:z.SCR].rearrange("(q e) -> q e", q=16), pad[:, f, :]).then_inc(scr_out, 16)
                sp.wait_ge(scr_out, 64)
                for f in range(2):
                    rows = bass.AP(d.scr.tensor, f * z.SCR, [[ROW, z.TROWS], [1, P]])
                    sp.dma_start(d.rows[:, f, :], rows).then_inc(rows_out, 16)
                sp.wait_ge(pair_key_ready, 1)
                sp.dma_start(d.scr[2, 0:z.EP].rearrange("(q e) -> q e", e=z.QE), pair_key).then_inc(pair_scr_out, 16)
                sp.dma_start(d.scr[2, z.EP:z.SCR].rearrange("(q e) -> q e", q=16), pad[:, 2, :]).then_inc(pair_scr_out, 16)
                sp.wait_ge(pair_scr_out, 32)
                for i, f in enumerate((0, 2)):
                    rows = bass.AP(d.scr.tensor, f * z.SCR + z.PBASE * PAIR_ROW, [[PAIR_ROW, z.PROWS], [1, P]])
                    sp.dma_start(d.pair_rows[:, i, :], rows).then_inc(m.pair_rows_out, 16)
                sp.wait_ge(rows_out, 32)

            @block.scalar
            def _(a):
                a.dma_start(m.x[:, 0:z.NB - 1, :], d.x[0:(z.NB - 1) * P, :].rearrange("(b p) f -> p b f", p=P))\
                 .then_inc(x_in, 16)
                a.wait_ge(padded, 2)
                a.dma_start(m.x[0:z.N - (z.NB - 1) * P, z.NB - 1, :], d.x[(z.NB - 1) * P:z.N, :]).then_inc(x_in, 16)
                for i, w in enumerate((d.w1_1, d.w2_1, d.w1_2, d.w2_2)):
                    a.dma_start(m.w12[z.D * (i % 2):z.D * (i % 2) + z.D, i // 2, :], w).then_inc(w_in, 16)
                a.dma_start(m.w3[:, :, :], d.w3.rearrange("r d f -> d r f")).then_inc(w_in, 16)
                a.wait_ge(m.square, 1)
                a.activation(m.stat[:, 2, :], m.stat[:, 1, :], ACT.Sqrt).then_inc(m.root, 1)
                a.wait_ge(w_in, 80)

            @block.gpsimd
            def _(g):
                patterns_for_all(g, z, m, made)
                small = dict(allow_small_or_imprecise_dtypes=True)
                g.iota(centre[:, :], pattern=[[z.STEP, z.QT], [0, P]], base=0,
                       channel_multiplier=z.STEP * z.QT, **small)
                g.iota(pair_no[:, :], pattern=[[z.PB, z.PAIR_BLOCKS]], base=z.PB * z.PAIR_BLOCK, channel_multiplier=1, **small)
                g.iota(group_no[:, :], pattern=[[1, z.GB]], base=0, channel_multiplier=z.GB, **small)
                g.iota(m.tile_base[:, :], pattern=[[z.STEP, z.TILES]], base=-MARGIN, channel_multiplier=0, **small)
                g.iota(offset[:, :, :, :], pattern=[[z.KEYS * z.GB, z.NB], [z.KEYS, z.GB], [0, GROUP_TILES]],
                       base=0, channel_multiplier=0, **small).then_inc(patterns, 1)
                g.wait_ge(starts, 1)
                g.wait_ge(rows_out, 32)
                for ct in range(z.CT):
                    k = ct // 4
                    if ct % 4 == 0 and k >= 4:
                        g.wait_ge(slots_free, k - 3)
                    c_, t_ = divmod(ct, GROUP_TILES)
                    g.indirect_dma_start(
                        got[:, ct % 16, :, :].rearrange("p f e -> p (f e)"), None,
                        d.rows.rearrange("r f e -> r (f e)"),
                        bass.IndirectOffsetOnAxis(ap=row_no[:, c_, t_:t_ + 1], axis=0),
                    ).then_inc(landed[k % 4], 16)

            @block.tensor
            def _(t):
                def turn_some(first, last):
                    for n in range(first, last):
                        what, k = turns[n]
                        if what == "rows":
                            t.wait_ge(landed[k % 4], 64 * (k // 4 + 1))
                        if n >= 4:
                            t.wait_ge(bank_free, n - 3)
                        if what == "flat":
                            f, t0, cntt = flat_groups[k]
                            list_ = (idx, dst, src)[f]
                            for j in range(cntt):
                                mm = t.transpose(turn[n % 4][:, j * z.Q:(j + 1) * z.Q],
                                                 list_[:, (t0 + j) * P:(t0 + j + 1) * P], m.ident[0:z.Q, 0:z.Q])
                        else:
                            for f in range(2):
                                for j in range(4):
                                    at = (f * 4 + j) * z.NB
                                    mm = t.transpose(turn[n % 4][:, at:at + z.NB], got[:, (k % 4) * 4 + j, f, :],
                                                     m.ident[0:z.NB, 0:z.NB])
                        mm.then_inc(turned, 1)

                t.wait_ge(counted, 1)
                for h in range(heads):
                    mm = t.matmul(p_cnt[0:z.NB, 0:z.GB], hot_hi[:, h, :], hot_mid[:, h, :],
                                  start=(h == 0), stop=(h == heads - 1))
                mm.then_inc(c_made, 1)
                t.wait_ge(c_copied, 1)
                t.transpose(p_misc[0:z.GB, 0:z.NB], cnt[:, :], m.ident[0:z.NB, 0:z.NB]).then_inc(ct_made, 1)
                t.wait_ge(ct_copied, 1)
                t.matmul(p_cnt[0:z.NB, 64:64 + z.GB], cnt_t[:, :], m.before[0:z.GB, 0:z.GB], start=True, stop=False)
                t.matmul(p_cnt[0:z.NB, 64:64 + z.GB], m.before[0:z.NB, 0:z.NB], total_b[:, :],
                         start=False, stop=True).then_inc(pre_made, 1)
                t.wait_ge(pair_hot, 1)
                for h in range(z.PHEADS):
                    mm = t.matmul(p_cnt[0:z.PB, 128:128 + z.NB], hot_pair[h // H2][:, h % H2, :], hot_block[:, h, :],
                                  start=(h == 0), stop=(h == z.PHEADS - 1))
                mm.then_inc(pair_counted, 1)
                t.wait_ge(pair_copied, 1)
                t.matmul(p_misc[0:z.NB, 128:128 + z.PB], pcnt[:, :], ones[:, :], start=True, stop=True).then_inc(pair_total, 1)
                t.wait_ge(total_copied, 1)
                t.matmul(p_cnt[0:z.PB, 256:256 + z.NB], m.before[0:z.PB, 0:z.PB], pcnt[:, :], start=True, stop=False)
                t.matmul(p_cnt[0:z.PB, 256:256 + z.NB], ptot[:, :], m.before[0:z.NB, 0:z.NB],
                         start=False, stop=True).then_inc(pair_prefix, 1)
                turn_some(0, len(turns))
                t.wait_ge(bad_ready, 1)
                t.matmul(p_misc[0:1, 256:257], bad1[:, :], m.ones[:, 0:1], start=True, stop=True).then_inc(bad_made, 1)

            @block.vector
            def _(v):
                c = Steps(v, m.steps)
                off = offset[:, :, :, :].rearrange("p b c t -> p b (c t)")
                half = 4 * z.NB

                def place_some(first, last):
                    for n in range(first, last):
                        what, k = turns[n]
                        v.wait_ge(turned, n + 1)
                        if what == "flat":
                            f, t0, cntt = flat_groups[k]
                            from_ = turn[n % 4][:, 0:cntt * z.Q].rearrange("p (j q) -> p q j", j=cntt)
                            at = lambda b: b[:, :].rearrange("p (q t) -> p q t", t=z.QT)[:, :, t0:t0 + cntt]
                            if f == 1:
                                c.did(v.tensor_tensor(at(m.in_window), from_, at(m.tile_base), ALU.subtract))
                            else:
                                c.did(v.tensor_copy(at((m.row_index, None, m.src_index)[f]), from_))
                        else:
                            view = lambda b: b[:, 0:z.NB * z.CT].rearrange("p (b c) -> p b c", c=z.CT)[:, :, 4 * k:4 * k + 4]
                            bank = turn[n % 4]
                            c.did(v.tensor_copy(view(m.low), bank[:, 0:half].rearrange("p (j b) -> p b j", j=4)))
                            c.did(v.tensor_tensor(view(m.key), bank[:, half:2 * half].rearrange("p (j b) -> p b j", j=4),
                                                  off[:, :, 4 * k:4 * k + 4], ALU.subtract))
                        c.wait()
                        if what == "rows":
                            v.sem_inc(slots_free, 1)
                        v.sem_inc(bank_free, 1)

                c.did(v.memset(src_i[:, rem:], z.NP - 1))
                c.did(v.memset(dst_i[:, rem:], z.NP - 1))
                c.did(v.memset(et_i[:, rem:], 0))
                c.did(v.memset(next_i[:, :], z.NP - 1))
                c.wait()
                v.sem_inc(padded, 1)
                c.did(v.memset(m.x[:, z.NB - 1, :], 0.0))
                c.wait()
                v.sem_inc(padded, 1)
                c.did(v.memset(m.key[:, z.NB * z.CT:], -1.0))
                c.did(v.memset(pad[:, 0, :], 0.0))
                c.did(v.memset(pad[:, 1:3, :], -1.0))
                c.did(v.memset(ones[:, :], 1.0))
                c.did(v.memset(bad[:, :], 0.0))
                c.wait()
                v.sem_inc(pad_ready, 1)
                constants_for_all(v, c, m, made)
                v.wait_ge(src_in, 32)
                c.did(v.tensor_scalar(high_i[:, :], src_i[:, :], 7, None, ALU.logical_shift_right))
                c.did(v.tensor_scalar(low_i[:, :], src_i[:, :], 127, None, ALU.bitwise_and))
                v.wait_ge(dst_in, 32)
                c.did(v.tensor_scalar(head_hi[:, :], dst_i[:, 0:z.QE:ROW], 7, None, ALU.logical_shift_right))
                c.did(v.tensor_scalar(head_mid[:, :], dst_i[:, 0:z.QE:ROW], 3, z.GB - 1,
                                      ALU.logical_shift_right, ALU.bitwise_and))
                c.wait()
                c.did(v.tensor_copy(low[:, :], low_i[:, :]))
                c.did(v.scalar_tensor_tensor(out=key[:, :], in0=dst_i[:, :], scalar=float(z.NB), in1=high_i[:, :],
                                             op0=ALU.mult, op1=ALU.add))
                c.wait()
                v.sem_inc(fields, 1)
                c.did(v.tensor_tensor(hot_hi[:, :, :], bcast(m.iota_row[0:z.Q, 0:z.NB], 1, [z.Q, heads, z.NB]),
                                      bcast(head_hi[:, :], 2, [z.Q, heads, z.NB]), ALU.is_equal))
                c.did(v.tensor_tensor(hot_mid[:, :, :], bcast(m.iota_row[0:z.Q, 0:z.GB], 1, [z.Q, heads, z.GB]),
                                      bcast(head_mid[:, :], 2, [z.Q, heads, z.GB]), ALU.is_equal))
                c.wait()
                v.sem_inc(counted, 1)
                c.did(v.tensor_copy(dst[:, :], dst_i[:, :]))
                c.did(v.tensor_copy(src[:, :], src_i[:, :]))
                v.wait_ge(et_in, 32)
                c.did(v.scalar_tensor_tensor(out=idx[:, :], in0=src_i[:, :], scalar=float(z.R), in1=et_i[:, :],
                                             op0=ALU.mult, op1=ALU.add))
                c.did(v.scalar_tensor_tensor(out=pair_key, in0=dst_i[:, :], scalar=float(z.R), in1=et_i[:, :],
                                             op0=ALU.mult, op1=ALU.add))
                v.wait_ge(c_made, 1)
                c.did(v.tensor_copy(cnt[:, :], p_cnt[0:z.NB, 0:z.GB]))
                c.wait()
                v.sem_inc(c_copied, 1)
                c.did(v.tensor_reduce(total[:, :], cnt[:, :], X, ALU.add))
                c.wait()
                c.did(v.tensor_copy(total_b[:, :], total[:, 0:1].broadcast_to([z.NB, z.GB])))
                v.wait_ge(ct_made, 1)
                c.did(v.tensor_copy(cnt_t[:, :], p_misc[0:z.GB, 0:z.NB]))
                c.wait()
                v.sem_inc(ct_copied, 1)
                v.wait_ge(pre_made, 1)
                c.did(v.tensor_scalar(start[:, :], p_cnt[0:z.NB, 64:64 + z.GB], -1.0, 0.0, ALU.add, ALU.max))
                c.wait()
                for t_ in range(GROUP_TILES):
                    c.did(v.tensor_scalar(row_no[:, :, t_], start[:, :], float(4 * t_), None, ALU.add))
                c.wait()
                v.sem_inc(starts, 1)
                c.did(v.scalar_tensor_tensor(out=pair_key, in0=pair_key, scalar=float(z.NB), in1=high_i[:, :],
                                             op0=ALU.mult, op1=ALU.add))
                c.did(v.tensor_scalar(pair_hi, dst_i[:, 0:z.QE:PAIR_ROW], 7, None, ALU.logical_shift_right))
                c.did(v.tensor_scalar(pair_mid, dst_i[:, 0:z.QE:PAIR_ROW], 1, z.PB - 1,
                                      ALU.logical_shift_right, ALU.bitwise_and))
                c.wait()
                v.sem_inc(pair_key_ready, 1)
                shape = [z.Q, z.PHEADS, z.NB]
                c.did(v.tensor_tensor(hot_block, bcast(m.iota_row[0:z.Q, 0:z.NB], 1, shape),
                                      bcast(pair_hi, 2, shape), ALU.is_equal))
                shape = [z.Q, H2, z.PB]
                for i in range(2):
                    c.did(v.tensor_tensor(hot_pair[i], bcast(m.iota_row[0:z.Q, 0:z.PB], 1, shape),
                                          bcast(pair_mid[:, i * H2:(i + 1) * H2], 2, shape), ALU.is_equal))
                c.wait()
                v.sem_inc(pair_hot, 1)
                v.wait_ge(pair_counted, 1)
                c.did(v.tensor_copy(pcnt[:, :], p_cnt[0:z.PB, 128:128 + z.NB]))
                c.wait()
                v.sem_inc(pair_copied, 1)
                v.wait_ge(pair_total, 1)
                c.did(v.tensor_copy(ptot[:, :], p_misc[0:z.NB, 128:128 + z.PB]))
                c.wait()
                v.sem_inc(total_copied, 1)
                v.wait_ge(pair_prefix, 1)
                c.did(v.tensor_scalar(pstart[:, :], p_cnt[0:z.PB, 256 + z.PAIR_BLOCK:256 + z.NB], -1.0 - z.PBASE, 0.0,
                                      ALU.add, ALU.max))
                c.wait()
                c.did(v.tensor_copy(m.pair_row[:, :], pstart[:, :]))
                v.wait_ge(patterns, 1)
                place_some(0, 2)
                v.wait_ge(next_in, 16)
                c.did(v.tensor_tensor(et_i[:, 0:z.QE - 1], dst[:, 0:z.QE - 1], dst[:, 1:z.QE], ALU.is_gt))
                c.did(v.tensor_tensor(bad[0:z.Q, 1:2], dst[:, z.QE - 1:z.QE], next_i[:, :], ALU.is_gt))
                c.did(v.tensor_tensor(centre[:, :], dst[:, :], centre[:, :], ALU.subtract))
                c.did(v.tensor_scalar(over[:, :], cnt[:, :], float(4 * GROUP_TILES - 1), None, ALU.is_gt))
                c.did(v.tensor_scalar(pover[:, :], pcnt[:, z.PAIR_BLOCK:z.NB], float(P // PAIR_ROW - 1), None, ALU.is_gt))
                c.did(v.tensor_scalar(pair_no[:, :], pair_no[:, :], float(-(-z.N // 2)), None, ALU.is_lt))
                c.did(v.tensor_scalar(group_no[:, :], group_no[:, :], float(z.FLAG_GROUPS), None, ALU.is_lt))
                c.wait()
                c.did(v.tensor_reduce(bad[0:z.Q, 0:1], et_i[:, 0:z.QE - 1], X, ALU.max))
                c.did(v.tensor_reduce(bad[0:z.Q, 6:7], centre[:, :], X, ALU.max))
                c.did(v.tensor_reduce(bad[0:z.Q, 7:8], centre[:, :], X, ALU.min))
                c.did(v.tensor_tensor(over[:, :], over[:, :], group_no[:, :], ALU.mult))
                c.did(v.tensor_tensor(pover[:, :], pover[:, :], pair_no[:, :], ALU.mult))
                c.wait()
                c.did(v.tensor_scalar(bad[0:z.Q, 2:3], bad[0:z.Q, 6:7], float(WIN - 1 - MARGIN), None, ALU.is_gt))
                c.did(v.tensor_scalar(bad[0:z.Q, 3:4], bad[0:z.Q, 7:8], float(-MARGIN), None, ALU.is_lt))
                c.did(v.tensor_reduce(bad[0:z.NB, 4:5], over[:, :], X, ALU.max))
                c.did(v.tensor_reduce(bad[0:z.PB, 5:6], pover[:, :], X, ALU.max))
                c.wait()
                place_some(2, TURNS_AT_NORM)
                v.wait_ge(x_in, 32)
                layernorm_start(v, c, z, m, m.x[:, :, :], m.h[:, :, :], m.s[:, :, :], m.stat, 1)
                place_some(TURNS_AT_NORM, TURNS_AT_NORM + 3)
                layernorm_end(v, c, z, m, m.h[:, :, :], m.stat, 1)
                place_some(TURNS_AT_NORM + 3, len(turns))
                groups = m.key[:, 0:GROUP_TILES * z.FLAG_GROUPS].rearrange("p (g t) -> p g t", t=GROUP_TILES)
                flat = m.s[:, :, :].rearrange("p b f -> p (b f)")
                own, later_ = flat[:, 0:z.FLAG_GROUPS], flat[:, z.FLAG_GROUPS:2 * z.FLAG_GROUPS]
                c.did(v.scalar_tensor_tensor(out=own, in0=groups[:, :, 0], scalar=float(z.KEYS), in1=groups[:, :, 0],
                                             op0=ALU.is_lt, op1=ALU.mult))
                c.did(v.tensor_scalar(later_, groups[:, :, 2], 0.0, FAR, ALU.is_lt, ALU.mult))
                c.wait()
                c.did(v.tensor_tensor(later_, later_, groups[:, :, 2], ALU.add))
                c.did(v.tensor_reduce(bad[:, 6:7], own, X, ALU.max))
                c.wait()
                c.did(v.tensor_reduce(bad[:, 7:8], later_, X, ALU.min))
                c.did(v.tensor_scalar(bad[:, 6:7], bad[:, 6:7], float(SPANS[0][1] * z.NB), None, ALU.is_ge))
                c.wait()
                c.did(v.tensor_scalar(bad[:, 7:8], bad[:, 7:8], float(SPANS[2][0] * z.NB), None, ALU.is_lt))
                c.wait()
                c.did(v.tensor_reduce(bad1[:, :], bad[:, :], X, ALU.add))
                c.wait()
                v.sem_inc(bad_ready, 1)
                v.wait_ge(bad_made, 1)
                c.did(v.tensor_copy(m.flag[:, :], p_misc[0:1, 256:257]))
                c.wait()


def build(nc, z, m, d, sem):
    low_hot, key_hot, group_made, pair_copied = (sem(n) for n in (
        "low_hot", "key_hot", "group_made", "pair_copied"))
    distance_made, scalar_hot = sem("key_distance_made"), sem("scalar_key_hot")
    stored = [sem(f"half_stored{i}") for i in range(2)]
    deg_made, step = sem("degrees_made"), sem("build_step")
    pairs = z.GB // 2
    half = z.GB * z.KEYS // 2
    with ExitStack() as ctx:
        sb = lambda n, s, t: ctx.enter_context(nc.sbuf_tensor(n, s, t))
        low = sb("low_hot_buf", [P, 2, P, 12], BF16)
        keys = sb("key_hot_buf", [P, 2, 12, z.KEYS], BF16)
        a_buf = sb("a_buf", [P, pairs, 2, z.KEYS], BF16)
        last = 3 * GROUP_TILES + 1
        scalar_tiles = ((GROUP_TILES + 1, last), (last,), (last,), (last,))
        distance = sb("key_distance", [P, 2, z.KEYS], BF16)
        bank = [ctx.enter_context(nc.psum_tensor(f"pair{i}", [P, 2, BANK], F32)) for i in range(2)]
        degree = ctx.enter_context(nc.psum_tensor("degree", [P, BANK], F32))
        reach = lambda j: tuple(z.NB * dst for dst in SPANS[j % GROUP_TILES])
        general = general_buffers(nc, z, ctx, "deg")
        gsem = general_run(m, sem, 0)

        with nc.Block() as block:

            @block.vector
            def _(v):
                bad = v.value_load(m.flag[0:1, 0:1], min_val=0, max_val=1024)
                with v.If(bad > 0):
                    general_vector(v, z, m, general, gsem, "degree")
                with v.Else():
                    with v.Fori(0, z.NB) as b:
                        for k in range(4):
                            v.wait_ge(group_made, z.GB * b + 4 * (k + 1))
                            v.tensor_tensor(low[:, k % 2, :, :], m.iota_low[:, :, :],
                                            bcast(m.low[:, bass.ds(z.CT * b + 12 * k, 12)], 1, [P, P, 12]),
                                            ALU.is_equal).then_inc(low_hot, 1)
                            for j in range(12):
                                if j in scalar_tiles[k % 4]:
                                    continue
                                lo, hi = reach(j)
                                ins = v.tensor_scalar(keys[:, k % 2, j, lo:hi], m.iota_keys[:, lo:hi],
                                                      m.key[:, bass.ds(z.CT * b + 12 * k + j, 1)], None, ALU.is_equal)
                                if j % GROUP_TILES == GROUP_TILES - 1:
                                    ins.then_inc(key_hot, 1)
                    v.wait_ge(deg_made, 1)
                    v.tensor_reduce(m.deg_out[:, :], degree[:, 0:z.KEYS].rearrange("p (g s) -> p s g", g=GROUP),
                                    X, ALU.add).then_inc(step, 1)
                    v.wait_ge(step, 1)

            @block.tensor
            def _(t):
                bad = t.value_load(m.flag[0:1, 0:1], min_val=0, max_val=1024)
                with t.If(bad > 0):
                    general_tensor(t, z, m, general, gsem, "degree")
                with t.Else():
                    t.sem_inc(group_made, 8)
                    t.sem_inc(pair_copied, 2)
                    t.sem_inc(scalar_hot, 1)
                    t.matmul(degree[:, 0:z.KEYS], m.zeros[0:1, 0:P], m.zeros[0:1, 0:z.KEYS], start=True, stop=False)

                    def degrees_of(q):
                        for c in range(2):
                            mm = t.matmul(degree[:, 0:z.KEYS], m.ident16[:, :], a_buf[:, q, c, :],
                                          start=False, stop=False)
                        return mm

                    with t.Fori(0, z.NB) as b:
                        for q in range(pairs):
                            t.wait_ge(pair_copied, pairs * b + (q + 1))
                            for c in range(2):
                                g = 2 * q + c
                                if g % 4 == 0:
                                    t.wait_ge(low_hot, 4 * b + (g // 4 + 1))
                                t.wait_ge(key_hot, z.GB * b + (g + 1))
                                if g * GROUP_TILES % 12 + 1 == scalar_tiles[g // 4][0]:
                                    t.wait_ge(scalar_hot, 4 * b + (g // 4 + 2))
                                for j in (1, 0, 2):
                                    at = g * GROUP_TILES + j
                                    lo, hi = reach(j)
                                    mm = t.matmul(bank[q % 2][:, c, lo:hi], low[:, at // 12 % 2, :, at % 12],
                                                  keys[:, at // 12 % 2, at % 12, lo:hi], start=(j == 1), stop=(j == 2))
                                mm.then_inc(group_made, 1)
                            if q >= 1:
                                t.wait_ge(pair_copied, pairs * b + (q + 2))
                                degrees_of(q - 1)
                        t.wait_ge(pair_copied, pairs * b + (pairs + 2))
                        degrees_of(pairs - 1)
                    t.matmul(degree[:, 0:z.KEYS], m.zeros[0:1, 0:P], m.zeros[0:1, 0:z.KEYS],
                             start=False, stop=True).then_inc(deg_made, 1)

            @block.scalar
            def _(a):
                bad = a.value_load(m.flag[0:1, 0:1], min_val=0, max_val=1024)
                with a.If(bad > 0):
                    general_scalar(a, z, m, general, gsem, "degree")
                with a.Else():
                    def keys_of(b, k):
                        a.wait_ge(scalar_hot, 4 * b + (k + 1))
                        tiles = scalar_tiles[k % 4]
                        for i, j in enumerate(tiles):
                            ins = a.activation(distance[:, i, :], m.iota_keys[:, 0:z.KEYS], ACT.Abs,
                                               bias=m.key[:, bass.ds(z.CT * b + 12 * k + j, 1)], scale=-1.0)
                        ins.then_inc(distance_made, 1)
                        a.wait_ge(group_made, z.GB * b + 4 * (k + 1))
                        a.wait_ge(distance_made, 4 * b + (k + 1))
                        a.activation(keys[:, k % 2, tiles[0]::2 * GROUP_TILES, :], distance[:, 0:len(tiles), :],
                                     ACT.Relu, bias=m.ones[:, 0:1], scale=-1.0).then_inc(scalar_hot, 1)

                    keys_of(0, 0)
                    with a.Fori(0, z.NB) as b:
                        for q in range(pairs):
                            if q % 2 == 0:
                                keys_of(b, q // 2 + 1)
                            if q % (pairs // 2) == 0:
                                a.wait_ge(stored[q // (pairs // 2)], 16 * b + 16)
                            a.wait_ge(group_made, z.GB * b + (8 + 2 * (q + 1)))
                            a.copy(a_buf[:, q, :, :], bank[q % 2][:, :, 0:z.KEYS]).then_inc(pair_copied, 1)

            @block.gpsimd
            def _(g):
                bad = g.value_load(m.flag[0:1, 0:1], min_val=0, max_val=1024)
                with g.If(bad > 0):
                    general_gpsimd(g, z, m, d, general, gsem, "degree")

            @block.sync
            def _(sp):
                bad = sp.value_load(m.flag[0:1, 0:1], min_val=0, max_val=1024)
                with sp.If(bad > 0):
                    sp.nop(nofuse=True)
                with sp.Else():
                    sp.sem_inc(stored[0], 16)
                    sp.sem_inc(stored[1], 16)
                    flat = a_buf[:, :, :, :].rearrange("p q c k -> p (q c k)")
                    with sp.Fori(0, z.NB) as b:
                        for h in range(2):
                            sp.wait_ge(pair_copied, pairs * b + (2 + pairs // 2 * (h + 1)))
                            sp.nop(nofuse=True)
                            sp.dma_start(d.a[bass.ds(b, 1), :, h * half:(h + 1) * half].rearrange("b p k -> (b p) k"),
                                         flat[:, h * half:(h + 1) * half]).then_inc(stored[h], 16)
                    for h in range(2):
                        sp.wait_ge(stored[h], 16 * (z.NB + 1))


def general_semaphores(sem):
    it = Named()
    it.hot = sem("general_hot")
    it.index = sem("general_index")
    it.used = sem("general_used")
    it.summed = sem("general_summed")
    it.moved = sem("general_moved")
    it.staged = sem("general_staged")
    it.turned = sem("general_turned")
    it.placed = sem("general_placed")
    it.own = Count(sem("general_own"))
    return it


def general_run(m, sem, run):
    it = Named()
    it.run = run
    it.rows = [sem(f"general_rows{run}{j}") for j in range(8 if run > 0 else 0)]
    g = m.general
    it.hot, it.index, it.used, it.summed, it.moved = g.hot, g.index, g.used, g.summed, g.moved
    it.staged, it.turned, it.placed, it.own = g.staged, g.turned, g.placed, g.own
    return it


def general_buffers(nc, z, ctx, tag):
    sb = lambda n, s, t: ctx.enter_context(nc.sbuf_tensor(f"{n}_{tag}", s, t))
    it = Named()
    it.rows = sb("general_rows", [P, 8, z.D + 1], F32)
    it.hot = sb("general_hot", [P, 8, BANK], F32)
    it.index = sb("general_index", [P, 8], U32)
    it.place = sb("general_place", [P, z.TILES], F32)
    it.sums = sb("general_sums", [z.D + 1, z.SEG * BANK], F32)
    it.stage = sb("general_stage", [z.D + 1, P], F32)
    it.acc = ctx.enter_context(nc.psum_tensor(f"general_acc_{tag}", [P, BANK], F32))
    it.turn = ctx.enter_context(nc.psum_tensor(f"general_turn_{tag}", [P, BANK], F32))
    return it



def general_width(z, kind):
    return {"degree": 1, "sum": z.D + 1, "relation": z.D}[kind]


def general_vector(v, z, m, w, s, kind):
    groups = z.TILES // 8
    p0, b0 = s.run * z.SEG, s.run * z.NB
    c = Steps(v, s.own)
    c.did(v.memset(w.rows[:, :, z.D:z.D + 1], 1.0))
    if kind == "degree":
        c.did(v.tensor_copy(w.place[:, :], m.src_index[:, :]))
    else:
        c.did(v.tensor_tensor(w.place[:, :], m.in_window[:, :], m.tile_base[:, :], ALU.add))
    c.wait()
    v.sem_inc(s.moved, 1)
    before = s.own.n
    with v.Fori(0, z.SEG) as p:
        with v.Fori(0, groups) as i:
            v.wait_ge(s.used, p * groups + i + (p0 * groups + 1))
            for j in range(8):
                ins = v.tensor_scalar(w.hot[:, j, :], m.iota_row[:, :], w.place[:, bass.ds(8 * i + j, 1)], None,
                                      ALU.is_equal)
            ins.then_inc(s.hot, 1)
        v.wait_ge(s.summed, p + (p0 + 1))
        v.tensor_copy(w.sums[0:general_width(z, kind), bass.ds(BANK * p, BANK)],
                      w.acc[0:general_width(z, kind), :]).then_inc(s.own.sem, 1)
        v.tensor_scalar(w.place[:, :], w.place[:, :], -float(BANK), None, ALU.add).then_inc(s.own.sem, 1)
        v.wait_ge(s.own.sem, 2 * p + (before + 2))
        v.sem_inc(s.moved, 1)
    s.own.n += 2 * z.SEG
    with v.Fori(0, z.NB) as b:
        v.wait_ge(s.turned, b + (b0 + 1))
        if kind == "degree":
            v.tensor_copy(m.deg_out[:, bass.ds(b, 1)], w.turn[:, 0:1]).then_inc(s.placed, 1)
        else:
            if kind == "sum":
                v.tensor_copy(m.deg_in[:, bass.ds(b, 1)], w.turn[:, z.D:z.D + 1])
            v.tensor_copy(m.s[:, bass.ds(b, 1), :].rearrange("p b f -> p (b f)"), w.turn[:, 0:z.D]).then_inc(s.placed, 1)
    v.wait_ge(s.placed, b0 + z.NB + 1)


def general_tensor(t, z, m, w, s, kind):
    groups = z.TILES // 8
    p0, b0 = s.run * z.SEG, s.run * z.NB
    R = general_width(z, kind)
    if s.run == 0:
        t.sem_inc(s.used, 1)
        t.sem_inc(s.placed, 1)
    with t.Fori(0, z.SEG) as p:
        t.wait_ge(s.moved, p + (p0 + s.run + 1))
        t.nop(nofuse=True)
        t.matmul(w.acc[0:R, :], m.zeros[0:1, 0:R], m.zeros[0:1, :], start=True, stop=False)
        with t.Fori(0, groups) as i:
            t.wait_ge(s.hot, p * groups + i + (p0 * groups + 1))
            t.nop(nofuse=True)
            if kind != "degree":
                for j in range(8):
                    t.wait_ge(s.rows[j], (p * groups + i) * 16 + 16)
                    t.nop(nofuse=True)
            for j in range(8):
                rows = m.ones[:, 0:1] if kind == "degree" else w.rows[:, j, 0:R]
                mm = t.matmul(w.acc[0:R, :], rows, w.hot[:, j, :], start=False, stop=False)
            mm.then_inc(s.used, 1)
        t.matmul(w.acc[0:R, :], m.zeros[0:1, 0:R], m.zeros[0:1, :], start=False, stop=True).then_inc(s.summed, 1)
    with t.Fori(0, z.NB) as b:
        t.wait_ge(s.placed, b + (b0 + 1))
        t.wait_ge(s.staged, b + (b0 + 1))
        t.nop(nofuse=True)
        t.transpose(w.turn[:, 0:R], w.stage[0:R, :], m.ident[0:R, 0:R]).then_inc(s.turned, 1)


def general_scalar(a, z, m, w, s, kind):
    groups = z.TILES // 8
    p0, b0 = s.run * z.SEG, s.run * z.NB
    R = general_width(z, kind)
    if kind != "degree":
        index = m.src_index if kind == "sum" else m.row_index
        with a.Fori(0, z.SEG) as p:
            with a.Fori(0, groups) as i:
                a.wait_ge(s.used, p * groups + i + (p0 * groups + 1))
                a.copy(w.index[:, :], index[:, bass.ds(8 * i, 8)]).then_inc(s.index, 1)
    a.wait_ge(s.moved, (s.run + 1) * (z.SEG + 1))
    with a.Fori(0, z.NB) as b:
        a.wait_ge(s.placed, b + (b0 + 1))
        a.copy(w.stage[0:R, :], w.sums[0:R, bass.ds(P * b, P)]).then_inc(s.staged, 1)


def general_gpsimd(g, z, m, d, w, s, kind):
    if kind == "degree":
        g.nop(nofuse=True)
        return
    groups = z.TILES // 8
    i0 = (s.run - 1) * z.SEG * groups
    table = d.g_table if kind == "sum" else d.t_table.rearrange("n r f -> (n r) f")
    with g.Fori(0, z.SEG) as p:
        with g.Fori(0, groups) as i:
            g.wait_ge(s.index, p * groups + i + (i0 + 1))
            g.nop(nofuse=True)
            for j in range(8):
                g.indirect_dma_start(w.rows[:, j, 0:z.D], None, table,
                                     bass.IndirectOffsetOnAxis(ap=w.index[:, j:j + 1], axis=0)).then_inc(s.rows[j], 16)


CHUNK = 7
HALVES = ((0, 4), (4, 3))


def part(m, z, k, at):
    return m.parts[:, at, k * z.D:(k + 1) * z.D]


def parts_order(z):
    chunks = z.NB // CHUNK
    return [(k, t - k) for t in range(chunks + PIECES - 1) for k in range(PIECES) if 0 <= t - k < chunks]


def aggregate(nc, z, m, d, sem, layer):
    blocks_made, sums_out, remainders, parts_made, g_out = (sem(f"{n}{layer}") for n in (
        "block_made", "sums_out", "remainders_made", "parts_made", "g_stored"))
    loaded = [sem(f"a_block_loaded{layer}{i}") for i in range(3)]
    cols = PIECES * z.D + 1
    order = parts_order(z)
    with ExitStack() as ctx:
        a_in = ctx.enter_context(nc.sbuf_tensor(f"a_in{layer}", [P, 3, z.GB * z.KEYS], BF16))
        bank = [ctx.enter_context(nc.psum_tensor(f"sums{layer}{i}", [P, BANK], F32)) for i in range(3)]
        general = general_buffers(nc, z, ctx, f"sum{layer}")
        gsem = general_run(m, sem, 1 + layer)
        rest = general.hot[:, :, :].rearrange("p a b -> p (a b)")[:, 0:z.NB * z.D].rearrange("p (b f) -> p b f", f=z.D)
        whole = (z.NB - 1) // 3
        assert z.NB == 3 * whole + 1

        def over_blocks(eng, one):
            one(0, 0, 0)
            with eng.Fori(0, whole) as i:
                for u in range(1, 4):
                    one(3 * i + u, i + u // 3, u % 3)

        with nc.Block() as block:

            @block.sync
            def _(sp):
                bad = sp.value_load(m.flag[0:1, 0:1], min_val=0, max_val=1024)
                with sp.If(bad > 0):
                    sp.wait_ge(remainders, order.index((0, z.NB // CHUNK - 1)) + 1)
                    sp.dma_start(d.g_table.rearrange("(b p) f -> p b f", p=P), m.s[:, :, :]).then_inc(g_out, 16)
                    sp.wait_ge(g_out, 16)
                with sp.Else():
                    def load(b, n, u):
                        sp.wait_ge(blocks_made, b + 1)
                        sp.nop(nofuse=True)
                        sp.dma_start(a_in[:, u, :], d.a[bass.ds(b, 1), :, :].rearrange("b p k -> (b p) k"))\
                          .then_inc(loaded[u], 16)
                    sp.sem_inc(blocks_made, 3)
                    over_blocks(sp, load)

            @block.tensor
            def _(t):
                bad = t.value_load(m.flag[0:1, 0:1], min_val=0, max_val=1024)
                with t.If(bad > 0):
                    general_tensor(t, z, m, general, gsem, "sum")
                with t.Else():
                    t.sem_inc(sums_out, 3)

                    def products(b, n, u, first=False):
                        t.wait_ge(loaded[u], 16 * n + 16)
                        t.wait_ge(sums_out, b + 1)
                        for k in range(z.NB):
                            if first and k % CHUNK == 0:
                                t.wait_ge(parts_made, order.index((PIECES - 1, k // CHUNK)) + 1)
                            mm = t.matmul(bank[u][:, 0:cols], a_in[:, u, k::z.NB], m.parts[:, k, :],
                                          start=(k == 0), stop=(k == z.NB - 1))
                        mm.then_inc(blocks_made, 1)
                    over_blocks(t, lambda b, n, u: products(b, n, u, first=isinstance(b, int)))

            @block.vector
            def _(v):
                c = Steps(v, m.steps)
                if layer == 0:
                    c.did(v.tensor_scalar(m.stat[:, 0, :], m.deg_out[:, :], 1.0, None, ALU.max))
                    c.did(v.memset(m.parts[:, :, PIECES * z.D:], 1.0))
                    c.wait()
                    v.sem_inc(m.square, 1)
                    inverse_root(v, c, m, m.stat[:, 0, :], m.do[:, :], m.stat[:, 1, :], 2)
                for k, i in order:
                    at = slice(CHUNK * i, CHUNK * (i + 1))
                    if k == 0:
                        ins = v.tensor_tensor(m.s[:, at, :], m.h[:, at, :], bcast(m.do[:, at], 2, [P, CHUNK, z.D]), ALU.mult)
                    else:
                        v.wait_ge(parts_made, order.index((k - 1, i)) + 1)
                        ins = v.tensor_tensor(rest[:, at, :], (m.s if k == 1 else rest)[:, at, :],
                                              part(m, z, k - 1, at), ALU.subtract)
                    ins.then_inc(remainders, 1)
                bad = v.value_load(m.flag[0:1, 0:1], min_val=0, max_val=1024)
                with v.If(bad > 0):
                    v.wait_ge(parts_made, len(order))
                    v.wait_ge(g_out, 16)
                    general_vector(v, z, m, general, gsem, "sum")
                with v.Else():
                    def sums(b, n, u):
                        v.wait_ge(blocks_made, b + 4)
                        if layer == 0:
                            v.tensor_copy(m.deg_in[:, bass.ds(b, 1)], bank[u][:, cols - 1:cols])
                        v.tensor_reduce(m.s[:, bass.ds(b, 1), :].rearrange("p b f -> p (b f)"),
                                        bank[u][:, 0:cols - 1].rearrange("p (k f) -> p f k", k=PIECES),
                                        X, ALU.add).then_inc(sums_out, 1)
                    over_blocks(v, sums)
                    v.wait_ge(sums_out, z.NB + 3)
                if layer == 0:
                    c.did(v.tensor_scalar(m.stat[:, 0, :], m.deg_in[:, :], 1.0, None, ALU.max))
                    c.wait()
                    v.sem_inc(m.square, 1)
                    inverse_root(v, c, m, m.stat[:, 0, :], m.di[:, :], m.stat[:, 1, :], 3)

            @block.scalar
            def _(a):
                if layer == 0:
                    a.wait_ge(m.square, 2)
                    a.activation(m.do[:, :], m.stat[:, 0, :], ACT.Sqrt).then_inc(m.root, 1)
                for n, (k, i) in enumerate(order):
                    at = slice(CHUNK * i, CHUNK * (i + 1))
                    a.wait_ge(remainders, n + 1)
                    a.copy(part(m, z, k, at), (rest if k > 0 else m.s)[:, at, :]).then_inc(parts_made, 1)
                bad = a.value_load(m.flag[0:1, 0:1], min_val=0, max_val=1024)
                with a.If(bad > 0):
                    general_scalar(a, z, m, general, gsem, "sum")
                if layer == 0:
                    a.wait_ge(m.square, 3)
                    a.activation(m.di[:, :], m.stat[:, 0, :], ACT.Sqrt).then_inc(m.root, 1)

            @block.gpsimd
            def _(g):
                bad = g.value_load(m.flag[0:1, 0:1], min_val=0, max_val=1024)
                with g.If(bad > 0):
                    g.wait_ge(g_out, 16)
                    g.nop(nofuse=True)
                    general_gpsimd(g, z, m, d, general, gsem, "sum")


def convolve(nc, z, m, d, sem, layer):
    uv_ready, turned, uvt_ready, made, used = (sem(f"{n}{layer}") for n in (
        "uv_ready", "uv_turned", "uvt_ready", "conv_made", "conv_used"))
    normed = sem("conv_normed") if layer == 1 else None
    assert z.NB % CHUNK == 0 and 2 * z.D == P
    chunks = z.NB // CHUNK
    full = [P, z.NB, z.D]
    with ExitStack() as ctx:
        sb = lambda n, s: ctx.enter_context(nc.sbuf_tensor(n, s, F32))
        uv = [sb(f"uv{layer}{i}", [P, n, 2, z.D]) for i, (_, n) in enumerate(HALVES)]
        uvt = [sb(f"uvt{layer}{i}", [P, n * P]) for i, (_, n) in enumerate(HALVES)]
        tb = [ctx.enter_context(nc.psum_tensor(f"uv_turn{layer}{i}", [P, BANK], F32)) for i in range(2)]
        ob = [ctx.enter_context(nc.psum_tensor(f"conv_out{layer}{i}", [P, BANK], F32)) for i in range(2)]
        layout = PairLayout(nc, z, m, d, sem, ctx) if layer == 1 else None
        with nc.Block() as block:

            @block.vector
            def _(v):
                def products(i, h):
                    b0, n = HALVES[h]
                    at = bass.ds(CHUNK * i + b0, n)
                    v.tensor_tensor(uv[h][:, :, 0, :], m.s[:, at, :], m.h[:, at, :], ALU.add)
                    v.tensor_tensor(uv[h][:, :, 1, :], m.s[:, at, :], m.h[:, at, :], ALU.mult).then_inc(uv_ready, 1)

                def results(i, h):
                    b0, n = HALVES[h]
                    at = bass.ds(CHUNK * i + b0, n)
                    v.wait_ge(made, 2 * i + (h + 1))
                    out = ob[h][:, 0:n * z.D].rearrange("p (b f) -> p b f", b=n)
                    if layer == 0:
                        v.tensor_scalar(m.h[:, at, :], out, 0.0, None, ALU.max).then_inc(used, 1)
                    else:
                        v.tensor_tensor(m.x[:, at, :], out, m.x[:, at, :], ALU.add).then_inc(used, 1)

                def norm_chunk(i):
                    at = bass.ds(CHUNK * i, CHUNK)
                    mean = m.stat[:, 0, at]
                    x, h, squares = m.x[:, at, :], m.h[:, at, :], m.s[:, at, :]
                    v.wait_ge(used, 2 * i + 4)
                    v.tensor_reduce(mean, x, X, ALU.add).then_inc(normed, 1)
                    v.wait_ge(normed, 5 * i + 1)
                    v.tensor_scalar(mean, mean, 1.0 / z.D, None, ALU.mult).then_inc(normed, 1)
                    v.wait_ge(normed, 5 * i + 2)
                    v.tensor_tensor(h, x, bcast(mean, 2, [P, CHUNK, z.D]), ALU.subtract).then_inc(normed, 1)
                    v.wait_ge(normed, 5 * i + 3)
                    v.tensor_tensor(squares, h, h, ALU.mult).then_inc(normed, 1)
                    v.wait_ge(normed, 5 * i + 4)
                    v.tensor_reduce(m.stat[:, 1, at], squares, X, ALU.add).then_inc(normed, 1)

                c = Steps(v, m.steps)
                c.did(v.tensor_tensor(m.s[:, :, :], m.s[:, :, :], bcast(m.di[:, :], 2, full), ALU.mult))
                c.wait()
                for h in range(2):
                    products(0, h)
                with v.Fori(0, chunks - 1) as i:
                    for h in range(2):
                        v.wait_ge(turned, 2 * i + (h + 1))
                        products(i + 1, h)
                    for h in range(2):
                        results(i, h)
                    if layer == 1:
                        norm_chunk(i)
                for h in range(2):
                    results(chunks - 1, h)
                if layer == 1:
                    norm_chunk(chunks - 1)
                v.wait_ge(used, 2 * chunks + 2)
                if layer == 1:
                    v.wait_ge(normed, 5 * chunks)
                    var = m.stat[:, 1, :]
                    c.did(v.tensor_scalar(var, var, 1.0 / z.D, EPS, ALU.mult, ALU.add))
                    c.wait()
                    v.sem_inc(m.square, 1)
                    layernorm_end(v, c, z, m, m.h[:, :, :], m.stat, 4)
                    layout.place(v, c)

            @block.tensor
            def _(t):
                t.sem_inc(uvt_ready, 2)
                t.sem_inc(used, 2)
                with t.Fori(0, chunks) as i:
                    for h, (b0, n) in enumerate(HALVES):
                        t.wait_ge(uv_ready, 2 * i + (h + 1))
                        t.wait_ge(uvt_ready, 2 * i + (h + 1))
                        for j in range(n):
                            mm = t.transpose(tb[h][:, j * P:(j + 1) * P], uv[h][:, j, :, :].rearrange("p k f -> p (k f)"),
                                             m.ident[:, :])
                        mm.then_inc(turned, 1)
                    for h, (b0, n) in enumerate(HALVES):
                        t.wait_ge(uvt_ready, 2 * i + (h + 3))
                        t.wait_ge(used, 2 * i + (h + 1))
                        for j in range(n):
                            mm = t.matmul(ob[h][:, j * z.D:(j + 1) * z.D], uvt[h][:, j * P:(j + 1) * P],
                                          m.w12[:, layer, :], start=True, stop=True)
                        mm.then_inc(made, 1)
                if layer == 1:
                    layout.turn_all(t)

            @block.gpsimd
            def _(g):
                if layer == 1:
                    layout.gather(g)

            @block.scalar
            def _(a):
                with a.Fori(0, chunks) as i:
                    for h, (b0, n) in enumerate(HALVES):
                        a.wait_ge(turned, 2 * i + (h + 1))
                        a.copy(uvt[h][:, :], tb[h][:, 0:n * P]).then_inc(uvt_ready, 1)
                if layer == 1:
                    a.wait_ge(m.square, 4)
                    a.activation(m.stat[:, 2, :], m.stat[:, 1, :], ACT.Sqrt).then_inc(m.root, 1)


class PairLayout:

    def __init__(self, nc, z, m, d, sem, ctx):
        self.z, self.m, self.d = z, m, d
        self.landed, self.turned, self.patterns = sem("pair_rows_landed"), sem("pairs_turned"), sem("pair_patterns")
        self.per = BANK // z.PB
        self.banks = -(-z.PAIR_BLOCKS // self.per)
        self.got = ctx.enter_context(nc.sbuf_tensor("pair_got", [z.PB, z.PAIR_BLOCKS, 2, P], F32))
        self.offset = ctx.enter_context(nc.sbuf_tensor("pair_offset", [P, z.PAIR_BLOCKS * z.PB], F32))
        self.turn = [[ctx.enter_context(nc.psum_tensor(f"pair_turn{f}{i}", [P, BANK], F32)) for i in range(self.banks)]
                     for f in range(2)]

    def gather(self, g):
        z, m = self.z, self.m
        g.wait_ge(m.pair_rows_out, 32)
        for b in range(z.PAIR_BLOCKS):
            g.indirect_dma_start(self.got[:, b, :, :].rearrange("p f e -> p (f e)"), None,
                                 self.d.pair_rows.rearrange("r f e -> r (f e)"),
                                 bass.IndirectOffsetOnAxis(ap=m.pair_row[:, b:b + 1], axis=0)).then_inc(self.landed, 16)
        g.iota(self.offset[:, :], pattern=[[z.PKEYS, z.PAIR_BLOCKS * z.PB]], base=z.PKEYS * z.PB * z.PAIR_BLOCK,
               channel_multiplier=0, allow_small_or_imprecise_dtypes=True).then_inc(self.patterns, 1)

    def turn_all(self, t):
        z = self.z
        t.wait_ge(self.landed, 16 * z.PAIR_BLOCKS)
        for f in range(2):
            for b in range(z.PAIR_BLOCKS):
                mm = t.transpose(self.turn[f][b // self.per][:, b % self.per * z.PB:(b % self.per + 1) * z.PB],
                                 self.got[:, b, f, :], self.m.ident[0:z.PB, 0:z.PB])
        mm.then_inc(self.turned, 1)

    def place(self, v, c):
        z, m = self.z, self.m
        v.wait_ge(self.turned, 1)
        v.wait_ge(self.patterns, 1)
        n = z.PAIR_BLOCKS * z.PB
        c.did(v.memset(m.pair_low[:, n:], 0.0))
        c.did(v.memset(m.pair_key[:, n:], -1.0))
        for i in range(self.banks):
            a, w = i * BANK, min(BANK, n - i * BANK)
            c.did(v.tensor_copy(m.pair_low[:, a:a + w], self.turn[0][i][:, 0:w]))
            c.did(v.tensor_tensor(m.pair_key[:, a:a + w], self.turn[1][i][:, 0:w], self.offset[:, a:a + w], ALU.subtract))
        c.wait()


def relation_table(nc, z, m, d, sem):
    parts_made, remainders = sem("h_parts_made"), sem("h_remainders_made")
    staged, turned, ht_ready, block_made, by_scalar, by_vector = (sem(n) for n in (
        "h_staged", "h_turned", "ht_ready", "table_made", "copied_by_scalar", "copied_by_vector"))
    stored = [sem(f"table_stored{i}") for i in range(2)]
    RF = z.R * z.D
    with ExitStack() as ctx:
        sb = lambda n, s: ctx.enter_context(nc.sbuf_tensor(n, s, F32))
        hs = [sb(f"hs{i}", [P, n, z.D]) for i, (_, n) in enumerate(HALVES)]
        ht = [sb(f"ht{i}", [z.D, n * P]) for i, (_, n) in enumerate(HALVES)]
        rest = sb("h_rest", [P, CHUNK, z.D])
        tab = [sb(f"tab{i}", [P, n, RF]) for i, (_, n) in enumerate(HALVES)]
        tb = [ctx.enter_context(nc.psum_tensor(f"h_turn{i}", [P, BANK], F32)) for i in range(2)]
        bank = [ctx.enter_context(nc.psum_tensor(f"table{i}", [P, BANK], F32)) for i in range(4)]
        with nc.Block() as block:

            @block.tensor
            def _(t):
                for s, n in ((turned, 2), (ht_ready, 2), (by_scalar, 2), (by_vector, 1)):
                    t.sem_inc(s, n)
                with t.Fori(0, z.NB // CHUNK) as i:
                    for h, (b0, n) in enumerate(HALVES):
                        t.wait_ge(staged, 2 * i + (h + 1))
                        t.wait_ge(ht_ready, 2 * i + (h + 1))
                        t.nop(nofuse=True)
                        for j in range(n):
                            mm = t.transpose(tb[h][0:z.D, j * P:(j + 1) * P], hs[h][:, j, :], m.ident[:, :])
                        mm.then_inc(turned, 1)
                    for h, (b0, n) in enumerate(HALVES):
                        t.wait_ge(ht_ready, 2 * i + (h + 3))
                        for j in range(n):
                            at = b0 + j
                            if at % 2 == 0:
                                t.wait_ge(by_scalar, 4 * i + (at // 2 + 1))
                            else:
                                t.wait_ge(by_vector, 3 * i + (at // 2 + 1))
                            t.matmul(bank[at % 4][:, 0:RF], ht[h][:, j * P:(j + 1) * P],
                                     m.w3[:, :, :].rearrange("d r f -> d (r f)"), start=True, stop=True
                                     ).then_inc(block_made, 1)

            @block.scalar
            def _(a):
                def cut(i, k):
                    at = bass.ds(CHUNK * i, CHUNK)
                    if k > 0:
                        a.wait_ge(remainders, 2 * i + k)
                    a.copy(part(m, z, k, at), m.h[:, at, :] if k == 0 else rest[:, :, :]).then_inc(parts_made, 1)

                def stage_blocks(i):
                    for h, (b0, n) in enumerate(HALVES):
                        a.wait_ge(turned, 2 * i + (h + 1))
                        a.copy(hs[h][:, :, :], m.h[:, bass.ds(CHUNK * i + b0, n), :]).then_inc(staged, 1)

                def one(i, more):
                    cut(i, 0)
                    for h, (b0, n) in enumerate(HALVES):
                        a.wait_ge(stored[h], 16 * i + 16)
                        for j in range(n):
                            if (b0 + j) % 2 == 0:
                                a.wait_ge(block_made, CHUNK * i + (b0 + j + 1))
                                a.copy(tab[h][:, j, :], bank[(b0 + j) % 4][:, 0:RF]).then_inc(by_scalar, 1)
                        if h == 0 and more:
                            stage_blocks(i + 1)
                        cut(i, h + 1)

                stage_blocks(0)
                with a.Fori(0, z.NB // CHUNK - 1) as i:
                    one(i, True)
                one(z.NB // CHUNK - 1, False)

            @block.vector
            def _(v):
                def remainder(i, k):
                    at = bass.ds(CHUNK * i, CHUNK)
                    v.wait_ge(parts_made, PIECES * i + k)
                    v.tensor_tensor(rest[:, :, :], m.h[:, at, :] if k == 1 else rest[:, :, :],
                                    part(m, z, k - 1, at), ALU.subtract).then_inc(remainders, 1)

                def scale(i):
                    at = bass.ds(CHUNK * i, CHUNK)
                    v.tensor_tensor(m.h[:, at, :], m.h[:, at, :], bcast(factor_h[:, at], 2, [P, CHUNK, z.D]), ALU.mult)

                c = Steps(v, m.steps)
                some, factor_h, factor_m = (m.stat[:, k, :] for k in range(3))
                c.did(v.tensor_scalar(some, m.deg_in[:, :], 0.0, None, ALU.is_gt))
                c.did(v.tensor_scalar(factor_m, m.deg_in[:, :], 1.0, None, ALU.max))
                c.wait()
                c.did(v.tensor_scalar(factor_h, some, 0.2 - 1.0, 1.0, ALU.mult, ALU.add))
                c.did(v.reciprocal(factor_m, factor_m))
                c.wait()
                c.did(v.tensor_scalar(factor_m, factor_m, 1.0 - 0.2, None, ALU.mult))
                c.wait()
                with v.Fori(0, z.NB // CHUNK) as i:
                    for h, (b0, n) in enumerate(HALVES):
                        v.wait_ge(turned, 2 * i + (h + 3))
                        v.tensor_copy(ht[h][:, :], tb[h][0:z.D, 0:n * P]).then_inc(ht_ready, 1)
                    remainder(i, 1)
                    for h, (b0, n) in enumerate(HALVES):
                        v.wait_ge(stored[h], 16 * i + 16)
                        for j in range(n):
                            if (b0 + j) % 2 == 1:
                                v.wait_ge(block_made, CHUNK * i + (b0 + j + 1))
                                v.tensor_copy(tab[h][:, j, :], bank[(b0 + j) % 4][:, 0:RF]).then_inc(by_vector, 1)
                        if h == 0:
                            remainder(i, 2)
                            scale(i)

            @block.sync
            def _(sp):
                sp.sem_inc(stored[0], 16)
                sp.sem_inc(stored[1], 16)
                table = d.t_table.rearrange("(b p) r f -> p b (r f)", p=P)
                with sp.Fori(0, z.NB // CHUNK) as i:
                    for h, (b0, n) in enumerate(HALVES):
                        sp.wait_ge(by_scalar, 4 * i + (2 + 2 * (h + 1)))
                        sp.nop(nofuse=True)
                        sp.wait_ge(by_vector, 3 * i + (1 + 2 + h))
                        sp.nop(nofuse=True)
                        sp.dma_start(table[:, bass.ds(CHUNK * i + b0, n), :], tab[h][:, :, :]).then_inc(stored[h], 16)
                for h in range(2):
                    sp.wait_ge(stored[h], 16 * (z.NB // CHUNK + 1))


GATHERS = 8
SLOTS = 4
BATCH = 4


def relate(nc, z, m, d, sem):
    index_ready, hot_ready, used, added = (sem(f"relate_{n}") for n in ("index", "hot", "used", "added"))
    rows_in = [sem(f"relation_rows_in{k}") for k in range(SLOTS)]
    staged, turned, placed, summed = (sem(f"relate_{n}") for n in ("staged", "turned", "placed", "summed"))
    batch_made, pair_made, pair_copied, unit_used, unit_reduced = (sem(f"dense_{n}") for n in (
        "hot_made", "pair_made", "pair_copied", "unit_used", "unit_reduced"))
    units_turned, turned_copied, weighted, dense_placed = (sem(f"dense_{n}") for n in (
        "turned", "turned_copied", "weighted", "placed"))
    span = z.STEP * (GATHERS - 1) + WIN
    PAIRS = UNITS * UNIT_PAIRS
    BATCHES = PAIRS // BATCH
    NEW = UNITS * UNIT
    DCOL = z.STEP * SLOTS * GATHERS * z.ITERS + 2 * P
    parts_cols = PIECES * z.D
    assert SLOTS * GATHERS * z.STEP == P and z.DENSE + P // 2 + span <= DCOL
    assert DCOL + NEW * z.ITERS <= z.SEG * BANK and z.PAIR_BLOCK % CHUNK == 0
    with ExitStack() as ctx:
        sb = lambda n, s, t: ctx.enter_context(nc.sbuf_tensor(n, s, t))
        general = general_buffers(nc, z, ctx, "relation")
        index = sb("relate_index", [P, SLOTS, GATHERS], U32)
        flat = general.hot[:, :, :].rearrange("p a b -> p (a b)")
        hots, gathered = 2 * GATHERS * WIN, SLOTS * GATHERS * z.D
        hot = flat[:, 0:hots].rearrange("p (k j w) -> p k j w", k=2, j=GATHERS)
        rows = flat[:, hots:hots + gathered].rearrange("p (k j f) -> p k j f", k=SLOTS, j=GATHERS)
        sums = general.sums[0:z.D, :]
        low = sb("pair_low_hot", [P, 2, P, BATCH], BF16)
        keys = sb("pair_key_hot", [P, 2, BATCH, z.PKEYS], BF16)
        a_buf = [m.s[:, :, :].rearrange("p b f -> p (b f)").bitcast(BF16),
                 *(sb(f"unit_a{i}", [P, UNIT_PAIRS * z.PKEYS], BF16)[:, :] for i in (1, 2))]
        halves, turned_cols = CHUNK * P, UNITS * P
        stage = [general.place[0:z.D, b0 * P:(b0 + n) * P] for b0, n in HALVES]
        turned_sums = general.place[0:z.D, halves:halves + turned_cols]
        per_relation = general.place[:, halves + turned_cols:halves + turned_cols + UNITS * z.D]\
                              .rearrange("p (u f) -> p u f", u=UNITS)
        bank = [ctx.enter_context(nc.psum_tensor(f"window{i}", [P, BANK], F32)) for i in range(2)]
        pair_bank = [ctx.enter_context(nc.psum_tensor(f"pair_bank{i}", [P, 2, BANK], F32)) for i in range(2)]
        unit_bank, tail_bank = general.turn, general.acc
        tb = bank
        gsem = general_run(m, sem, 3)
        with nc.Block() as block:

            @block.scalar
            def _(a):
                bad = a.value_load(m.flag[0:1, 0:1], min_val=0, max_val=1024)
                with a.If(bad > 0):
                    general_scalar(a, z, m, general, gsem, "relation")
                with a.Else():
                    def next_index(i, k):
                        a.copy(index[:, k, :], m.row_index[:, bass.ds(GATHERS * (SLOTS * i + k), GATHERS)])\
                         .then_inc(index_ready, 1)

                    def copy_pairs(i, first, last):
                        for p in range(first, last):
                            a.wait_ge(pair_made, PAIRS * i + (p + 1))
                            at = p % UNIT_PAIRS * z.PKEYS
                            a.copy(a_buf[p // UNIT_PAIRS % UNITS][:, at:at + z.PKEYS].rearrange("p (c k) -> p c k", c=2),
                                   pair_bank[p % 2][:, :, 0:z.KEYS]).then_inc(pair_copied, 1)

                    def buffer_free(i, u):
                        a.wait_ge(unit_used, UNITS * i + u)

                    def copy_turned(i):
                        a.wait_ge(units_turned, i + 1)
                        a.copy(turned_sums, tail_bank[0:z.D, 0:UNITS * P]).then_inc(turned_copied, 1)

                    def place(i):
                        a.wait_ge(weighted, i + 1)
                        a.copy(sums[:, bass.ds(NEW * i + (DCOL - NEW), NEW)],
                               tail_bank[0:z.D, UNITS * P:UNITS * P + NEW]).then_inc(dense_placed, 1)

                    for k in range(SLOTS):
                        next_index(0, k)
                    copy_pairs(0, 0, UNIT_PAIRS)
                    with a.Fori(0, z.ITERS) as i:
                        buffer_free(i, 1)
                        copy_pairs(i, UNIT_PAIRS, 2 * UNIT_PAIRS)
                        copy_turned(i)
                        a.wait_ge(used, SLOTS * i + 3)
                        next_index(i + 1, 0)
                        buffer_free(i, 2)
                        copy_pairs(i, 2 * UNIT_PAIRS, 2 * UNIT_PAIRS + BATCH)
                        a.wait_ge(used, SLOTS * i + 4)
                        next_index(i + 1, 1)
                        copy_pairs(i, 2 * UNIT_PAIRS + BATCH, 3 * UNIT_PAIRS)
                        place(i)
                        a.wait_ge(used, SLOTS * i + 5)
                        next_index(i + 1, 2)
                        buffer_free(i, 3)
                        copy_pairs(i, 3 * UNIT_PAIRS, 4 * UNIT_PAIRS)
                        a.wait_ge(used, SLOTS * i + 6)
                        next_index(i + 1, 3)
                    copy_turned(z.ITERS)
                    place(z.ITERS)
                    a.wait_ge(added, SLOTS * z.ITERS + 2)
                    a.wait_ge(dense_placed, z.ITERS + 2)
                    a.copy(sums[:, DCOL - P // 2:DCOL], sums[:, z.DENSE - P // 2 + MARGIN:z.DENSE + MARGIN])\
                     .then_inc(dense_placed, 1)
                    a.wait_ge(dense_placed, z.ITERS + 3)
                    for first, last, at in ((0, z.PAIR_BLOCK, MARGIN), (z.PAIR_BLOCK, z.NB, DCOL - z.DENSE)):
                        with a.Fori(first // CHUNK, last // CHUNK) as i:
                            for h, (b0, n) in enumerate(HALVES):
                                a.wait_ge(turned, 2 * i + (h + 1))
                                a.copy(stage[h], sums[:, bass.ds(P * (CHUNK * i + b0) + at, n * P)])\
                                 .then_inc(staged, 1)

            @block.gpsimd
            def _(g):
                bad = g.value_load(m.flag[0:1, 0:1], min_val=0, max_val=1024)
                with g.If(bad > 0):
                    general_gpsimd(g, z, m, d, general, gsem, "relation")
                with g.Else():
                    table = d.t_table.rearrange("n r f -> (n r) f")
                    with g.Fori(0, z.ITERS) as i:
                        for k in range(SLOTS):
                            g.wait_ge(index_ready, SLOTS * i + (k + 1))
                            g.nop(nofuse=True)
                            for j in range(GATHERS):
                                g.indirect_dma_start(rows[:, k, j, :], None, table,
                                                     bass.IndirectOffsetOnAxis(ap=index[:, k, j:j + 1], axis=0)
                                                     ).then_inc(rows_in[k], 16)

            @block.vector
            def _(v):
                bad = v.value_load(m.flag[0:1, 0:1], min_val=0, max_val=1024)
                with v.If(bad > 0):
                    general_vector(v, z, m, general, gsem, "relation")
                    c = Steps(v, gsem.own)
                    c.did(v.tensor_tensor(m.s[:, :, :], m.s[:, :, :], bcast(m.stat[:, 2, :], 2, [P, z.NB, z.D]), ALU.mult))
                    c.wait()
                    c.did(v.tensor_tensor(m.s[:, :, :], m.s[:, :, :], m.h[:, :, :], ALU.add))
                    c.wait()
                    c.did(v.scalar_tensor_tensor(out=m.s[:, :, :], in0=m.s[:, :, :], scalar=0.0, in1=m.x[:, :, :],
                                                 op0=ALU.max, op1=ALU.add))
                with v.Else():
                    def pair_hots(i, n):
                        at = PAIRS * i + (z.PB // 2 + BATCH * n)
                        v.tensor_tensor(low[:, n % 2, :, :], m.iota_low[:, :, 0:BATCH],
                                        bcast(m.pair_low[:, bass.ds(at, BATCH)], 1, [P, P, BATCH]), ALU.is_equal)
                        for j in range(BATCH):
                            ins = v.tensor_scalar(keys[:, n % 2, j, :], m.iota_keys[:, :],
                                                  m.pair_key[:, bass.ds(at + j, 1)], None, ALU.is_equal)
                        ins.then_inc(batch_made, 1)

                    def batch(i, n):
                        v.wait_ge(pair_made, PAIRS * i + BATCH * (n - 1))
                        pair_hots(i, n)

                    def window_hots(i, k):
                        v.wait_ge(used, SLOTS * i + (k + 1))
                        v.tensor_tensor(hot[:, k % 2, :, :], bcast(m.iota_row[:, 0:WIN], 1, [P, GATHERS, WIN]),
                                        bcast(m.in_window[:, bass.ds(GATHERS * (SLOTS * i + k), GATHERS)], 2,
                                              [P, GATHERS, WIN]), ALU.is_equal).then_inc(hot_ready, 1)

                    def add_window(i, k):
                        v.wait_ge(used, SLOTS * i + (k + 3))
                        v.wait_ge(added, SLOTS * i + (k + 2))
                        at = sums[:, bass.ds(z.STEP * GATHERS * (SLOTS * i + k), span)]
                        v.tensor_tensor(at, bank[k % 2][0:z.D, 0:span], at, ALU.add).then_inc(added, 1)

                    def reduce_unit(i, u):
                        v.wait_ge(unit_used, UNITS * i + (u + 3))
                        if u == 0:
                            v.wait_ge(units_turned, i + 1)
                        v.tensor_reduce(per_relation[:, u, :],
                                        unit_bank[:, 0:parts_cols].rearrange("p (k f) -> p f k", k=PIECES),
                                        X, ALU.add).then_inc(unit_reduced, 1)

                    v.memset(sums[:, 0:DCOL - P // 2], 0.0).then_inc(added, 2)
                    v.memset(per_relation[:, :, :], 0.0).then_inc(unit_reduced, 1)
                    pair_hots(0, 0)
                    pair_hots(0, 1)
                    batch(0, 2)
                    batch(0, 3)
                    with v.Fori(0, z.ITERS) as i:
                        window_hots(i, 0)
                        window_hots(i, 1)
                        batch(i, 4)
                        batch(i, 5)
                        reduce_unit(i, 0)
                        add_window(i, 0)
                        window_hots(i, 2)
                        batch(i, 6)
                        add_window(i, 1)
                        window_hots(i, 3)
                        batch(i, 7)
                        reduce_unit(i, 1)
                        add_window(i, 2)
                        batch(i, 8)
                        batch(i, 9)
                        reduce_unit(i, 2)
                        add_window(i, 3)
                    with v.Fori(0, z.NB // CHUNK) as i:
                        for h, (b0, n) in enumerate(HALVES):
                            v.wait_ge(turned, 2 * i + (h + 3))
                            at = bass.ds(CHUNK * i + b0, n)
                            v.tensor_tensor(m.s[:, at, :], tb[h][:, 0:n * z.D].rearrange("p (b f) -> p b f", b=n),
                                            bcast(m.stat[:, 2, at], 2, [P, n, z.D]), ALU.mult).then_inc(placed, 1)
                        at = bass.ds(CHUNK * i, CHUNK)
                        s, h, x = m.s[:, at, :], m.h[:, at, :], m.x[:, at, :]
                        v.wait_ge(placed, 2 * i + 4)
                        v.tensor_tensor(s, s, h, ALU.add).then_inc(summed, 1)
                        v.wait_ge(summed, i + 1)
                        v.scalar_tensor_tensor(out=s, in0=s, scalar=0.0, in1=x, op0=ALU.max, op1=ALU.add)

            @block.tensor
            def _(t):
                bad = t.value_load(m.flag[0:1, 0:1], min_val=0, max_val=1024)
                with t.If(bad > 0):
                    general_tensor(t, z, m, general, gsem, "relation")
                with t.Else():
                    def build_pair(i, p):
                        if p % BATCH == 0:
                            t.wait_ge(batch_made, BATCHES * i + (p // BATCH + 1))
                        t.wait_ge(pair_copied, PAIRS * i + (p + 1))
                        for c in range(2):
                            mm = t.matmul(pair_bank[p % 2][:, c, 0:z.KEYS], low[:, p // BATCH % 2, :, p % BATCH],
                                          keys[:, p // BATCH % 2, p % BATCH, c * z.KEYS:(c + 1) * z.KEYS],
                                          start=True, stop=True)
                        mm.then_inc(pair_made, 1)

                    def build_under_use(i, u, first, last):
                        if first == 0:
                            t.wait_ge(unit_reduced, UNITS * i + (u + 1))
                        each = -(-z.NB // UNIT_PAIRS)
                        for q in range(first, last):
                            build_pair(i, (u + 1) * UNIT_PAIRS + q)
                            if q == 0:
                                t.wait_ge(pair_copied, PAIRS * i + ((u + 1) * UNIT_PAIRS + 2))
                            for k in range(q * each, min((q + 1) * each, z.NB)):
                                mm = t.matmul(unit_bank[:, 0:parts_cols], a_buf[u][:, k::z.NB],
                                              m.parts[:, k, 0:parts_cols], start=(k == 0), stop=(k == z.NB - 1))
                        if last == UNIT_PAIRS:
                            mm.then_inc(unit_used, 1)

                    def sum_group(i, k):
                        t.wait_ge(added, SLOTS * i + (k + 1))
                        t.nop(nofuse=True)
                        t.matmul(bank[k % 2][0:z.D, 0:span], m.zeros[0:1, 0:z.D], m.zeros[0:1, 0:span],
                                 start=True, stop=False)
                        t.wait_ge(hot_ready, SLOTS * i + (k + 1))
                        t.wait_ge(rows_in[k], 16 * GATHERS * i + 16 * GATHERS)
                        t.nop(nofuse=True)
                        for j in range(GATHERS):
                            mm = t.matmul(bank[k % 2][0:z.D, z.STEP * j:z.STEP * j + WIN], rows[:, k, j, :],
                                          hot[:, k % 2, j, :], start=False, stop=(j == GATHERS - 1))
                        mm.then_inc(used, 1)

                    def turn_units(i):
                        t.wait_ge(unit_reduced, UNITS * i + 1)
                        t.nop(nofuse=True)
                        t.wait_ge(dense_placed, i + 1)
                        t.nop(nofuse=True)
                        for u in range(UNITS):
                            mm = t.transpose(tail_bank[0:z.D, u * P:(u + 1) * P], per_relation[:, u, :], m.ident[:, :])
                        mm.then_inc(units_turned, 1)

                    def weigh(i):
                        t.wait_ge(turned_copied, i + 1)
                        t.nop(nofuse=True)
                        for r in range(z.R):
                            mm = t.matmul(tail_bank[0:z.D, UNITS * P:UNITS * P + NEW], m.w3[:, r, :],
                                          turned_sums[:, r::z.R], start=(r == 0), stop=(r == z.R - 1))
                        mm.then_inc(weighted, 1)

                    t.sem_inc(used, 2)
                    t.sem_inc(pair_copied, 2)
                    t.sem_inc(unit_used, 2)
                    t.sem_inc(dense_placed, 1)
                    for p in range(UNIT_PAIRS):
                        build_pair(0, p)
                    with t.Fori(0, z.ITERS) as i:
                        build_under_use(i, 0, 0, UNIT_PAIRS)
                        turn_units(i)
                        sum_group(i, 0)
                        build_under_use(i, 1, 0, BATCH)
                        sum_group(i, 1)
                        build_under_use(i, 1, BATCH, UNIT_PAIRS)
                        weigh(i)
                        sum_group(i, 2)
                        build_under_use(i, 2, 0, UNIT_PAIRS)
                        sum_group(i, 3)
                    turn_units(z.ITERS)
                    weigh(z.ITERS)
                    t.wait_ge(added, SLOTS * z.ITERS + 2)
                    t.sem_inc(turned, 2)
                    t.sem_inc(placed, 2)
                    with t.Fori(0, z.NB // CHUNK) as i:
                        for h, (b0, n) in enumerate(HALVES):
                            t.wait_ge(staged, 2 * i + (h + 1))
                            t.wait_ge(placed, 2 * i + (h + 1))
                            t.nop(nofuse=True)
                            for j in range(n):
                                mm = t.transpose(tb[h][:, j * z.D:(j + 1) * z.D], stage[h][:, j * P:(j + 1) * P],
                                                 m.ident[0:z.D, 0:z.D])
                            mm.then_inc(turned, 1)


def store(nc, z, m, d, sem):
    stored = sem("out_stored")
    rem = z.N - (z.NB - 1) * P
    with nc.Block() as block:

        @block.sync
        def _(sp):
            sp.dma_start(d.out[0:(z.NB - 1) * P, :].rearrange("(b p) f -> p b f", p=P),
                         m.s[:, 0:z.NB - 1, :]).then_inc(stored, 16)
            sp.dma_start(d.out[(z.NB - 1) * P:z.N, :], m.s[0:rem, z.NB - 1, :]).then_inc(stored, 16)
            sp.wait_ge(stored, 32)


def program(nc, x, src, dst, etype, w1_1, w2_1, w1_2, w2_2, w3, out, stop=None):
    z = sizes(x.shape[0], src.shape[0], x.shape[1], w3.shape[0])
    dram = lambda n, s, t: nc.dram_tensor(n, s, t, kind="Internal").ap()
    d = Named()
    d.x = x
    d.src = src
    d.dst = dst
    d.etype = etype
    d.w1_1 = w1_1
    d.w2_1 = w2_1
    d.w1_2 = w1_2
    d.w2_2 = w2_2
    d.w3 = w3
    d.out = out
    d.scr = dram("edge_fields", (3, z.SCR), F32)
    d.rows = dram("edge_rows", (z.TROWS, 2, P), F32)
    d.pair_rows = dram("pair_rows", (z.PROWS, 2, P), F32)
    d.a = dram("adjacency", (z.NB, P, z.GB * z.KEYS), BF16)
    d.g_table = dram("g_rows", (z.NP, z.D), F32)
    d.t_table = dram("relation_rows", (z.NP, z.R, z.D), F32)
    with ExitStack() as ctx:
        sb = lambda n, s, t: ctx.enter_context(nc.sbuf_tensor(n, s, t))
        sem = lambda n: ctx.enter_context(nc.semaphore(n))
        nodes = [P, z.NB, z.D]
        m = Named()
        m.steps = Count(sem("vector_step"))
        m.general = general_semaphores(sem)
        m.pair_rows_out = sem("pair_rows_written")
        m.square, m.root = sem("square_ready"), sem("root_ready")
        m.x = sb("x", nodes, F32)
        m.h = sb("h", nodes, F32)
        m.s = sb("s", nodes, F32)
        m.low = sb("low", [P, z.NB * z.CT], BF16)
        m.key = sb("key", [P, z.NB * z.CT + 12], F32)
        m.row_index = sb("row_index", [P, z.TILES], U32)
        m.src_index = sb("src_index", [P, z.TILES], U32)
        m.in_window = sb("in_window", [P, z.TILES], F32)
        m.tile_base = sb("tile_base", [P, z.TILES], F32)
        m.deg_out = sb("deg_out", [P, z.NB], F32)
        m.deg_in = sb("deg_in", [P, z.NB], F32)
        m.do = sb("do", [P, z.NB], F32)
        m.di = sb("di", [P, z.NB], F32)
        m.stat = sb("stat", [P, 4, z.NB], F32)
        m.w12 = sb("w12", [P, 2, z.D], F32)
        m.w3 = sb("w3", [z.D, z.R, z.D], F32)
        m.iota_row = sb("iota_row", [P, BANK], F32)
        m.iota_part = sb("iota_part", [P, 1], F32)
        m.iota_keys = sb("iota_keys", [P, z.PKEYS], F16)
        m.pair_row = sb("pair_row", [z.PB, z.PAIR_BLOCKS], U32)
        m.iota_low = sb("iota_low", [P, P, 12], BF16)
        m.ident = sb("ident", [P, P], F32)
        m.ident16 = sb("ident16", [P, P], BF16)
        m.before = sb("before", [P, P], F32)
        m.zeros = sb("zeros", [P, BANK], F32)
        m.ones = sb("ones", [P, 1], F32)
        m.flag = sb("flag", [1, 1], I32)

        def later():
            m.parts = sb("parts", [P, z.NB, PIECES * z.D + 1], BF16)
            m.pair_low = sb("pair_low", [P, z.PAIR_BLOCKS * z.PB + 2 * UNIT_PAIRS], BF16)
            m.pair_key = sb("pair_keys", [P, z.PAIR_BLOCKS * z.PB + 2 * UNIT_PAIRS], F32)

        stages = [
            lambda: prepare(nc, z, m, d, sem),
            later,
            lambda: build(nc, z, m, d, sem),
            lambda: aggregate(nc, z, m, d, sem, 0),
            lambda: convolve(nc, z, m, d, sem, 0),
            lambda: aggregate(nc, z, m, d, sem, 1),
            lambda: convolve(nc, z, m, d, sem, 1),
            lambda: relation_table(nc, z, m, d, sem),
            lambda: relate(nc, z, m, d, sem),
            lambda: store(nc, z, m, d, sem),
        ]
        for stage in stages[:stop]:
            stage()
        return m


_INS = ["x", "src", "dst", "edge_type_8", "L0_gnn_W1_1", "L0_gnn_W2_1", "L0_gnn_W1_2", "L0_gnn_W2_2",
        "L1_gnn_weight_r"]


def kernel(**inputs):
    import numpy as np
    import concourse.bacc as bacc
    from concourse.bass_utils import run_bass_kernel_spmd

    nc = bacc.Bacc("TRN2", target_bir_lowering=False, num_devices=1)
    arrays, args = {}, []
    for name in _INS:
        a = np.ascontiguousarray(inputs[name])
        arrays[f"in_{name}"] = a
        args.append(nc.dram_tensor(f"in_{name}", a.shape, mybir.dt.from_np(a.dtype), kind="ExternalInput").ap())
    args.append(nc.dram_tensor("out", inputs["x"].shape, F32, kind="ExternalOutput").ap())
    program(nc, *args)
    return run_bass_kernel_spmd(nc, [arrays], core_ids=[0]).results[0]["out"]
```
